# Optimizing a Trainium2 kernel written in Bass

```python
import numpy as np
import jax
import jax.numpy as jnp

def _softmax(x, axis=-1):
    return jax.nn.softmax(x, axis=axis)

def _gelu(x):
    return jax.nn.gelu(x, approximate=True)

def _silu(x):
    return jax.nn.silu(x)

def _sigmoid(x):
    return jax.nn.sigmoid(x)

def _layernorm(x, axis=-1, eps=1e-05):
    m = jnp.mean(x, axis=axis, keepdims=True)
    v = jnp.var(x, axis=axis, keepdims=True)
    return (x - m) / jnp.sqrt(v + eps)

def _scatter_add(tgt, idx, src, axis=0):
    return tgt.at[idx].add(src)

def _segment_sum(src, seg, n):
    return jax.ops.segment_sum(src, seg, n)
kernel_name = 'mk_perceiver_d1_seqx_r8_3b6902'

def setup_inputs(seed: int=0):
    np.random.seed(seed)
    _w = jnp.asarray

    def _rec_inputs():
        import jax
        import jax.numpy as jnp
        _rk = jax.random.key(seed)
        x = -0.0005207 + 1.001 * jax.random.normal(jax.random.fold_in(_rk, 1), (4, 128, 128), jnp.float32)
        _lenS = 128 - jax.random.randint(jax.random.fold_in(_rk, 7), (4,), 0, max(1, 128 // 4) + 1, jnp.int32)
        _lenS2 = 2048 - jax.random.randint(jax.random.fold_in(_rk, 8), (4,), 0, max(1, 2048 // 4) + 1, jnp.int32)
        _ctx_1024P = jax.random.normal(jax.random.fold_in(_rk, 11), (4, 16, 128), jnp.float32)
        _ctx_1024c = jax.random.dirichlet(jax.random.fold_in(_rk, 511), 0.3 * jnp.ones((16,), jnp.float32), (4, 2048))
        _ctx_1024t = jnp.einsum('bsk,bkd->bsd', _ctx_1024c, _ctx_1024P)
        _ctx_1024t = _ctx_1024t * jax.lax.rsqrt(jnp.mean(jnp.square(_ctx_1024t)) + 1e-12) * 0.953939
        ctx_1024 = 2.81802e-05 + 1.00001 * (_ctx_1024t + 0.3 * jax.random.normal(jax.random.fold_in(_rk, 611), (4, 2048, 128), jnp.float32))
        _validS = jnp.arange(128)[None, :] < _lenS[:, None]
        _validS2 = jnp.arange(2048)[None, :] < _lenS2[:, None]
        _causal = jnp.tril(jnp.ones((128, 128), dtype=bool))
        mask_BxSxS2_bk0 = jnp.logical_not(jnp.broadcast_to(_validS2[:, None, :], (4, 128, 2048)))
        return (x, ctx_1024, mask_BxSxS2_bk0)
    x, ctx_1024, mask_BxSxS2_bk0 = _rec_inputs()

    def _L0_xattn_setup():
        import jax, jax.numpy as jnp
        import numpy as np
        B, TQ, TKV, D, H = (4, 64, 512, 128, 8)
        HEAD_DIM = D // H

        def _split_heads(x, h):
            b, t, c = x.shape
            return x.reshape(b, t, h, c // h).transpose(0, 2, 1, 3)
        key = jax.random.key(seed)
        ks = jax.random.split(key, 8)
        s = 0.02
        inputs_q = jax.random.normal(ks[0], (B, TQ, D), jnp.float32)
        inputs_kv = jax.random.normal(ks[1], (B, TKV, D), jnp.float32)
        attention_mask = jax.random.randint(ks[2], (B, TQ, TKV), 0, 2).astype(bool)
        Wq = jax.random.normal(ks[3], (D, D), jnp.float32) * s
        Wk = jax.random.normal(ks[4], (D, D), jnp.float32) * s
        Wv = jax.random.normal(ks[5], (D, D), jnp.float32) * s
        Wo = jax.random.normal(ks[6], (D, D), jnp.float32) * s
        zb = jnp.zeros((D,), jnp.float32)
        return {'inputs_q': inputs_q, 'inputs_kv': inputs_kv, 'attention_mask': attention_mask, 'Wq': Wq, 'bq': zb, 'Wk': Wk, 'bk': zb, 'Wv': Wv, 'bv': zb, 'Wo': Wo, 'bo': zb}
    _L0_xattn_all = _L0_xattn_setup()
    _L0_xattn_in = {k: v for k, v in _L0_xattn_all.items() if k in ('Wq', 'bq', 'Wk', 'bk', 'Wv', 'bv', 'Wo', 'bo')}
    del _L0_xattn_all

    def _L0_attn_setup():
        import jax, jax.numpy as jnp
        import numpy as np
        DIM = 128
        SQRT_DIM = float(np.sqrt(DIM))
        key = jax.random.key(seed)
        inputs = jax.random.normal(key, (512, 4, DIM), dtype=jnp.float32)
        return {'inputs': inputs}
    _L0_attn_all = _L0_attn_setup()
    _L0_attn_in = {k: v for k, v in _L0_attn_all.items() if k in ()}
    del _L0_attn_all

    def _L0_ffn_setup():
        import jax, jax.numpy as jnp
        import numpy as np
        NUM_EXPERTS = 8
        TOP_K = 2
        NUM_GRIDS = 8
        INV_DENOM = 0.5
        GRID = np.linspace(-1.2, 0.2, NUM_GRIDS).astype(np.float32)
        LN_EPS = 1e-05

        def _layernorm(x, g, b):
            mu = x.mean(-1, keepdims=True)
            var = x.var(-1, keepdims=True)
            return (x - mu) * jax.lax.rsqrt(var + LN_EPS) * g + b

        def _rswaf(x, grid):
            t = jnp.tanh((x[..., None] - grid) * INV_DENOM)
            return 1.0 - t * t
        key = jax.random.key(seed)
        ks = jax.random.split(key, 8)
        B, S, H, F = (1, 256, 128, 512)
        F2 = F // 2
        E2 = NUM_EXPERTS // 2
        G = NUM_GRIDS
        s = 0.02
        return {'hidden_states': jax.random.normal(ks[0], (B, S, H), jnp.float32), 'gate_W': jax.random.normal(ks[1], (H, NUM_EXPERTS), jnp.float32) * s, 'mlp_W1': jax.random.normal(ks[2], (E2, H, F), jnp.float32) * s, 'mlp_b1': jnp.zeros((E2, F), jnp.float32), 'mlp_W2': jax.random.normal(ks[3], (E2, F, H), jnp.float32) * s, 'mlp_b2': jnp.zeros((E2, H), jnp.float32), 'kan_ln_g0': jnp.ones((E2, H), jnp.float32), 'kan_ln_b0': jnp.zeros((E2, H), jnp.float32), 'kan_sl_W0': jax.random.normal(ks[4], (E2, H * G, F2), jnp.float32) * s, 'kan_sl_b0': jnp.zeros((E2, F2), jnp.float32), 'kan_ln_g1': jnp.ones((E2, F2), jnp.float32), 'kan_ln_b1': jnp.zeros((E2, F2), jnp.float32), 'kan_sl_W1': jax.random.normal(ks[5], (E2, F2 * G, H), jnp.float32) * s, 'kan_sl_b1': jnp.zeros((E2, H), jnp.float32)}
    _L0_ffn_all = _L0_ffn_setup()
    _L0_ffn_in = {k: v for k, v in _L0_ffn_all.items() if k in ('gate_W', 'mlp_W1', 'mlp_b1', 'mlp_W2', 'mlp_b2', 'kan_ln_g0', 'kan_ln_b0', 'kan_sl_W0', 'kan_sl_b0', 'kan_ln_g1', 'kan_ln_b1', 'kan_sl_W1', 'kan_sl_b1')}
    del _L0_ffn_all
    return {'x': x, 'ctx_1024': ctx_1024, 'mask_BxSxS2_bk0': mask_BxSxS2_bk0, 'L0_xattn_Wq': _L0_xattn_in['Wq'], 'L0_xattn_bq': _L0_xattn_in['bq'], 'L0_xattn_Wk': _L0_xattn_in['Wk'], 'L0_xattn_bk': _L0_xattn_in['bk'], 'L0_xattn_Wv': _L0_xattn_in['Wv'], 'L0_xattn_bv': _L0_xattn_in['bv'], 'L0_xattn_Wo': _L0_xattn_in['Wo'], 'L0_xattn_bo': _L0_xattn_in['bo'], 'L0_ffn_gate_W': _L0_ffn_in['gate_W'], 'L0_ffn_mlp_W1': _L0_ffn_in['mlp_W1'], 'L0_ffn_mlp_b1': _L0_ffn_in['mlp_b1'], 'L0_ffn_mlp_W2': _L0_ffn_in['mlp_W2'], 'L0_ffn_mlp_b2': _L0_ffn_in['mlp_b2'], 'L0_ffn_kan_ln_g0': _L0_ffn_in['kan_ln_g0'], 'L0_ffn_kan_ln_b0': _L0_ffn_in['kan_ln_b0'], 'L0_ffn_kan_sl_W0': _L0_ffn_in['kan_sl_W0'], 'L0_ffn_kan_sl_b0': _L0_ffn_in['kan_sl_b0'], 'L0_ffn_kan_ln_g1': _L0_ffn_in['kan_ln_g1'], 'L0_ffn_kan_ln_b1': _L0_ffn_in['kan_ln_b1'], 'L0_ffn_kan_sl_W1': _L0_ffn_in['kan_sl_W1'], 'L0_ffn_kan_sl_b1': _L0_ffn_in['kan_sl_b1']}

def reference(x, ctx_1024, mask_BxSxS2_bk0, L0_xattn_Wq, L0_xattn_bq, L0_xattn_Wk, L0_xattn_bk, L0_xattn_Wv, L0_xattn_bv, L0_xattn_Wo, L0_xattn_bo, L0_ffn_gate_W, L0_ffn_mlp_W1, L0_ffn_mlp_b1, L0_ffn_mlp_W2, L0_ffn_mlp_b2, L0_ffn_kan_ln_g0, L0_ffn_kan_ln_b0, L0_ffn_kan_sl_W0, L0_ffn_kan_sl_b0, L0_ffn_kan_ln_g1, L0_ffn_kan_ln_b1, L0_ffn_kan_sl_W1, L0_ffn_kan_sl_b1):
    import jax
    import jax.numpy as jnp

    def _L0_xattn_ref(inputs_q, inputs_kv, attention_mask, Wq, bq, Wk, bk, Wv, bv, Wo, bo):
        import jax, jax.numpy as jnp
        import numpy as np
        B, TQ, TKV, D, H = (4, 64, 512, 128, 8)
        HEAD_DIM = D // H

        def _split_heads(x, h):
            b, t, c = x.shape
            return x.reshape(b, t, h, c // h).transpose(0, 2, 1, 3)
        q = _split_heads(inputs_q @ Wq + bq, H)
        k = _split_heads(inputs_kv @ Wk + bk, H)
        v = _split_heads(inputs_kv @ Wv + bv, H)
        scale = 1.0 / np.sqrt(HEAD_DIM).astype(np.float32)
        scores = jnp.einsum('bhtd,bhTd->bhtT', q, k) * scale
        large_k = jnp.asarray(1e+30, scores.dtype)
        scores = jnp.where(attention_mask[:, None, :, :], scores, -large_k)
        probs = jax.nn.softmax(scores, axis=-1)
        summed = jnp.einsum('bhtT,bhTd->bhtd', probs, v)
        b, h, t, d = summed.shape
        summed = summed.transpose(0, 2, 1, 3).reshape(b, t, h * d)
        wipe = jnp.all(~attention_mask, axis=-1, keepdims=True)
        summed = jnp.where(wipe, jnp.zeros_like(summed), summed)
        return summed @ Wo + bo

    def _L0_attn_ref(inputs):
        import jax, jax.numpy as jnp
        import numpy as np
        DIM = 128
        SQRT_DIM = float(np.sqrt(DIM))
        x = jnp.transpose(inputs, (1, 0, 2))
        scores = jnp.einsum('bsd,btd->bst', x, x) / SQRT_DIM
        attn = jax.nn.softmax(scores, axis=-1)
        out = jnp.einsum('bst,btd->bsd', attn, x)
        return jnp.transpose(out, (1, 0, 2))

    def _L0_ffn_ref(hidden_states, gate_W, mlp_W1, mlp_b1, mlp_W2, mlp_b2, kan_ln_g0, kan_ln_b0, kan_sl_W0, kan_sl_b0, kan_ln_g1, kan_ln_b1, kan_sl_W1, kan_sl_b1):
        import jax, jax.numpy as jnp
        import numpy as np
        NUM_EXPERTS = 8
        TOP_K = 2
        NUM_GRIDS = 8
        INV_DENOM = 0.5
        GRID = np.linspace(-1.2, 0.2, NUM_GRIDS).astype(np.float32)
        LN_EPS = 1e-05

        def _layernorm(x, g, b):
            mu = x.mean(-1, keepdims=True)
            var = x.var(-1, keepdims=True)
            return (x - mu) * jax.lax.rsqrt(var + LN_EPS) * g + b

        def _rswaf(x, grid):
            t = jnp.tanh((x[..., None] - grid) * INV_DENOM)
            return 1.0 - t * t
        B, S, H = hidden_states.shape
        E2, _, F2 = (kan_sl_W0.shape[0], kan_sl_W0.shape[1], kan_sl_W0.shape[2])
        G = NUM_GRIDS
        x = hidden_states.reshape(-1, H)
        T = x.shape[0]
        logits = x @ gate_W
        probs = jax.nn.softmax(logits.astype(jnp.float32), axis=-1)
        rw, sel = jax.lax.top_k(probs, TOP_K)
        rw = rw / rw.sum(axis=-1, keepdims=True)
        w_full = jnp.sum(jax.nn.one_hot(sel, NUM_EXPERTS, dtype=rw.dtype) * rw[..., None], axis=1)
        w_full = w_full.astype(x.dtype)
        h = jnp.einsum('th,ehf->etf', x, mlp_W1) + mlp_b1[:, None, :]
        h = jax.nn.gelu(h, approximate=False)
        mlp_out = jnp.einsum('etf,efh->eth', h, mlp_W2) + mlp_b2[:, None, :]
        grid = jnp.asarray(GRID)
        h0 = _layernorm(x[None], kan_ln_g0[:, None, :], kan_ln_b0[:, None, :])
        basis0 = _rswaf(h0, grid).reshape(E2, T, H * G)
        z = jnp.einsum('eti,eio->eto', basis0, kan_sl_W0) + kan_sl_b0[:, None, :]
        h1 = _layernorm(z, kan_ln_g1[:, None, :], kan_ln_b1[:, None, :])
        basis1 = _rswaf(h1, grid).reshape(E2, T, F2 * G)
        kan_out = jnp.einsum('eti,eio->eto', basis1, kan_sl_W1) + kan_sl_b1[:, None, :]
        expert_out = jnp.concatenate([mlp_out, kan_out], axis=0)
        out = jnp.einsum('eth,te->th', expert_out, w_full)
        return out.reshape(B, S, H)
    x = x + _L0_xattn_ref(_layernorm(x, axis=-1), ctx_1024, mask_BxSxS2_bk0, L0_xattn_Wq, L0_xattn_bq, L0_xattn_Wk, L0_xattn_bk, L0_xattn_Wv, L0_xattn_bv, L0_xattn_Wo, L0_xattn_bo)
    x = x + _L0_attn_ref(_layernorm(x, axis=-1))
    x = x + _L0_ffn_ref(_layernorm(x, axis=-1), L0_ffn_gate_W, L0_ffn_mlp_W1, L0_ffn_mlp_b1, L0_ffn_mlp_W2, L0_ffn_mlp_b2, L0_ffn_kan_ln_g0, L0_ffn_kan_ln_b0, L0_ffn_kan_sl_W0, L0_ffn_kan_sl_b0, L0_ffn_kan_ln_g1, L0_ffn_kan_ln_b1, L0_ffn_kan_sl_W1, L0_ffn_kan_sl_b1)
    return x

_drawn_inputs = setup_inputs


def setup_inputs(seed=0):
    import zlib

    import numpy as np

    out = dict(_drawn_inputs(seed))
    spreads = {'L0_xattn_bq': (0.0, 0.8),
     'L0_xattn_bk': (0.0, 0.8),
     'L0_xattn_bv': (0.0, 0.1),
     'L0_xattn_bo': (0.0, 0.1),
     'L0_ffn_mlp_b1': (0.0, 0.8),
     'L0_ffn_mlp_b2': (0.0, 0.312),
     'L0_ffn_kan_ln_g0': (1.0, 0.6),
     'L0_ffn_kan_ln_b0': (0.0, 0.8),
     'L0_ffn_kan_sl_b0': (0.0, 0.616),
     'L0_ffn_kan_ln_g1': (1.0, 0.6),
     'L0_ffn_kan_ln_b1': (0.0, 0.8),
     'L0_ffn_kan_sl_b1': (0.0, 0.34)}
    factors = {'L0_xattn_Wq': 8.0, 'L0_xattn_Wk': 8.0, 'L0_ffn_mlp_W1': 4.244, 'L0_ffn_mlp_W2': 3.825}
    for name, (base, spread) in spreads.items():
        noise = np.random.default_rng([zlib.crc32(name.encode()), seed]).standard_normal(out[name].shape)
        drawn = base * np.exp(spread * noise) if base else spread * noise
        out[name] = jnp.asarray(drawn.astype(out[name].dtype))
    for name, factor in factors.items():
        out[name] = (out[name] * factor).astype(out[name].dtype)
    return out
```

```python
from contextlib import ExitStack

import concourse.bass as bass
from concourse import mybir
import numpy as np

F32 = mybir.dt.float32
I32 = mybir.dt.int32
U32 = mybir.dt.uint32
U8 = mybir.dt.uint8
ALU = mybir.AluOpType
ACT = mybir.ActivationFunctionType
AX = mybir.AxisListType.X

P = 128
B = 4
H = 8
HD = 16
VW = 32
KEYS = 2048
TILES = KEYS // P
TAIL = 4
HEAD = TILES - TAIL
CREDIT = 1
EPS = 1e-5
NEG = 1e30

EX = 8
E2 = 4
G = 8
GRID = np.linspace(-1.2, 0.2, G).astype(np.float32)
F = 512
F2 = 256
SLOTS = 160
ROUNDS = 4
ROWS = SLOTS * ROUNDS
REST = SLOTS - P
ZP = 120

BQ, BK, G0, B0, SB0, G1, B1, SB1, MB2, MB1, NV = 0, 1, 2, 6, 10, 18, 26, 34, 38, 42, 58
C_ID, C_U, C_HM, C_IOTA, C_EOFF, C_LT, NC = 0, 128, 256, 264, 264 + SLOTS, 272 + SLOTS, 336 + SLOTS


def layer(nc, x, ctxT, mask, Wq, Wk, Wv, Wo, rows2, gateW, KW0, KW1, MW1, MW2, vecs, consts, out):
    y_table = nc.dram_tensor("y_table", [EX * ROWS, P], F32, kind="Internal").ap()
    with ExitStack() as ctx:
        def sb(name, shape, dt=F32):
            return ctx.enter_context(nc.sbuf_tensor(name, shape, dt))

        def sem(name):
            return ctx.enter_context(nc.semaphore(name))

        cst = sb("cst", [P, NC])
        vec = sb("vec", [P, NV])
        hvec = sb("hvec", [P, 32])
        wq = sb("wq", [P, P])
        wk = sb("wk", [P, P])
        wv = sb("wv", [P, P])
        wo = sb("wo", [P, P])
        rows = sb("rows", [P, 2, P])
        gate = sb("gate", [P, EX])
        kw0 = sb("kw0", [P, E2, G, F2])
        mw1 = sb("mw1", [P, E2, F])
        mw2 = sb("mw2", [P, E2, 4, P])
        ones = sb("ones", [P, P])
        mean_w = sb("mean_w", [P, P])
        zeros = sb("zeros", [P, 256])
        xs = sb("xs", [P, B, P])
        xb = sb("xb", [P, B, P])
        xn = sb("xn", [P, B, P])
        x1 = sb("x1", [P, B, P])
        xn1 = sb("xn1", [P, B, P])
        x2 = sb("x2", [P, B, P])
        xf = sb("xf", [P, B, P])
        xln = sb("xln", [P, B, P])
        stats = sb("stats", [P, B, 6])
        mv = sb("mv", [P, B, 2])
        vare = sb("vare", [P, B])
        rstd = sb("rstd", [P, B])
        mhalf = sb("mhalf", [P, B])
        flags = sb("flags", [P, B, TILES])
        hflags = sb("hflags", [1, B])
        flag_i = sb("flag_i", [1, B * TAIL + B], I32)
        notwipe = sb("notwipe", [P, B])
        mx = sb("mx", [P, B, H, TAIL + 1])
        mxb = sb("mxb", [P, B, H])
        mxt = sb("mxt", [P, H])
        den = sb("den", [P, B, H])
        rden = sb("rden", [P, B, H])
        rdw = sb("rdw", [P, B, H])
        sc = sb("sc", [P, B, B])
        scm = sb("scm", [P, B])
        scd = sb("scd", [P, B, B])
        sce = sb("sce", [P, B, B])
        scs = sb("scs", [P, B])
        scr = sb("scr", [P, B])
        scp = sb("scp", [P, B, B])
        lgm = sb("lgm", [P, B])
        lgd = sb("lgd", [P, B, EX])
        lge = sb("lge", [P, B, EX])
        cmp_gt = sb("cmp_gt", [P, B, EX, EX])
        cmp_eq = sb("cmp_eq", [P, B, EX, EX])
        rank = sb("rank", [P, B, EX])
        first = sb("first", [P, 2, B, EX])
        sel = sb("sel", [P, B, EX])
        cum = sb("cum", [P, B + 1, EX])
        wsum = sb("wsum", [P, 2, B])
        wtmp = sb("wtmp", [P, 2, B, EX])
        wden = sb("wden", [P, B])
        wgt = sb("wgt", [P, 2, B])
        posm = sb("posm", [P, B, EX])
        rowid = sb("rowid", [P, B, EX])
        dtmp = sb("dtmp", [P, 2, B, EX])
        destf = sb("destf", [P, 2, B])
        dest = sb("dest", [P, 2, B], U32)
        cmax = sb("cmax", [1, 1])
        over_i = sb("over_i", [1, 1], I32)

        ARENA = 31400
        arena = sb("arena", [P, ARENA])
        at = [0]

        def part(size, pattern=None, **kw):
            a = arena[:, at[0]:at[0] + size]
            at[0] += size
            return a.rearrange(pattern, **kw) if pattern else a

        S = part(2 * TAIL * H * P, "p (u t h k) -> p u t h k", u=2, t=TAIL, h=H)
        PT = part(2 * H * P, "p (u n) -> p u n", u=2)
        V = part(B * TAIL * H * VW, "p (b t h w) -> p b t h w", b=B, t=TAIL, h=H)
        QM = part(H * B * P, "p (h b q) -> p h b q", h=H, b=B)
        kT = part(B * TAIL * P, "p (b n) -> p b n", b=B)
        ctx_t = part(B * TAIL * P, "p (b n) -> p b n", b=B)
        mask_f = part(B * KEYS // 4)
        mbias = part(B * TAIL * P, "p (b t k) -> p b t k", b=B, t=TAIL)
        h_ctx = part(P)
        h_mask = part(P // 4)
        h_bias = part(P)
        h_kT = part(P)
        h_V = part(H * VW, "p (h w) -> p h w", h=H)
        h_S = part(H * P, "p (h k) -> p h k", h=H)
        h_PT = part(H * P)
        xnT = PT[:, 0, 0:B * P]
        qs = PT[:, 1, 0:B * P]
        mask_u8 = mask_f.bitcast(U8).rearrange("p (b k) -> p b k", b=B)
        mask_i32 = mask_f.bitcast(I32).rearrange("p (t w) -> p t w", w=P // 4)
        h_mask_u8 = h_mask.bitcast(U8)
        oT = mask_f[:, 0:B * 256].rearrange("p (b n) -> p b n", b=B)
        on = S[:, 0, 0:2].rearrange("p t h k -> p (t h k)")[:, 0:B * P]
        onT = S[:, 0, 2:4].rearrange("p t h k -> p (t h k)")[:, 0:B * P]
        prod = S[:, 1, 0].rearrange("p h k -> p (h k)")[:, 0:B * P].rearrange("p (t d) -> p t d", t=B)

        at[0] = 0
        T1 = part(2 * G * 2 * SLOTS, "p (u g c s) -> p u g c s", u=2, g=G, c=2)
        SQ1 = part(2 * G * 2 * (SLOTS + 1), "p (u g c s) -> p u g c s", u=2, g=G, c=2)
        T0 = T1[:, :, :, 0]
        SQ0 = SQ1[:, :, :, 0]
        onehot = part(2 * B * SLOTS, "p (u i s) -> p u i s", u=2, i=B)
        xe = part(EX * SLOTS, "p (n s) -> p n s", n=EX)
        zs = part(E2 * 2 * SLOTS, "p (n c s) -> p n c s", n=E2, c=2)
        zd = part(E2 * 2 * SLOTS, "p (n c s) -> p n c s", n=E2, c=2)
        zq = part(E2 * 2 * SLOTS, "p (n c s) -> p n c s", n=E2, c=2)
        var = part(E2 * SLOTS, "p (n s) -> p n s", n=E2)
        rsd = part(E2 * SLOTS, "p (n s) -> p n s", n=E2)
        hT = part(2 * 4 * SLOTS, "p (u c s) -> p u c s", u=2, c=4)
        yT = part(2 * SLOTS, "p (u s) -> p u s", u=2)
        yn = part(EX * 2 * P, "p (n j d) -> p n j d", n=EX, j=2)
        cz = part(E2 * 2, "p (n c) -> p n c", n=E2)
        cy = part(E2)
        xfT = part(B * P)
        yg = part(2 * B * P, "p (k i d) -> p k i d", k=2, i=B)
        kw1 = part(E2 * 2 * G * P, "p (e c g o) -> p e c g o", e=E2, c=2, g=G)
        fin = onehot.rearrange("p u i s -> p (u i s)")[:, 0:B * P].rearrange("p (i d) -> p i d", i=B)

        ident = cst[:, C_ID:C_ID + P]
        upper = cst[:, C_U:C_U + P]
        hmask = cst[:, C_HM:C_HM + H]
        iota1 = cst[:, C_IOTA:C_IOTA + SLOTS]
        eoff = cst[:, C_EOFF:C_EOFF + EX]
        lower = cst[:, C_LT:C_LT + EX * EX].rearrange("p (a b) -> p a b", a=EX)

        A = [ctx.enter_context(nc.psum_tensor(f"A{i}", [P, 1024], F32)) for i in range(2)]
        C = [ctx.enter_context(nc.psum_tensor(f"C{i}", [P, 512], F32)) for i in range(2)]
        D = [ctx.enter_context(nc.psum_tensor(f"D{i}", [P, 512], F32)) for i in range(2)]
        OV = D[0]
        X = [C[0], C[1]]
        Z = [A[0][:, 0:512], A[0][:, 512:1024]]
        MEAN = A[1][:, 0:512]
        VAR = A[1][:, 512:1024]
        Y = D[0]
        YN = D[1]

        x_in = sem("x_in")
        cst_in = sem("cst_in")
        wq_in = sem("wq_in")
        wkv_in = sem("wkv_in")
        mask_in = sem("mask_in")
        ctx_in = [sem(f"ctx_in{b}") for b in range(B)]
        wo_in = sem("wo_in")
        ffn_in = sem("ffn_in")
        kw1_in = sem("kw1_in")
        ones_made = sem("ones_made")
        pads_made = sem("pads_made")
        vhalf_made = sem("vhalf_made")
        dv = sem("dv")
        var_ready = sem("var_ready")
        eps_added = sem("eps_added")
        rstd_made = sem("rstd_made")
        xn_made = sem("xn_made")
        xnT_made = sem("xnT_made")
        xnT_kept = sem("xnT_kept")
        qT_made = sem("qT_made")
        qm_made = sem("qm_made")
        kv_made = sem("kv_made")
        kv_kept = sem("kv_kept")
        flags_made = sem("flags_made")
        anyq_made = sem("anyq_made")
        flag_ready = sem("flag_ready")
        bias_made = sem("bias_made")
        xb_made = sem("xb_made")
        scores_made = sem("scores_made")
        scores_kept = sem("scores_kept")
        tile_max = sem("tile_max")
        batch_max = sem("batch_max")
        shifted = sem("shifted")
        probs_made = sem("probs_made")
        probsT_made = sem("probsT_made")
        probsT_kept = sem("probsT_kept")
        ov_zeroed = sem("ov_zeroed")
        mixed = sem("mixed")
        oT_kept = sem("oT_kept")
        h_in = sem("h_in")
        h_biased = sem("h_biased")
        h_kv = sem("h_kv")
        h_kvkept = sem("h_kvkept")
        h_scores = sem("h_scores")
        h_kept = sem("h_kept")
        h_max = sem("h_max")
        h_vec = sem("h_vec")
        h_probs = sem("h_probs")
        h_T = sem("h_T")
        h_Tkept = sem("h_Tkept")
        h_mixed = sem("h_mixed")
        on_made = sem("on_made")
        o_tok = sem("o_tok")
        onT_made = sem("onT_made")
        onT_kept = sem("onT_kept")
        proj_made = sem("proj_made")
        sc_ready = sem("sc_ready")
        sc_exp = sem("sc_exp")
        xf_made = sem("xf_made")
        xln_made = sem("xln_made")
        xfT_made = sem("xfT_made")
        xfT_kept = sem("xfT_kept")
        logits_made = sem("logits_made")
        lg_ready = sem("lg_ready")
        lg_exp = sem("lg_exp")
        sel_made = sem("sel_made")
        pos_made = sem("pos_made")
        over_made = sem("over_made")
        dest_made = sem("dest_made")
        sq_ones = sem("sq_ones")
        onehot_made = sem("onehot_made")
        gathered = sem("gathered")
        xe_kept = sem("xe_kept")
        t0_made = sem("t0_made")
        sq0_made = sem("sq0_made")
        z_made = sem("z_made")
        z_kept = sem("z_kept")
        mean_made = sem("mean_made")
        zd_made = sem("zd_made")
        zq_made = sem("zq_made")
        vars_made = sem("vars_made")
        vars_kept = sem("vars_kept")
        std_made = sem("std_made")
        hid_made = sem("hid_made")
        hid_kept = sem("hid_kept")
        u1_made = sem("u1_made")
        t1_made = sem("t1_made")
        sq1_made = sem("sq1_made")
        l1_done = sem("l1_done")
        y_made = sem("y_made")
        yT_kept = sem("yT_kept")
        yn_made = sem("yn_made")
        yn_kept = sem("yn_kept")
        y_stored = sem("y_stored")
        fv = sem("fv")
        rows_cleared = sem("rows_cleared")
        y_back = sem("y_back")
        fin_made = sem("fin_made")
        out_done = sem("out_done")
        STORED = EX * 32

        def tanh_bias(g):
            return float(-0.5 * GRID[g])

        block = ctx.enter_context(nc.Block())

        def tile_no(b, t):
            return b * TAIL + t

        def maxima_no(b):
            return 0 if b == 0 else 2 * b - 1

        def sums_no(b):
            return 2 * b + 2 if b < B - 1 else 2 * B - 1

        def load_flags(eng):
            eng.wait_ge(flag_ready, 2)
            tail = [[eng.value_load(flag_i[0:1, tile_no(b, t):tile_no(b, t) + 1]) for t in range(TAIL)] for b in range(B)]
            head = [eng.value_load(flag_i[0:1, B * TAIL + b:B * TAIL + b + 1]) for b in range(B)]
            return tail, head

        def when(eng, flag, body, passed_over):
            with eng.If(flag > 0):
                body()
            with eng.Else():
                eng.drain()
                for s, n in passed_over:
                    eng.sem_inc(s, n)

        @block.sync
        def _(sp):
            sp.dma_start(xs[:], x).then_inc(x_in, 16)
            sp.dma_start(mask_u8, mask).then_inc(mask_in, 16)
            for b in range(B):
                sp.dma_start(ctx_t[:, b], ctxT[b, :, HEAD * P:]).then_inc(ctx_in[b], 16)
            sp.dma_start(mw1[:], MW1).then_inc(ffn_in, 16)
            sp.dma_start(mw2[:], MW2).then_inc(ffn_in, 16)
            sp.dma_start(gate[:], gateW).then_inc(ffn_in, 16)
            sp.wait_ge(ones_made, 4)
            for e in range(EX):
                sp.dma_start(y_table[e * ROWS + SLOTS:(e + 1) * ROWS, :].rearrange("(p r) w -> p r w", p=ZP),
                             zeros[0:ZP, 0:P].unsqueeze(1).broadcast_to([ZP, (ROWS - SLOTS) // ZP, P])).then_inc(rows_cleared, 16)
            tail, head = load_flags(sp)

            def stream(b, seq):
                def body():
                    with sp.Fori(0, HEAD) as i:
                        sp.wait_ge(h_kv, CREDIT + i + HEAD * seq)
                        sp.wait_ge(h_biased, CREDIT + i + HEAD * seq)
                        sp.dma_start(h_ctx, ctxT[b, :, bass.ds(i * P, P)]).then_inc(h_in, 16)
                        sp.dma_start(h_mask_u8, mask[:, b, bass.ds(i * P, P)]).then_inc(h_in, 16)
                    sp.wait_ge(h_in, 32 * HEAD * (seq + 1))
                when(sp, head[b], body, [(h_in, 32 * HEAD)])

            stream(0, maxima_no(0))
            for b in range(B):
                if b + 1 < B:
                    stream(b + 1, maxima_no(b + 1))
                stream(b, sums_no(b))
            sp.wait_ge(o_tok, 1)
            sp.dma_start(kw1, KW1).then_inc(kw1_in, 16)

            def store_round(off, row):
                for n in range(EX):
                    e = n
                    sp.wait_ge(yn_kept, off * EX + n + 1)
                    sp.dma_start(y_table[bass.ds(row + e * ROWS, P), :], yn[:, n, 0]).then_inc(y_stored, 16)
                    sp.dma_start(y_table[bass.ds(row + e * ROWS + P, REST), :], yn[0:REST, n, 1]).then_inc(y_stored, 16)

            store_round(0, 0)
            sp.wait_ge(rows_cleared, 16 * EX)
            sp.wait_ge(over_made, 1)
            over = sp.value_load(over_i[0:1, 0:1])
            with sp.If(over > 0):
                with sp.Fori(1, ROUNDS) as r:
                    store_round(r, r * SLOTS)
            sp.wait_ge(fin_made, B)
            sp.dma_start(out, fin).then_inc(out_done, 16)
            sp.wait_ge(out_done, 16)

        @block.gpsimd
        def _(pool):
            nc.gpsimd.memset(ones[:], 1.0).then_inc(ones_made, 1)
            nc.gpsimd.memset(mhalf[:], -0.5).then_inc(ones_made, 1)
            nc.gpsimd.memset(mean_w[:], 1.0 / F2).then_inc(ones_made, 1)
            nc.gpsimd.memset(zeros[:], 0.0).then_inc(ones_made, 1)
            norm = [0]

            def rstd_step():
                pool.wait_ge(var_ready, norm[0] + 1)
                nc.gpsimd.tensor_scalar(vare[:], mv[:, :, 1], EPS, None, ALU.add).then_inc(eps_added, 1)
                pool.wait_ge(eps_added, norm[0] + 1)
                nc.gpsimd.tensor_tensor(rstd[:], vare[:], mhalf[:], ALU.pow).then_inc(rstd_made, 1)
                norm[0] += 1

            pool.wait_ge(ones_made, 2)
            rstd_step()
            for v in (V.rearrange("p b t h w -> p (b t h) w"), h_V):
                nc.gpsimd.memset(v[:, :, HD + 1:], 0.0).then_inc(pads_made, 1)
                nc.gpsimd.memset(v[:, :, HD:HD + 1], 1.0).then_inc(pads_made, 1)
            pool.wait_ge(mask_in, 16)
            for b in range(B):
                nc.gpsimd.tensor_scalar(mbias[:, b], mask_u8[:, b, HEAD * P:].rearrange("p (t k) -> p t k", t=TAIL),
                                        NEG, -NEG, ALU.mult, ALU.add).then_inc(bias_made, 1)
            pool.wait_ge(wo_in, 32)
            for b in range(B):
                nc.gpsimd.tensor_tensor(xb[:, b], xs[:, b], rows[:, 1], ALU.add).then_inc(xb_made, 1)
            for _ in range(3):
                rstd_step()
            pool.wait_ge(over_made, 1)
            over = pool.value_load(over_i[0:1, 0:1])
            pool.wait_ge(y_stored, STORED)
            pool.wait_ge(rows_cleared, 16 * EX)
            with pool.If(over > 0):
                pool.wait_ge(y_stored, ROUNDS * STORED)
            pool.wait_ge(dest_made, 1)
            for i in range(B):
                for k in range(2):
                    pool.indirect_dma_start(out=yg[:, k, i], out_offset=None, in_=y_table,
                                            in_offset=bass.IndirectOffsetOnAxis(ap=dest[:, k, i:i + 1], axis=0)
                                            ).then_inc(y_back, 16)

        @block.scalar
        def _(act):
            for s in (h_kvkept, h_Tkept):
                act.sem_inc(s, CREDIT)
            act.dma_start(cst[:], consts).then_inc(cst_in, 16)
            act.dma_start(vec[:], vecs).then_inc(cst_in, 16)
            act.dma_start(wq[:], Wq).then_inc(wq_in, 16)
            act.dma_start(wk[:], Wk).then_inc(wkv_in, 16)
            act.dma_start(wv[:], Wv).then_inc(wkv_in, 16)
            act.dma_start(wo[:], Wo).then_inc(wo_in, 16)
            act.dma_start(rows[:], rows2.partition_broadcast(P)).then_inc(wo_in, 16)
            act.dma_start(kw0[:], KW0).then_inc(ffn_in, 16)
            act.wait_ge(cst_in, 32)
            for b in range(B):
                act.wait_ge(kv_made, b + 1)
                act.activation(kT[:, b], A[0][:, (b % 2) * 512:(b % 2 + 1) * 512], ACT.Identity,
                               bias=vec[:, BK:BK + 1], scale=1.0).then_inc(kv_kept, 1)
                act.activation(V[:, b, :, :, 0:HD],
                               A[1][:, (b % 2) * 512:(b % 2 + 1) * 512].rearrange("p (t h w) -> p t h w", t=TAIL, h=H),
                               ACT.Copy).then_inc(kv_kept, 1)
            tail, head = load_flags(act)

            def stream(b, seq, sums):
                def body():
                    with act.Fori(0, HEAD) as i:
                        act.wait_ge(h_kv, CREDIT + i + HEAD * seq + 1)
                        act.wait_ge(h_scores, CREDIT + i + HEAD * seq)
                        act.activation(h_kT, C[0][:, 0:P], ACT.Identity, bias=vec[:, BK:BK + 1], scale=1.0
                                       ).then_inc(h_kvkept, 1)
                        act.wait_ge(h_mixed, CREDIT + (i + HEAD * b if sums else HEAD * max(b - 1, 0)))
                        act.activation(h_V[:, :, 0:HD], C[0][:, P:2 * P].rearrange("p (h w) -> p h w", h=H), ACT.Copy
                                       ).then_inc(h_kvkept, 1)
                        if sums:
                            act.wait_ge(h_vec, CREDIT + i + HEAD * seq + 1)
                            act.activation(h_S, h_S, ACT.Exp).then_inc(h_probs, 1)
                            for g in range(2):
                                act.wait_ge(h_T, CREDIT + i * 2 + 2 * HEAD * b + g + 1)
                                act.activation(h_PT[:, g * 512:(g + 1) * 512], C[g][:, :], ACT.Copy).then_inc(h_Tkept, 1)
                when(act, head[b], body,
                     [(h_kvkept, 2 * HEAD)] + ([(h_probs, HEAD), (h_Tkept, 2 * HEAD)] if sums else []))

            def probs(b, t):
                k = tile_no(b, t)

                def body():
                    s = S[:, b % 2, t]
                    act.wait_ge(shifted, k + 1)
                    act.activation(s, s, ACT.Exp).then_inc(probs_made, 1)
                    if k >= 2:
                        act.wait_ge(mixed, k - 1)
                    for g in range(2):
                        act.wait_ge(probsT_made, 2 * k + g + 1)
                        act.activation(PT[:, k % 2, g * 512:(g + 1) * 512], C[g][:, :], ACT.Copy).then_inc(probsT_kept, 1)
                when(act, tail[b][t], body, [(probs_made, 1), (probsT_kept, 2)])

            stream(0, maxima_no(0), False)
            for b in range(B):
                if b + 1 < B:
                    stream(b + 1, maxima_no(b + 1), False)
                stream(b, sums_no(b), True)
                for t in range(TAIL):
                    probs(b, t)
            act.wait_ge(onT_made, 1)
            act.activation(onT, C[0][:, :], ACT.Copy).then_inc(onT_kept, 1)
            act.wait_ge(sc_ready, 1)
            act.activation(sce[:], scd[:], ACT.Exp, scale=float(P) ** -0.5).then_inc(sc_exp, 1)
            act.wait_ge(xfT_made, 1)
            act.activation(xfT, C[0][:, :], ACT.Copy).then_inc(xfT_kept, 1)
            act.wait_ge(lg_ready, 1)
            act.activation(lge[:], lgd[:], ACT.Exp).then_inc(lg_exp, 1)

            def ffn(r, again):
                if again:
                    act.wait_ge(y_stored, r * STORED)

                def basis0(n):
                    act.wait_ge(xe_kept, r * EX + n + 1)
                    for g in range(G):
                        if g % 4 == 0 and n >= 2:
                            act.wait_ge(sq0_made, r * 8 + 2 * (n - 2) + g // 4 + 1)
                        i = act.activation(T0[:, n % 2, g], xe[:, n], ACT.Tanh, bias=tanh_bias(g))
                        if g % 4 == 3:
                            i.then_inc(t0_made, 1)

                def hidden(m):
                    for c in range(4):
                        k = 4 * m + c
                        act.wait_ge(hid_made, r * 16 + k + 1)
                        if c == 0 and m >= 2:
                            act.wait_ge(y_made, r * EX + m - 1)
                        act.activation(hT[:, m % 2, c], Z[k % 2][:, 0:SLOTS], ACT.Gelu,
                                       bias=vec[:, MB1 + k:MB1 + k + 1], scale=1.0).then_inc(hid_kept, 1)

                def basis1(n):
                    act.wait_ge(u1_made, r * E2 + n + 1)
                    for g in range(G):
                        if g % 2 == 0 and n >= 2:
                            act.wait_ge(sq1_made, r * 16 + 4 * (n - 2) + g // 2 + 1)
                        if n == 0 and g == 0:
                            act.wait_ge(sq0_made, r * 8 + 8)
                        i = act.activation(T1[:, n % 2, g], zs[:, n], ACT.Tanh, bias=tanh_bias(g))
                        if g % 2 == 1:
                            i.then_inc(t1_made, 1)

                def rows_out(n):
                    act.wait_ge(yn_made, r * EX + n + 1)
                    act.activation(yn[:, n, 0], YN[:, 0:P], ACT.Copy)
                    act.activation(yn[0:REST, n, 1], YN[0:REST, P:2 * P], ACT.Copy).then_inc(yn_kept, 1)

                for n in range(E2):
                    basis0(n)
                hidden(0)
                hidden(1)
                act.wait_ge(vars_kept, r * E2 + E2)
                act.activation(var, var, ACT.Sqrt).then_inc(std_made, 1)
                hidden(2)
                rows_out(0)
                hidden(3)
                rows_out(1)
                rows_out(2)
                for n in range(E2):
                    basis1(n)
                    rows_out(3 + n)
                rows_out(7)

            act.wait_ge(cst_in, 32)
            ffn(0, False)
            act.wait_ge(over_made, 1)
            over = act.value_load(over_i[0:1, 0:1])
            with act.If(over > 0):
                with act.Fori(1, ROUNDS) as r:
                    ffn(r, True)

        @block.tensor
        def _(pe):
            mm = nc.tensor.matmul
            for s in (h_kv, h_scores, h_T, h_mixed):
                pe.sem_inc(s, CREDIT)
            pe.wait_ge(cst_in, 32)
            for b in range(B):
                pe.wait_ge(xn_made, b + 1)
                last = nc.tensor.transpose(C[0][:, b * P:(b + 1) * P], xn[:, b], ident)
            last.then_inc(xnT_made, 1)
            pe.wait_ge(wkv_in, 32)

            def keys_values(b):
                pe.wait_ge(ctx_in[b], 16)
                if b >= 2:
                    pe.wait_ge(kv_kept, 2 * (b - 1))
                mm(A[0][:, (b % 2) * 512:(b % 2 + 1) * 512], wk[:], ctx_t[:, b], start=True, stop=True)
                for t in range(TAIL):
                    last = mm(A[1][:, (b % 2) * 512 + t * P:(b % 2) * 512 + (t + 1) * P],
                              ctx_t[:, b, t * P:(t + 1) * P], wv[:], start=True, stop=True)
                last.then_inc(kv_made, 1)

            pe.wait_ge(xnT_kept, 1)
            pe.wait_ge(wq_in, 16)
            mm(C[1][:, :], wq[:], xnT, start=True, stop=True).then_inc(qT_made, 1)
            pe.wait_ge(ones_made, 4)
            pe.wait_ge(flags_made, 2)
            mm(D[1][0:1, 0:B * TILES], ones[:, 0:1], flags[:].rearrange("p b t -> p (b t)"), start=True, stop=True
               ).then_inc(anyq_made, 1)
            for b in range(B):
                keys_values(b)
            pe.wait_ge(kv_kept, 2 * B)
            tail, head = load_flags(pe)
            pe.wait_ge(pads_made, 4)

            def stream(b, seq, sums):
                def body():
                    pe.wait_ge(scores_kept, tile_no(b + 1, 0) if sums and b + 1 < B else tile_no(b, 0) if not sums
                               else B * TAIL) if (b or sums) else None
                    if sums or b:
                        if 2 * TAIL * (b if sums else b - 1) > 0:
                            pe.wait_ge(probsT_kept, 2 * TAIL * (b if sums else b - 1))
                    with pe.Fori(0, HEAD) as i:
                        pe.wait_ge(h_in, i * 32 + 32 * (HEAD * seq + 1))
                        pe.wait_ge(h_kvkept, CREDIT + i * 2 + 2 * HEAD * seq)
                        if sums:
                            pe.wait_ge(h_Tkept, CREDIT + i * 2 + 2 * HEAD * b)
                        mm(C[0][:, 0:P], wk[:], h_ctx, start=True, stop=True)
                        mm(C[0][:, P:2 * P], h_ctx, wv[:], start=True, stop=True).then_inc(h_kv, 1)
                        pe.wait_ge(h_kvkept, CREDIT + i * 2 + 2 * HEAD * seq + 2)
                        pe.wait_ge(h_kept, CREDIT + i + HEAD * seq)
                        for h in range(H):
                            last = mm(A[0][:, h * P:(h + 1) * P], QM[:, h, b], h_kT, start=True, stop=True)
                        last.then_inc(h_scores, 1)
                        if sums:
                            pe.wait_ge(h_probs, i + HEAD * b + 1)
                            for g in range(2):
                                for j in range(4):
                                    last = nc.tensor.transpose(C[g][:, j * P:(j + 1) * P], h_S[:, 4 * g + j], ident)
                                last.then_inc(h_T, 1)
                            pe.wait_ge(h_Tkept, CREDIT + i * 2 + 2 * HEAD * b + 2)
                            for h in range(H):
                                last = mm(OV[VW * (h % 4):VW * (h % 4 + 1), (h // 4) * P:(h // 4 + 1) * P], h_V[:, h],
                                          h_PT[:, h * P:(h + 1) * P], start=False, stop=True, skip_group_check=True)
                            last.then_inc(h_mixed, 1)
                    pe.wait_ge(h_kept, CREDIT + HEAD * (seq + 1))
                when(pe, head[b], body, [(h_kv, HEAD), (h_scores, HEAD)]
                     + ([(h_T, 2 * HEAD), (h_mixed, HEAD)] if sums else []))

            def scores(b, t):
                k = tile_no(b, t)

                def body():
                    if k >= 2:
                        pe.wait_ge(scores_kept, k - 1)
                    for h in range(H):
                        last = mm(A[k % 2][:, h * P:(h + 1) * P], QM[:, h, b], kT[:, b, t * P:(t + 1) * P],
                                  start=True, stop=True)
                    last.then_inc(scores_made, 1)
                when(pe, tail[b][t], body, [(scores_made, 1)])

            def transposes(b, t):
                k = tile_no(b, t)

                def body():
                    pe.wait_ge(probs_made, k + 1)
                    for g in range(2):
                        if k:
                            pe.wait_ge(probsT_kept, 2 * k - 1 + g)
                        for j in range(4):
                            last = nc.tensor.transpose(C[g][:, j * P:(j + 1) * P], S[:, b % 2, t, 4 * g + j], ident)
                        last.then_inc(probsT_made, 1)
                when(pe, tail[b][t], body, [(probsT_made, 2)])

            def mix(b, t):
                k = tile_no(b, t)

                def body():
                    pe.wait_ge(probsT_kept, 2 * k + 2)
                    for h in range(H):
                        last = mm(OV[VW * (h % 4):VW * (h % 4 + 1), (h // 4) * P:(h // 4 + 1) * P], V[:, b, t, h],
                                  PT[:, k % 2, h * P:(h + 1) * P], start=False, stop=True, skip_group_check=True)
                    last.then_inc(mixed, 1)
                when(pe, tail[b][t], body, [(mixed, 1)])

            pe.wait_ge(qm_made, H)
            stream(0, maxima_no(0), False)
            for t in range(TAIL):
                scores(0, t)
            for b in range(B):
                if b + 1 < B:
                    stream(b + 1, maxima_no(b + 1), False)
                if b:
                    pe.wait_ge(oT_kept, b)
                mm(OV[:, 0:256], zeros[:, 0:P], zeros[:, :], start=True, stop=True, skip_group_check=True
                   ).then_inc(ov_zeroed, 1)
                stream(b, sums_no(b), True)
                for t in range(TAIL):
                    if b + 1 < B:
                        scores(b + 1, t)
                    transposes(b, t)
                    if t:
                        mix(b, t - 1)
                mix(b, TAIL - 1)
            pe.wait_ge(scores_kept, B * TAIL)
            pe.wait_ge(oT_kept, B)
            for b in range(B):
                for g in range(2):
                    n = 2 * b + g
                    last = nc.tensor.transpose(A[0][:, n * P:(n + 1) * P], oT[:, b, g * P:(g + 1) * P], ident)
            last.then_inc(o_tok, 1)
            pe.wait_ge(on_made, B)
            pe.wait_ge(probsT_kept, 2 * B * TAIL)
            for b in range(B):
                last = nc.tensor.transpose(C[0][:, b * P:(b + 1) * P], on[:, b * P:(b + 1) * P], ident)
            last.then_inc(onT_made, 1)
            pe.wait_ge(onT_kept, 1)
            pe.wait_ge(wo_in, 32)
            for b in range(B):
                last = mm(C[1][:, b * P:(b + 1) * P], onT[:, b * P:(b + 1) * P], wo[:], start=True, stop=True)
            last.then_inc(proj_made, 1)
            pe.wait_ge(ffn_in, 64)
            for b in range(B):
                pe.wait_ge(xf_made, b + 1)
                last = nc.tensor.transpose(C[0][:, b * P:(b + 1) * P], xf[:, b], ident)
            last.then_inc(xfT_made, 1)
            pe.wait_ge(xfT_kept, 1)
            for b in range(B):
                last = mm(D[1][:, b * EX:(b + 1) * EX], xfT[:, b * P:(b + 1) * P], gate[:], start=True, stop=True)
            last.then_inc(logits_made, 1)
            pe.wait_ge(sel_made, 2)
            mm(D[1][:, 0:B * EX], upper, sel[:].rearrange("p i e -> p (i e)"), start=True, stop=False)
            mm(D[1][:, 0:B * EX], ones[:], cum[:, 0:B].rearrange("p i e -> p (i e)"), start=False, stop=True)
            mm(D[1][:, 64:64 + EX], ones[:], cum[:, B], start=True, stop=True).then_inc(pos_made, 1)

            def ffn(r, again):
                if again:
                    pe.wait_ge(y_stored, r * STORED)

                def gather(n):
                    src = xln if n < E2 else xf
                    pe.wait_ge(onehot_made, r * EX + n + 1)
                    if n >= 2:
                        pe.wait_ge(xe_kept, r * EX + n - 1)
                    for i in range(B):
                        last = mm(X[n % 2][:, 0:SLOTS], src[:, i], onehot[:, n % 2, i], start=(i == 0), stop=(i == B - 1))
                    last.then_inc(gathered, 1)

                def layer0(n):
                    if n >= 2:
                        pe.wait_ge(z_kept, r * E2 + n - 1)
                    for c in range(2):
                        for g in range(G):
                            if c == 0 and g % 4 == 0:
                                pe.wait_ge(sq0_made, r * 8 + 2 * n + g // 4 + 1)
                            last = mm(Z[n % 2][:, c * (SLOTS + 1):(c + 1) * (SLOTS + 1)], kw0[:, n, g, c * P:(c + 1) * P],
                                      SQ0[:, n % 2, g], start=(g == 0), stop=(g == G - 1))
                    last.then_inc(z_made, 1)

                def means(n):
                    pe.wait_ge(z_kept, r * E2 + n + 1)
                    if n:
                        pe.wait_ge(zd_made, r * E2 + n)
                    for c in range(2):
                        last = mm(MEAN[:, 0:SLOTS], mean_w[:], zs[:, n, c], start=(c == 0), stop=(c == 1))
                    last.then_inc(mean_made, 1)

                def variances(n):
                    pe.wait_ge(zq_made, r * E2 + n + 1)
                    if n:
                        pe.wait_ge(vars_kept, r * E2 + n)
                    for c in range(2):
                        last = mm(VAR[:, 0:SLOTS], mean_w[:], zq[:, n, c], start=(c == 0), stop=(c == 1))
                    last.then_inc(vars_made, 1)

                def up(m):
                    pe.wait_ge(xe_kept, r * EX + E2 + m + 1)
                    for c in range(4):
                        k = 4 * m + c
                        if k >= 2:
                            pe.wait_ge(hid_kept, r * 16 + k - 1)
                        mm(Z[k % 2][:, 0:SLOTS], mw1[:, m, c * P:(c + 1) * P], xe[:, E2 + m], start=True, stop=True
                           ).then_inc(hid_made, 1)

                def down(m):
                    pe.wait_ge(hid_kept, r * 16 + 4 * m + 4)
                    if m:
                        pe.wait_ge(yT_kept, r * EX + m)
                    for c in range(4):
                        last = mm(Y[:, 0:SLOTS], mw2[:, m, c], hT[:, m % 2, c], start=(c == 0), stop=(c == 3))
                    last.then_inc(y_made, 1)

                def layer1(n):
                    pe.wait_ge(yT_kept, r * EX + E2 + n)
                    for g in range(G):
                        if g % 2 == 0:
                            pe.wait_ge(sq1_made, r * 16 + 4 * n + g // 2 + 1)
                        for c in range(2):
                            last = mm(Y[:, 0:SLOTS + 1], kw1[:, n, c, g], SQ1[:, n % 2, g, c],
                                      start=(g == 0 and c == 0), stop=(g == G - 1 and c == 1))
                    last.then_inc(y_made, 1)

                def to_rows(n):
                    pe.wait_ge(yT_kept, r * EX + n + 1)
                    if n:
                        pe.wait_ge(yn_kept, r * EX + n)
                    nc.tensor.transpose(YN[:, 0:P], yT[:, n % 2, 0:P], ident)
                    nc.tensor.transpose(YN[0:REST, P:2 * P], yT[:, n % 2, P:SLOTS], ident).then_inc(yn_made, 1)

                gather(0)
                gather(1)
                for n in range(E2):
                    layer0(n)
                    gather(n + 2)
                    if n:
                        means(n - 1)
                    if n >= 2:
                        variances(n - 2)
                pe.wait_ge(z_kept, r * E2 + E2)
                up(0)
                means(3)
                gather(6)
                variances(2)
                gather(7)
                up(1)
                variances(3)
                down(0)
                up(2)
                to_rows(0)
                down(1)
                up(3)
                to_rows(1)
                down(2)
                down(3)
                to_rows(2)
                pe.wait_ge(kw1_in, 16)
                for n in range(E2):
                    layer1(n)
                    to_rows(3 + n)
                to_rows(7)

            ffn(0, False)
            pe.wait_ge(over_made, 1)
            over = pe.value_load(over_i[0:1, 0:1])
            with pe.If(over > 0):
                with pe.Fori(1, ROUNDS) as r:
                    ffn(r, True)

        @block.vector
        def _(dve):
            v = nc.vector
            for s in (h_biased, h_kept, h_vec):
                dve.sem_inc(s, CREDIT)
            count = [0]

            def own(ins):
                count[0] += 1
                ins.then_inc(dv, 1)

            def own_done():
                dve.wait_ge(dv, count[0])

            norms = [0]

            def layer_norm(src, dst, made, ready=None):
                for b in range(B):
                    if ready:
                        ready(b)
                    own(v.bn_stats(stats[:, b], src[:, b]))
                for b in range(B):
                    dve.wait_ge(dv, count[0] - (B - 1) if b == 0 else count[0] - (B - 1) + 0)
                    i = v.bn_aggr(mv[:, b], stats[:, b])
                    if b < B - 1:
                        own(i)
                    else:
                        i.then_inc(var_ready, 1)
                own_done()
                norms[0] += 1
                dve.wait_ge(var_ready, norms[0])
                dve.wait_ge(rstd_made, norms[0])
                for b in range(B):
                    v.tensor_scalar(dst[:, b], src[:, b], mv[:, b, 0:1], rstd[:, b:b + 1], ALU.subtract, ALU.mult
                                    ).then_inc(made, 1)

            own(v.memset(mx[:], -NEG))
            dve.wait_ge(x_in, 16)
            layer_norm(xs, xn, xn_made)
            dve.wait_ge(mask_in, 16)
            own(v.tensor_reduce(flags[:].rearrange("p b t -> p (b t)"), mask_i32, AX, ALU.max))
            own_done()
            v.tensor_scalar(flags[:], flags[:], 0.0, None, ALU.is_gt).then_inc(flags_made, 1)
            dve.wait_ge(flags_made, 1)
            v.tensor_reduce(notwipe[:], flags[:], AX, ALU.max).then_inc(flags_made, 1)
            dve.wait_ge(xnT_made, 1)
            v.tensor_copy(xnT, C[0][:, :]).then_inc(xnT_kept, 1)
            dve.wait_ge(anyq_made, 1)
            anyq = D[1][0:1, 0:B * TILES].rearrange("p (b t) -> p b t", b=B)
            v.tensor_copy(flag_i[0:1, 0:B * TAIL].rearrange("p (b t) -> p b t", b=B), anyq[:, :, HEAD:]).then_inc(flag_ready, 1)
            v.tensor_reduce(flag_i[0:1, B * TAIL:], anyq[:, :, 0:HEAD], AX, ALU.max).then_inc(flag_ready, 1)
            dve.wait_ge(qT_made, 1)
            dve.wait_ge(cst_in, 32)
            own(v.tensor_scalar(qs, C[1][:, :], vec[:, BQ:BQ + 1], float(HD) ** -0.5, ALU.add, ALU.mult))
            own_done()
            for h in range(H):
                v.tensor_scalar(QM[:, h].rearrange("p b q -> p (b q)"), qs, hmask[:, h:h + 1], None, ALU.mult
                                ).then_inc(qm_made, 1)
            own(v.tensor_scalar(hvec[:, 0:8], vec[:, G0:G0 + 8], 0.5, None, ALU.mult))
            own(v.tensor_scalar(hvec[:, 8:24], vec[:, G1:G1 + 16], 0.5, None, ALU.mult))
            tail, head = load_flags(dve)
            dve.wait_ge(bias_made, B)

            def bias(ap):
                return ap.unsqueeze(1).broadcast_to([P, H, P])

            def spread(ap, n):
                return ap.unsqueeze(2).broadcast_to([P, H, n])

            def stream(b, seq, sums):
                def body():
                    with dve.Fori(0, HEAD) as i:
                        dve.wait_ge(h_in, i * 32 + 32 * (HEAD * seq + 1))
                        dve.wait_ge(h_vec, CREDIT + i + HEAD * seq)
                        v.tensor_scalar(h_bias, h_mask_u8, NEG, -NEG, ALU.mult, ALU.add).then_inc(h_biased, 1)
                        dve.wait_ge(h_scores, CREDIT + i + HEAD * seq + 1)
                        dve.wait_ge(h_biased, CREDIT + i + HEAD * seq + 1)
                        if sums:
                            dve.wait_ge(h_T, CREDIT + i * 2 + 2 * HEAD * b)
                        elif b > 1:
                            dve.wait_ge(h_T, CREDIT + 2 * HEAD * (b - 1))
                        v.tensor_tensor(h_S, A[0][:, :].rearrange("p (h k) -> p h k", h=H), bias(h_bias), ALU.add
                                        ).then_inc(h_kept, 1)
                        dve.wait_ge(h_kept, CREDIT + i + HEAD * seq + 1)
                        if sums:
                            v.tensor_tensor(h_S, h_S, spread(mxb[:, b], P), ALU.subtract).then_inc(h_vec, 1)
                        else:
                            v.tensor_reduce(mxt[:], h_S, AX, ALU.max).then_inc(h_max, 1)
                            dve.wait_ge(h_max, i + HEAD * b + 1)
                            v.tensor_tensor(mx[:, b, :, TAIL], mx[:, b, :, TAIL], mxt[:], ALU.max).then_inc(h_vec, 1)
                when(dve, head[b], body, [(h_biased, HEAD), (h_kept, HEAD), (h_vec, HEAD)] + ([] if sums else [(h_max, HEAD)]))

            def keep_scores(b, t):
                k = tile_no(b, t)

                def body():
                    dve.wait_ge(scores_made, k + 1)
                    if b >= 2:
                        dve.wait_ge(probsT_made, 2 * tile_no(b - 2, t) + 2)
                    s = S[:, b % 2, t]
                    v.tensor_tensor(s, A[k % 2][:, :].rearrange("p (h k) -> p h k", h=H), bias(mbias[:, b, t]), ALU.add
                                    ).then_inc(scores_kept, 1)
                    dve.wait_ge(scores_kept, k + 1)
                    v.tensor_reduce(mx[:, b, :, t], s, AX, ALU.max).then_inc(tile_max, 1)
                when(dve, tail[b][t], body, [(scores_kept, 1), (tile_max, 1)])

            def shift(b, t):
                def body():
                    s = S[:, b % 2, t]
                    v.tensor_tensor(s, s, spread(mxb[:, b], P), ALU.subtract).then_inc(shifted, 1)
                when(dve, tail[b][t], body, [(shifted, 1)])

            def maximum(b):
                dve.wait_ge(tile_max, TAIL * (b + 1))
                dve.wait_ge(h_vec, CREDIT + HEAD * (maxima_no(b) + 1))
                v.tensor_reduce(mxb[:, b], mx[:, b], AX, ALU.max).then_inc(batch_max, 1)

            own_done()
            stream(0, maxima_no(0), False)
            for t in range(TAIL):
                keep_scores(0, t)
            for b in range(B):
                if b + 1 < B:
                    stream(b + 1, maxima_no(b + 1), False)
                maximum(b)
                dve.wait_ge(batch_max, b + 1)
                stream(b, sums_no(b), True)
                for t in range(TAIL):
                    shift(b, t)
                    if b + 1 < B:
                        keep_scores(b + 1, t)
                dve.wait_ge(ov_zeroed, b + 1)
                dve.wait_ge(mixed, TAIL * (b + 1))
                dve.wait_ge(h_mixed, CREDIT + HEAD * (b + 1))
                if b == 0:
                    dve.wait_ge(bias_made, B)
                v.tensor_copy(oT[:, b], OV[:, 0:256]).then_inc(oT_kept, 1)

            dve.wait_ge(o_tok, 1)
            otok = A[0][:, :].rearrange("p (b h w) -> p b h w", b=B, h=H)
            own(v.tensor_scalar(den[:], otok[:, :, :, HD], 0.5, None, ALU.max))
            own_done()
            own(v.reciprocal(rden[:], den[:]))
            own_done()
            own(v.tensor_tensor(rdw[:], rden[:], notwipe[:].unsqueeze(2).broadcast_to([P, B, H]), ALU.mult))
            own_done()
            own(v.tensor_tensor(on.rearrange("p (n w) -> p n w", w=HD),
                                A[0][:, :].rearrange("p (n w) -> p n w", w=VW)[:, :, 0:HD],
                                rdw[:].rearrange("p b h -> p (b h)").unsqueeze(2).broadcast_to([P, B * H, HD]), ALU.mult))
            dve.wait_ge(wo_in, 32)
            own_done()
            for b in range(B):
                v.scalar_tensor_tensor(on[:, b * P:(b + 1) * P], rows[:, 0], notwipe[:, b:b + 1], on[:, b * P:(b + 1) * P],
                                       ALU.mult, ALU.add).then_inc(on_made, 1)
            dve.wait_ge(proj_made, 1)
            dve.wait_ge(xb_made, B)
            own(v.tensor_tensor(x1[:].rearrange("p b d -> p (b d)"), C[1][:, :], xb[:].rearrange("p b d -> p (b d)"), ALU.add))
            own_done()
            layer_norm(x1, xn1, dv)
            count[0] += B
            own_done()
            for s in range(B):
                n = B - s
                own(v.tensor_tensor(prod[:, 0:n], xn1[:, s:B], xn1[:, s:s + 1].broadcast_to([P, n, P]), ALU.mult))
                own_done()
                own(v.tensor_reduce(sc[:, s, s:B], prod[:, 0:n], AX, ALU.add))
                own_done()
            for s in range(B - 1):
                own(v.tensor_copy(sc[:, s + 1:B, s], sc[:, s, s + 1:B]))
            own_done()
            own(v.tensor_reduce(scm[:], sc[:], AX, ALU.max))
            own_done()
            v.tensor_tensor(scd[:], sc[:], scm[:].unsqueeze(2).broadcast_to([P, B, B]), ALU.subtract).then_inc(sc_ready, 1)
            dve.wait_ge(sc_exp, 1)
            own(v.tensor_reduce(scs[:], sce[:], AX, ALU.add))
            own_done()
            own(v.reciprocal(scr[:], scs[:]))
            own_done()
            own(v.tensor_tensor(scp[:], sce[:], scr[:].unsqueeze(2).broadcast_to([P, B, B]), ALU.mult))
            own_done()
            for t in range(B):
                for s in range(B):
                    if t:
                        dve.wait_ge(dv, count[0] - (B - 1))
                    own(v.scalar_tensor_tensor(x2[:, s], xn1[:, t], scp[:, s, t:t + 1], (x2 if t else x1)[:, s], ALU.mult, ALU.add))
            own_done()
            layer_norm(x2, xf, xf_made)
            dve.wait_ge(xf_made, B)
            layer_norm(xf, xln, xln_made)
            dve.wait_ge(logits_made, 1)
            lg = D[1][:, 0:B * EX].rearrange("p (i e) -> p i e", i=B)
            own(v.tensor_reduce(lgm[:], lg, AX, ALU.max))
            own_done()
            v.tensor_tensor(lgd[:], lg, lgm[:].unsqueeze(2).broadcast_to([P, B, EX]), ALU.subtract).then_inc(lg_ready, 1)
            dve.wait_ge(lg_exp, 1)
            mine = lge[:].unsqueeze(3).broadcast_to([P, B, EX, EX])
            other = lge[:].unsqueeze(2).broadcast_to([P, B, EX, EX])
            own(v.tensor_tensor(cmp_gt[:], other, mine, ALU.is_gt))
            own(v.tensor_tensor(cmp_eq[:], other, mine, ALU.is_equal))
            own_done()
            own(v.tensor_tensor(cmp_eq[:], cmp_eq[:], lower.unsqueeze(1).broadcast_to([P, B, EX, EX]), ALU.mult))
            own_done()
            own(v.tensor_tensor(cmp_gt[:], cmp_gt[:], cmp_eq[:], ALU.add))
            own_done()
            own(v.tensor_reduce(rank[:], cmp_gt[:], AX, ALU.add))
            own_done()
            v.tensor_scalar(sel[:], rank[:], 1.5, None, ALU.is_lt).then_inc(sel_made, 1)
            for k in range(2):
                own(v.tensor_scalar(first[:, k], rank[:], float(k), None, ALU.is_equal))
            own(v.memset(cum[:, 0], 0.0))
            dve.wait_ge(sel_made, 1)
            for i in range(B):
                own_done()
                ins = v.tensor_tensor(cum[:, i + 1], cum[:, i], sel[:, i], ALU.add)
                if i < B - 1:
                    own(ins)
                else:
                    ins.then_inc(sel_made, 1)
            dve.wait_ge(pos_made, 1)
            own(v.tensor_reduce(cmax[:], D[1][0:1, 64:64 + EX], AX, ALU.max))
            pos = D[1][:, 0:B * EX].rearrange("p (i e) -> p i e", i=B)
            own(v.scalar_tensor_tensor(posm[:], pos, 1.0, sel[:], ALU.add, ALU.mult))
            own(v.tensor_tensor(rowid[:], pos, eoff.unsqueeze(1).broadcast_to([P, B, EX]), ALU.add))
            own_done()
            v.tensor_scalar(over_i[:], cmax[:], float(SLOTS), None, ALU.is_gt).then_inc(over_made, 1)
            v.memset(SQ1[:, :, :, :, SLOTS:], 1.0).then_inc(sq_ones, 1)
            dve.wait_ge(sq_ones, 1)

            def route_weights():
                own(v.tensor_tensor(wtmp[:, 0], lge[:], first[:, 0], ALU.mult))
                own(v.tensor_tensor(wtmp[:, 1], lge[:], first[:, 1], ALU.mult))
                own(v.tensor_tensor(dtmp[:, 0], rowid[:], first[:, 0], ALU.mult))
                own(v.tensor_tensor(dtmp[:, 1], rowid[:], first[:, 1], ALU.mult))
                own_done()
                own(v.tensor_reduce(wsum[:], wtmp[:], AX, ALU.add))
                own(v.tensor_reduce(destf[:], dtmp[:], AX, ALU.add))
                own_done()
                v.tensor_copy(dest[:], destf[:]).then_inc(dest_made, 1)
                own(v.tensor_tensor(wden[:], wsum[:, 0], wsum[:, 1], ALU.add))
                own_done()
                own(v.reciprocal(wden[:], wden[:]))
                own_done()
                own(v.tensor_tensor(wgt[:], wsum[:], wden[:].unsqueeze(1).broadcast_to([P, 2, B]), ALU.mult))

            def ffn(r, again, off):
                mine = [0]

                def step(ins):
                    mine[0] += 1
                    ins.then_inc(fv, 1)

                def step_done(back=0):
                    dve.wait_ge(fv, off + (mine[0] - back))

                if again:
                    dve.wait_ge(y_stored, r * STORED)
                    step(v.tensor_scalar(posm[:], posm[:], -float(SLOTS), None, ALU.add))
                    step_done()

                def choose(n):
                    e = E2 + n if n < E2 else n - E2
                    if n >= 2:
                        dve.wait_ge(gathered, r * EX + n - 1)
                    for i in range(B):
                        ins = v.tensor_scalar(onehot[:, n % 2, i], iota1, posm[:, i, e:e + 1], None, ALU.is_equal)
                    ins.then_inc(onehot_made, 1)

                def keep_tokens(n):
                    dve.wait_ge(gathered, r * EX + n + 1)
                    if n < E2:
                        ins = v.tensor_scalar(xe[:, n], X[n % 2][:, 0:SLOTS], hvec[:, n:n + 1], hvec[:, 4 + n:5 + n],
                                              ALU.mult, ALU.add)
                    else:
                        ins = v.tensor_copy(xe[:, n], X[n % 2][:, 0:SLOTS])
                    ins.then_inc(xe_kept, 1)

                def squares0(n):
                    for g in range(0, G, 4):
                        dve.wait_ge(t0_made, r * 8 + 2 * n + g // 4 + 1)
                        if n >= 2 and g == 0:
                            dve.wait_ge(z_made, r * E2 + n - 1)
                        t = T0[:, n % 2, g:g + 4]
                        v.tensor_tensor(SQ0[:, n % 2, g:g + 4, 0:SLOTS], t, t, ALU.mult).then_inc(sq0_made, 1)

                def keep_z(n):
                    dve.wait_ge(z_made, r * E2 + n + 1)
                    z = Z[n % 2][:, 0:2 * (SLOTS + 1)].rearrange("p (c s) -> p c s", c=2)
                    step(v.tensor_tensor(cz[:, n], z[:, :, SLOTS], vec[:, SB0 + 2 * n:SB0 + 2 * n + 2], ALU.add))
                    step_done()
                    step(v.tensor_scalar(zs[:, n, 0], z[:, 0, 0:SLOTS], -1.0, cz[:, n, 0:1], ALU.mult, ALU.add))
                    v.tensor_scalar(zs[:, n, 1], z[:, 1, 0:SLOTS], -1.0, cz[:, n, 1:2], ALU.mult, ALU.add).then_inc(z_kept, 1)

                def centre(n):
                    dve.wait_ge(mean_made, r * E2 + n + 1)
                    v.tensor_tensor(zd[:, n], zs[:, n], MEAN[:, 0:SLOTS].unsqueeze(1).broadcast_to([P, 2, SLOTS]), ALU.subtract
                                    ).then_inc(zd_made, 1)
                    dve.wait_ge(zd_made, r * E2 + n + 1)
                    v.tensor_tensor(zq[:, n], zd[:, n], zd[:, n], ALU.mult).then_inc(zq_made, 1)

                def keep_var(n):
                    dve.wait_ge(vars_made, r * E2 + n + 1)
                    v.tensor_scalar(var[:, n], VAR[:, 0:SLOTS], EPS, None, ALU.add).then_inc(vars_kept, 1)

                def normalise(n):
                    if n == 0:
                        dve.wait_ge(std_made, r + 1)
                        step(v.reciprocal(rsd, var))
                        step_done()
                    step(v.tensor_tensor(zq[:, n], zd[:, n], rsd[:, n].unsqueeze(1).broadcast_to([P, 2, SLOTS]), ALU.mult))
                    step_done()
                    for c in range(2):
                        k = 2 * n + c
                        ins = v.tensor_scalar(zs[:, n, c], zq[:, n, c], hvec[:, 8 + k:9 + k], hvec[:, 16 + k:17 + k], ALU.mult, ALU.add)
                        if c == 0:
                            step(ins)
                        else:
                            step_done()
                            ins.then_inc(u1_made, 1)

                def squares1(n):
                    for g in range(0, G, 2):
                        dve.wait_ge(t1_made, r * 16 + 4 * n + g // 2 + 1)
                        if g == 0 and n >= 2:
                            dve.wait_ge(y_made, r * EX + E2 + n - 1)
                        if g == 0 and n == 0:
                            dve.wait_ge(z_made, r * E2 + E2)
                        for c in range(2):
                            t = T1[:, n % 2, g:g + 2, c]
                            ins = v.tensor_tensor(SQ1[:, n % 2, g:g + 2, c, 0:SLOTS], t, t, ALU.mult)
                        ins.then_inc(sq1_made, 1)

                def keep_y(n):
                    dve.wait_ge(y_made, r * EX + n + 1)
                    if n >= 2:
                        dve.wait_ge(yn_made, r * EX + n - 1)
                    if n < E2:
                        v.tensor_scalar(yT[:, n % 2], Y[:, 0:SLOTS], vec[:, MB2 + n:MB2 + n + 1], None, ALU.add).then_inc(yT_kept, 1)
                    else:
                        k = n - E2
                        step(v.tensor_tensor(cy[:, k:k + 1], Y[:, SLOTS:SLOTS + 1], vec[:, SB1 + k:SB1 + k + 1], ALU.add))
                        step_done()
                        v.tensor_scalar(yT[:, n % 2], Y[:, 0:SLOTS], -1.0, cy[:, k:k + 1], ALU.mult, ALU.add).then_inc(yT_kept, 1)

                choose(0)
                choose(1)
                keep_tokens(0)
                keep_tokens(1)
                if not again:
                    route_weights()
                for n in range(E2):
                    choose(n + 2)
                    squares0(n)
                    if n:
                        keep_z(n - 1)
                    keep_tokens(n + 2)
                    if n:
                        centre(n - 1)
                    if n >= 2:
                        keep_var(n - 2)
                keep_z(3)
                choose(6)
                keep_tokens(6)
                centre(3)
                keep_var(2)
                choose(7)
                keep_tokens(7)
                keep_var(3)
                keep_y(0)
                keep_y(1)
                normalise(0)
                normalise(1)
                keep_y(2)
                keep_y(3)
                normalise(2)
                normalise(3)
                for n in range(E2):
                    squares1(n)
                    keep_y(E2 + n)
                return mine[0]

            own_done()
            steps = ffn(0, False, 0)
            over = dve.value_load(over_i[0:1, 0:1])
            with dve.If(over > 0):
                with dve.Fori(1, ROUNDS) as r:
                    assert ffn(r, True, r * (steps + 1) - 1) == steps + 1
            own_done()
            for i in range(B):
                dve.wait_ge(y_back, 2 * B * 16)
                own(v.scalar_tensor_tensor(fin[:, i], yg[:, 0, i], wgt[:, 0, i:i + 1], x2[:, i], ALU.mult, ALU.add))
            own_done()
            for i in range(B):
                v.scalar_tensor_tensor(fin[:, i], yg[:, 1, i], wgt[:, 1, i:i + 1], fin[:, i], ALU.mult, ALU.add).then_inc(fin_made, 1)


def constants():
    c = np.zeros((P, NC), np.float32)
    p = np.arange(P)
    c[:, C_ID:C_ID + P] = np.eye(P)
    c[:, C_U:C_U + P] = p[:, None] < p[None, :]
    c[:, C_HM:C_HM + H] = p[:, None] // HD == np.arange(H)[None, :]
    c[:, C_IOTA:C_IOTA + SLOTS] = 1 + np.arange(SLOTS)
    c[:, C_EOFF:C_EOFF + EX] = ROWS * np.arange(EX)
    e = np.arange(EX)
    c[:, C_LT:C_LT + EX * EX] = (e[None, :] < e[:, None]).reshape(-1)
    return c


def arrays_of(i):
    def a(name):
        return np.asarray(i[name])

    rows = [a("L0_xattn_bq").reshape(1, P), a("L0_xattn_bk").reshape(1, P), a("L0_ffn_kan_ln_g0"), a("L0_ffn_kan_ln_b0"),
            a("L0_ffn_kan_sl_b0").reshape(-1, P), a("L0_ffn_kan_ln_g1").reshape(-1, P), a("L0_ffn_kan_ln_b1").reshape(-1, P),
            a("L0_ffn_kan_sl_b1"), a("L0_ffn_mlp_b2"), a("L0_ffn_mlp_b1").reshape(-1, P)]
    return {
        "x": a("x").transpose(1, 0, 2),
        "ctxT": a("ctx_1024").transpose(0, 2, 1),
        "mask": a("mask_BxSxS2_bk0").transpose(1, 0, 2),
        "Wq": a("L0_xattn_Wq"), "Wk": a("L0_xattn_Wk"), "Wv": a("L0_xattn_Wv"), "Wo": a("L0_xattn_Wo"),
        "rows2": np.stack([a("L0_xattn_bv"), a("L0_xattn_bo")]),
        "gateW": a("L0_ffn_gate_W"),
        "KW0": a("L0_ffn_kan_sl_W0").reshape(E2, P, G, F2).transpose(1, 0, 2, 3),
        "KW1": a("L0_ffn_kan_sl_W1").reshape(E2, 2, P, G, P).transpose(2, 0, 1, 3, 4),
        "MW1": a("L0_ffn_mlp_W1").transpose(1, 0, 2),
        "MW2": a("L0_ffn_mlp_W2").reshape(E2, 4, P, P).transpose(2, 0, 1, 3),
        "vecs": np.concatenate(rows, 0).T,
        "consts": constants(),
    }


def build(nc, arrays):
    args = []
    for name, value in arrays.items():
        args.append(nc.dram_tensor(name, value.shape, mybir.dt.from_np(value.dtype), kind="ExternalInput").ap())
    out = nc.dram_tensor("out", (B, P, P), F32, kind="ExternalOutput").ap()
    args[2] = args[2].bitcast(U8) if args[2].dtype != U8 else args[2]
    layer(nc, *args, out.rearrange("b q d -> q b d"))


def kernel(**inputs):
    import concourse.bacc as bacc
    from concourse.bass_utils import run_bass_kernel_spmd

    arrays = {k: np.ascontiguousarray(v) for k, v in arrays_of(inputs).items()}
    nc = bacc.Bacc("TRN2", target_bir_lowering=False, num_devices=1)
    build(nc, arrays)
    r = run_bass_kernel_spmd(nc, [arrays], core_ids=[0])
    return r.results[0]["out"]
```

```python
from contextlib import ExitStack

import concourse.bass as bass
from concourse import mybir
import numpy as np

F32 = mybir.dt.float32
I32 = mybir.dt.int32
U32 = mybir.dt.uint32
U8 = mybir.dt.uint8
ALU = mybir.AluOpType
ACT = mybir.ActivationFunctionType
AX = mybir.AxisListType.X

P = 128
B = 4
H = 8
HD = 16
VW = 32
KEYS = 2048
TILES = KEYS // P
TAIL = 4
HEAD = TILES - TAIL
CREDIT = 1
EPS = 1e-5
NEG = 1e30

NORMS = 4
GROUPS = ((0, 0, 4), (1, 0, 4), (2, 0, 2), (2, 2, 4), (3, 0, 2), (3, 2, 4))

EX = 8
E2 = 4
G = 8
GRID = np.linspace(-1.2, 0.2, G).astype(np.float32)
F = 512
F2 = 256
SLOTS = 160
ROUNDS = 4
ROWS = SLOTS * ROUNDS
REST = SLOTS - P
ZP = 120

BQ, BK, G0, B0, SB0, G1, B1, SB1, MB2, MB1, NV = 0, 1, 2, 6, 10, 18, 26, 34, 38, 42, 58
C_ID, C_U, C_HM, C_IOTA, C_EOFF, C_LT, C_POW, NC = 0, 128, 256, 264, 264 + SLOTS, 272 + SLOTS, 336 + SLOTS, 353 + SLOTS


def layer(nc, x, ctxT, mask, Wq, Wk, Wv, Wo, rows2, gateW, KW0, KW1, MW1, MW2, vecs, consts, out):
    y_table = nc.dram_tensor("y_table", [EX * ROWS, P], F32, kind="Internal").ap()
    with ExitStack() as ctx:
        def sb(name, shape, dt=F32):
            return ctx.enter_context(nc.sbuf_tensor(name, shape, dt))

        def sem(name):
            return ctx.enter_context(nc.semaphore(name))

        cst = sb("cst", [P, NC])
        vec = sb("vec", [P, NV])
        hvec = sb("hvec", [P, 32])
        wq = sb("wq", [P, P])
        wk = sb("wk", [P, P])
        wv = sb("wv", [P, P])
        wo = sb("wo", [P, P])
        rows = sb("rows", [P, 2, P])
        gate = sb("gate", [P, EX])
        kw0 = sb("kw0", [P, E2, G, F2])
        mw1 = sb("mw1", [P, E2, F])
        mw2 = sb("mw2", [P, E2, 4, P])
        ones = sb("ones", [P, P])
        mean_w = sb("mean_w", [P, P])
        zeros = sb("zeros", [P, 256])
        xs = sb("xs", [P, B, P])
        xb = sb("xb", [P, B, P])
        xn = sb("xn", [P, B, P])
        x1 = sb("x1", [P, B, P])
        xn1 = sb("xn1", [P, B, P])
        x2 = sb("x2", [P, B, P])
        xf = sb("xf", [P, B, P])
        xln = sb("xln", [P, B, P])
        stats = sb("stats", [P, NORMS, B, 6])
        mv = sb("mv", [P, NORMS, B, 2])
        vare = sb("vare", [P, NORMS, B])
        rstd = sb("rstd", [P, NORMS, B])
        mhalf = sb("mhalf", [P, B])
        flags = sb("flags", [P, B, TILES])
        anyf = sb("anyf", [1, B * TAIL + 1])
        word_f = sb("word_f", [1, 1])
        word_i = sb("word_i", [1, 1], I32)
        notwipe = sb("notwipe", [P, B])
        mx = sb("mx", [P, B, H, TAIL + 1])
        mxb = sb("mxb", [P, B, H])
        mxt = sb("mxt", [P, H])
        den = sb("den", [P, B, H])
        rden = sb("rden", [P, B, H])
        rdw = sb("rdw", [P, B, H])
        sc = sb("sc", [P, B, B])
        scm = sb("scm", [P, B])
        scd = sb("scd", [P, B, B])
        sce = sb("sce", [P, B, B])
        scs = sb("scs", [P, B])
        scr = sb("scr", [P, B])
        scp = sb("scp", [P, B, B])
        lgm = sb("lgm", [P, B])
        lgd = sb("lgd", [P, B, EX])
        lge = sb("lge", [P, B, EX])
        cmp_gt = sb("cmp_gt", [P, B, EX, EX])
        cmp_eq = sb("cmp_eq", [P, B, EX, EX])
        rank = sb("rank", [P, B, EX])
        first = sb("first", [P, 2, B, EX])
        sel = sb("sel", [P, B, EX])
        cum = sb("cum", [P, B + 1, EX])
        wsum = sb("wsum", [P, 2, B])
        wtmp = sb("wtmp", [P, 2, B, EX])
        wden = sb("wden", [P, B])
        wgt = sb("wgt", [P, 2, B])
        posm = sb("posm", [P, B, EX])
        rowid = sb("rowid", [P, B, EX])
        dtmp = sb("dtmp", [P, 2, B, EX])
        destf = sb("destf", [P, 2, B])
        dest = sb("dest", [P, 2, B], U32)
        cmax = sb("cmax", [1, 1])
        over_i = sb("over_i", [1, 1], I32)

        ARENA = 31440
        arena = sb("arena", [P, ARENA])
        at = [0]

        def part(size, pattern=None, **kw):
            a = arena[:, at[0]:at[0] + size]
            at[0] += size
            return a.rearrange(pattern, **kw) if pattern else a

        S = part(2 * TAIL * H * P, "p (u t h k) -> p u t h k", u=2, t=TAIL, h=H)
        PT = part(2 * H * P, "p (u n) -> p u n", u=2)
        V = part(B * TAIL * H * VW, "p (b t h w) -> p b t h w", b=B, t=TAIL, h=H)
        QM = part(H * B * P, "p (b h q) -> p b h q", h=H, b=B)
        kT = part(B * TAIL * P, "p (b n) -> p b n", b=B)
        ctx_t = part(B * TAIL * P, "p (b n) -> p b n", b=B)
        mask_f = part(B * KEYS // 4)
        mbias = part(B * TAIL * P, "p (b t k) -> p b t k", b=B, t=TAIL)
        h_ctx = part(P)
        h_mask = part(P // 4)
        h_bias = part(P)
        h_kT = part(P)
        h_V = part(H * VW, "p (h w) -> p h w", h=H)
        h_S = part(H * P, "p (h k) -> p h k", h=H)
        h_PT = part(H * P)
        xnT = PT[:, 0, 0:B * P]
        qs = PT[:, 1, 0:B * P]
        mask_u8 = mask_f.bitcast(U8).rearrange("p (b k) -> p b k", b=B)
        mask_i32 = mask_f.bitcast(I32).rearrange("p (t w) -> p t w", w=P // 4)
        h_mask_u8 = h_mask.bitcast(U8)
        oT = mask_f[:, 0:B * 256].rearrange("p (b n) -> p b n", b=B)
        on = S[:, 0, 0:2].rearrange("p t h k -> p (t h k)")[:, 0:B * P]
        onT = S[:, 0, 2:4].rearrange("p t h k -> p (t h k)")[:, 0:B * P]
        prod = S[:, 1, 0]
        squares = S[:, 1, 1, 0:B]

        at[0] = 0
        T1 = part(2 * G * 2 * SLOTS, "p (u g c s) -> p u g c s", u=2, g=G, c=2)
        SQ1 = part(2 * G * 2 * (SLOTS + 1), "p (u g c s) -> p u g c s", u=2, g=G, c=2)
        hT = T1[:, 1].rearrange("p g c s -> p (g c s)").rearrange("p (m c s) -> p m c s", m=E2, c=4)
        T0 = T1[:, :, :, 0]
        SQ0 = SQ1[:, :, :, 0]
        onehot = part(4 * B * SLOTS, "p (u i s) -> p u i s", u=4, i=B)
        xe = part(EX * SLOTS, "p (n s) -> p n s", n=EX)
        zs = part(E2 * 2 * SLOTS, "p (n c s) -> p n c s", n=E2, c=2)
        zd = part(E2 * 2 * SLOTS, "p (n c s) -> p n c s", n=E2, c=2)
        zq = part(E2 * 2 * SLOTS, "p (n c s) -> p n c s", n=E2, c=2)
        var = part(E2 * SLOTS, "p (n s) -> p n s", n=E2)
        rsd = part(E2 * SLOTS, "p (n s) -> p n s", n=E2)
        yT = part(2 * SLOTS, "p (u s) -> p u s", u=2)
        yn = part(EX * 2 * P, "p (n j d) -> p n j d", n=EX, j=2)
        cz = part(E2 * 2, "p (n c) -> p n c", n=E2)
        cy = part(E2)
        xfT = part(B * P)
        kw1 = part(E2 * 2 * G * P, "p (e c g o) -> p e c g o", e=E2, c=2, g=G)
        onehot_flat = onehot.rearrange("p u i s -> p (u i s)")
        yg = onehot_flat[:, 0:2 * B * P].rearrange("p (k i d) -> p k i d", k=2, i=B)
        fin = onehot_flat[:, 2 * B * P:3 * B * P].rearrange("p (i d) -> p i d", i=B)

        ident = cst[:, C_ID:C_ID + P]
        upper = cst[:, C_U:C_U + P]
        hmask = cst[:, C_HM:C_HM + H]
        iota1 = cst[:, C_IOTA:C_IOTA + SLOTS]
        eoff = cst[:, C_EOFF:C_EOFF + EX]
        powers = cst[0:1, C_POW:C_POW + B * TAIL + 1]
        lower = cst[:, C_LT:C_LT + EX * EX].rearrange("p (a b) -> p a b", a=EX)

        A = [ctx.enter_context(nc.psum_tensor(f"A{i}", [P, 1024], F32)) for i in range(2)]
        C = [ctx.enter_context(nc.psum_tensor(f"C{i}", [P, 512], F32)) for i in range(2)]
        D = [ctx.enter_context(nc.psum_tensor(f"D{i}", [P, 512], F32)) for i in range(2)]
        OV = D
        KV = [C, D]
        X = [C[0], C[1]]
        Z = [A[0][:, 0:512], A[0][:, 512:1024]]
        MEAN = A[1][:, 0:512]
        VAR = A[1][:, 512:1024]
        Y = [d[:, 0:SLOTS + 1] for d in D]
        YN = X

        x_in = sem("x_in")
        cst_in = sem("cst_in")
        wq_in = sem("wq_in")
        wkv_in = sem("wkv_in")
        mask_in = sem("mask_in")
        ctx_in = [sem(f"ctx_in{b}") for b in range(B)]
        wo_in = sem("wo_in")
        ffn_in = sem("ffn_in")
        kw1_in = sem("kw1_in")
        ones_made = sem("ones_made")
        pads_made = sem("pads_made")
        vhalf_made = sem("vhalf_made")
        dv = sem("dv")
        var_ready = sem("var_ready")
        eps_added = sem("eps_added")
        rstd_made = sem("rstd_made")
        xn_made = sem("xn_made")
        xnT_made = sem("xnT_made")
        xnT_kept = sem("xnT_kept")
        qT_made = sem("qT_made")
        q_scaled = sem("q_scaled")
        qm_made = sem("qm_made")
        qm_rest = sem("qm_rest")
        kv_made = sem("kv_made")
        kv_kept = sem("kv_kept")
        flags_made = sem("flags_made")
        anyq_made = sem("anyq_made")
        word_made = sem("word_made")
        bias_made = sem("bias_made")
        xb_made = sem("xb_made")
        scores_made = sem("scores_made")
        scores_kept = sem("scores_kept")
        tile_max = sem("tile_max")
        batch_max = sem("batch_max")
        shifted = sem("shifted")
        shifted_last = sem("shifted_last")
        probs_made = sem("probs_made")
        probsT_made = sem("probsT_made")
        probsT_kept = sem("probsT_kept")
        probsT_last = sem("probsT_last")
        ov_zeroed = sem("ov_zeroed")
        mixed = sem("mixed")
        oT_cleared = sem("oT_cleared")
        oT_kept = sem("oT_kept")
        h_in = sem("h_in")
        h_biased = sem("h_biased")
        h_kv = sem("h_kv")
        h_kvkept = sem("h_kvkept")
        h_scores = sem("h_scores")
        h_kept = sem("h_kept")
        h_max = sem("h_max")
        h_vec = sem("h_vec")
        h_probs = sem("h_probs")
        h_T = sem("h_T")
        h_Tkept = sem("h_Tkept")
        h_mixed = sem("h_mixed")
        h_added = sem("h_added")
        on_made = sem("on_made")
        o_tok = sem("o_tok")
        onT_made = sem("onT_made")
        onT_kept = sem("onT_kept")
        proj_made = sem("proj_made")
        xn1_made = sem("xn1_made")
        sc_own = sem("sc_own")
        x1_made = sem("x1_made")
        sc_ready = sem("sc_ready")
        sc_exp = sem("sc_exp")
        xf_made = sem("xf_made")
        xln_made = sem("xln_made")
        xfT_made = sem("xfT_made")
        xfT_kept = sem("xfT_kept")
        logits_made = sem("logits_made")
        lg_ready = sem("lg_ready")
        lg_exp = sem("lg_exp")
        sel_made = sem("sel_made")
        pos_made = sem("pos_made")
        over_made = sem("over_made")
        dest_made = sem("dest_made")
        sq_ones = sem("sq_ones")
        onehot_made = sem("onehot_made")
        gathered = sem("gathered")
        xe_kept = sem("xe_kept")
        t0_made = sem("t0_made")
        sq0_made = sem("sq0_made")
        z_made = sem("z_made")
        z_kept = sem("z_kept")
        mean_made = sem("mean_made")
        zd_made = sem("zd_made")
        zq_made = sem("zq_made")
        vars_made = sem("vars_made")
        vars_kept = sem("vars_kept")
        std_made = sem("std_made")
        hid_made = sem("hid_made")
        hid_kept = sem("hid_kept")
        u1_made = sem("u1_made")
        t1_made = sem("t1_made")
        sq1_made = sem("sq1_made")
        l1_done = sem("l1_done")
        y_made = sem("y_made")
        yT_kept = sem("yT_kept")
        yn_made = sem("yn_made")
        yn_kept_mlp = sem("yn_kept_mlp")
        yn_kept_kan = sem("yn_kept_kan")
        y_stored = sem("y_stored")
        fv = sem("fv")
        rows_cleared = sem("rows_cleared")
        y_back = [sem(f"y_back{i}") for i in range(B)]
        fin_made = sem("fin_made")
        out_done = sem("out_done")
        STORED = EX * 32

        def tanh_bias(g):
            return float(-0.5 * GRID[g])

        block = ctx.enter_context(nc.Block())

        def tile_no(b, t):
            return b * TAIL + t

        LAST = (B - 1) * TAIL

        def out_of_psum(k, g):
            if k < LAST:
                return probsT_kept, 2 * k + g + 1
            return (probsT_last if g else probsT_kept), (0 if g else 2 * LAST) + k - LAST + 1

        def kv_before(seq):
            return CREDIT + HEAD * (seq if seq < B else 2 * seq - B)

        def load_flags(eng):
            eng.wait_ge(word_made, 1)
            word = eng.value_load(word_i[0:1, 0:1])
            return [(word >> k) & 1 for k in range(B * TAIL)], word >> (B * TAIL)

        def rows_kept(r, n):
            return (yn_kept_mlp if n < E2 else yn_kept_kan), r * E2 + n % E2 + 1

        def when(eng, flag, body, passed_over):
            with eng.If(flag > 0):
                body()
            with eng.Else():
                eng.drain()
                for s, n in passed_over:
                    eng.sem_inc(s, n)

        @block.sync
        def _(sp):
            sp.dma_start(xs[:], x).then_inc(x_in, 16)
            sp.dma_start(mask_u8, mask).then_inc(mask_in, 16)
            for b in range(B):
                sp.dma_start(ctx_t[:, b], ctxT[b, :, HEAD * P:]).then_inc(ctx_in[b], 16)
            sp.dma_start(mw1[:], MW1).then_inc(ffn_in, 16)
            sp.dma_start(mw2[:], MW2).then_inc(ffn_in, 16)
            sp.dma_start(gate[:], gateW).then_inc(ffn_in, 16)
            sp.wait_ge(ones_made, 4)
            for e in range(EX):
                sp.dma_start(y_table[e * ROWS + SLOTS:(e + 1) * ROWS, :].rearrange("(p r) w -> p r w", p=ZP),
                             zeros[0:ZP, 0:P].unsqueeze(1).broadcast_to([ZP, (ROWS - SLOTS) // ZP, P])).then_inc(rows_cleared, 16)
            tail, head = load_flags(sp)

            def stream(first):
                for seq in range(first, first + B):
                    with sp.Fori(0, HEAD) as i:
                        sp.wait_ge(h_kv, CREDIT + i + HEAD * seq)
                        sp.wait_ge(h_biased, CREDIT + i + HEAD * seq)
                        sp.dma_start(h_ctx, ctxT[seq % B, :, bass.ds(i * P, P)]).then_inc(h_in, 16)
                        sp.dma_start(h_mask_u8, mask[:, seq % B, bass.ds(i * P, P)]).then_inc(h_in, 16)
                sp.wait_ge(h_in, 32 * HEAD * (first + B))

            for first in (0, B):
                when(sp, head, lambda: stream(first), [(h_in, 32 * HEAD * B)])
            sp.wait_ge(o_tok, B)
            sp.dma_start(kw1, KW1).then_inc(kw1_in, 16)

            def store_round(off, row):
                for n in range(EX):
                    e = n
                    sp.wait_ge(*rows_kept(off, n))
                    sp.dma_start(y_table[bass.ds(row + e * ROWS, P), :], yn[:, n, 0]).then_inc(y_stored, 16)
                    sp.dma_start(y_table[bass.ds(row + e * ROWS + P, REST), :], yn[0:REST, n, 1]).then_inc(y_stored, 16)

            store_round(0, 0)
            sp.wait_ge(rows_cleared, 16 * EX)
            sp.wait_ge(over_made, 1)
            over = sp.value_load(over_i[0:1, 0:1])
            with sp.If(over > 0):
                with sp.Fori(1, ROUNDS) as r:
                    store_round(r, r * SLOTS)
            for i in range(B):
                sp.wait_ge(fin_made, i + 1)
                sp.dma_start(out[:, i], fin[:, i]).then_inc(out_done, 16)
            sp.wait_ge(out_done, 16 * B)

        @block.gpsimd
        def _(pool):
            nc.gpsimd.memset(ones[:], 1.0).then_inc(ones_made, 1)
            nc.gpsimd.memset(mhalf[:], -0.5).then_inc(ones_made, 1)
            nc.gpsimd.memset(mean_w[:], 1.0 / F2).then_inc(ones_made, 1)
            nc.gpsimd.memset(zeros[:], 0.0).then_inc(ones_made, 1)
            def rstd_step(j):
                n, lo, hi = GROUPS[j]
                pool.wait_ge(var_ready, j + 1)
                nc.gpsimd.tensor_scalar(vare[:, n, lo:hi], mv[:, n, lo:hi, 1], EPS, None, ALU.add).then_inc(eps_added, 1)
                pool.wait_ge(eps_added, j + 1)
                nc.gpsimd.tensor_tensor(rstd[:, n, lo:hi], vare[:, n, lo:hi], mhalf[:, lo:hi], ALU.pow).then_inc(rstd_made, 1)

            pool.wait_ge(ones_made, 2)
            rstd_step(0)
            for v in (V.rearrange("p b t h w -> p (b t h) w"), h_V):
                nc.gpsimd.memset(v[:, :, HD + 1:], 0.0).then_inc(pads_made, 1)
                nc.gpsimd.memset(v[:, :, HD:HD + 1], 1.0).then_inc(pads_made, 1)
            pool.wait_ge(mask_in, 16)
            for b in range(B):
                nc.gpsimd.tensor_scalar(mbias[:, b], mask_u8[:, b, HEAD * P:].rearrange("p (t k) -> p t k", t=TAIL),
                                        NEG, -NEG, ALU.mult, ALU.add).then_inc(bias_made, 1)
            pool.wait_ge(q_scaled, 1)
            pool.wait_ge(cst_in, 32)
            pool.wait_ge(flags_made, 1)
            pool.wait_ge(bias_made, B)
            nc.gpsimd.memset(oT[:, 2:], 0.0).then_inc(oT_cleared, 1)
            for b in range(1, B):
                nc.gpsimd.tensor_tensor(QM[:, b], qs[:, b * P:(b + 1) * P].unsqueeze(1).broadcast_to([P, H, P]),
                                        hmask.unsqueeze(2).broadcast_to([P, H, P]), ALU.mult).then_inc(qm_rest, 1)
            tail, _ = load_flags(pool)

            def shift(b, t):
                def body():
                    for g in range(2):
                        s = S[:, b % 2, t, 4 * g:4 * g + 4]
                        nc.gpsimd.tensor_tensor(s, s, mxb[:, b, 4 * g:4 * g + 4].unsqueeze(2).broadcast_to([P, 4, P]),
                                                ALU.subtract).then_inc(shifted, 1)
                when(pool, tail[tile_no(b, t)], body, [(shifted, 2)])

            for b in range(B - 1):
                pool.wait_ge(batch_max, b + 1)
                for t in range(TAIL):
                    shift(b, t)
            pool.wait_ge(wo_in, 32)
            for b in range(B):
                nc.gpsimd.tensor_tensor(xb[:, b], xs[:, b], rows[:, 1], ALU.add).then_inc(xb_made, 1)
            for j in range(1, len(GROUPS)):
                rstd_step(j)
            pool.wait_ge(over_made, 1)
            over = pool.value_load(over_i[0:1, 0:1])
            pool.wait_ge(y_stored, STORED)
            pool.wait_ge(rows_cleared, 16 * EX)
            with pool.If(over > 0):
                pool.wait_ge(y_stored, ROUNDS * STORED)
            pool.wait_ge(dest_made, 1)
            for i in range(B):
                for k in range(2):
                    pool.indirect_dma_start(out=yg[:, k, i], out_offset=None, in_=y_table,
                                            in_offset=bass.IndirectOffsetOnAxis(ap=dest[:, k, i:i + 1], axis=0)
                                            ).then_inc(y_back[i], 16)

        @block.scalar
        def _(act):
            for s in (h_kvkept, h_Tkept):
                act.sem_inc(s, CREDIT)
            act.dma_start(cst[:], consts).then_inc(cst_in, 16)
            act.dma_start(vec[:], vecs).then_inc(cst_in, 16)
            act.dma_start(wq[:], Wq).then_inc(wq_in, 16)
            act.dma_start(wk[:], Wk).then_inc(wkv_in, 16)
            act.dma_start(wv[:], Wv).then_inc(wkv_in, 16)
            act.dma_start(wo[:], Wo).then_inc(wo_in, 16)
            act.dma_start(rows[:], rows2.partition_broadcast(P)).then_inc(wo_in, 16)
            act.dma_start(kw0[:], KW0).then_inc(ffn_in, 16)
            act.wait_ge(cst_in, 32)
            for b in range(B):
                act.wait_ge(kv_made, b + 1)
                act.activation(kT[:, b], KV[b % 2][0][:, :], ACT.Identity, bias=vec[:, BK:BK + 1], scale=1.0
                               ).then_inc(kv_kept, 1)
                act.activation(V[:, b, :, :, 0:HD], KV[b % 2][1][:, :].rearrange("p (t h w) -> p t h w", t=TAIL, h=H),
                               ACT.Copy).then_inc(kv_kept, 1)
            tail, head = load_flags(act)

            def stream(sums):
                for b in range(B):
                    seq = b + B * sums
                    with act.Fori(0, HEAD) as i:
                        act.wait_ge(h_kv, CREDIT + i + HEAD * seq + 1)
                        act.wait_ge(h_scores, CREDIT + i + HEAD * seq)
                        act.activation(h_kT, C[0][:, 0:P], ACT.Identity, bias=vec[:, BK:BK + 1], scale=1.0
                                       ).then_inc(h_kvkept, 1)
                        if sums:
                            act.wait_ge(h_mixed, CREDIT + i + HEAD * b)
                            act.activation(h_V[:, :, 0:HD], C[0][:, P:2 * P].rearrange("p (h w) -> p h w", h=H), ACT.Copy
                                           ).then_inc(h_kvkept, 1)
                            act.wait_ge(h_vec, CREDIT + i + HEAD * seq + 1)
                            act.activation(h_S, h_S, ACT.Exp).then_inc(h_probs, 1)
                            for g in range(2):
                                act.wait_ge(h_T, CREDIT + i * 2 + 2 * HEAD * b + g + 1)
                                act.activation(h_PT[:, g * 512:(g + 1) * 512], C[g][:, :], ACT.Copy).then_inc(h_Tkept, 1)

            def exponentials(k):
                def body():
                    for g in range(2):
                        if k < LAST:
                            act.wait_ge(shifted, 2 * k + g + 1)
                        else:
                            act.wait_ge(shifted_last, 2 * (k - LAST) + g + 1)
                        s = S[:, k // TAIL % 2, k % TAIL, 4 * g:4 * g + 4]
                        act.activation(s, s, ACT.Exp).then_inc(probs_made, 1)
                when(act, tail[k], body, [(probs_made, 2)])

            def keep_probsT(k):
                def body():
                    if k >= 2:
                        act.wait_ge(mixed, k - 1)
                    for g in range(2 if k < LAST else 1):
                        act.wait_ge(probsT_made, 2 * k + g + 1)
                        act.activation(PT[:, k % 2, g * 512:(g + 1) * 512], C[g][:, :], ACT.Copy).then_inc(probsT_kept, 1)
                when(act, tail[k], body, [(probsT_kept, 2 if k < LAST else 1)])

            when(act, head, lambda: stream(False), [(h_kvkept, HEAD * B)])
            for k in range(B * TAIL):
                if k and k % TAIL == 0:
                    keep_probsT(k - 1)
                if k == LAST:
                    when(act, head, lambda: stream(True), [(h_kvkept, 2 * HEAD * B), (h_probs, HEAD * B), (h_Tkept, 2 * HEAD * B)])
                exponentials(k)
                if k % TAIL:
                    keep_probsT(k - 1)
            keep_probsT(B * TAIL - 1)
            act.wait_ge(onT_made, 1)
            act.activation(onT[:, 0:(B - 1) * P], A[0][:, 0:(B - 1) * P], ACT.Copy).then_inc(onT_kept, 1)
            act.wait_ge(onT_made, 2)
            act.activation(onT[:, (B - 1) * P:], C[0][:, 0:P], ACT.Copy).then_inc(onT_kept, 1)
            for s in range(B):
                act.wait_ge(xn1_made, s + 1)
                act.activation(squares[:, s], xn1[:, s], ACT.Square, accum_out=sc[:, s, s:s + 1]).then_inc(sc_own, 1)
            act.wait_ge(sc_ready, 1)
            act.activation(sce[:], scd[:], ACT.Exp, scale=float(P) ** -0.5).then_inc(sc_exp, 1)
            for i in range(2):
                act.wait_ge(xfT_made, i + 1)
                act.activation(xfT[:, 2 * i * P:2 * (i + 1) * P], C[i][:, 0:2 * P], ACT.Copy).then_inc(xfT_kept, 1)
            act.wait_ge(lg_ready, 1)
            act.activation(lge[:], lgd[:], ACT.Exp).then_inc(lg_exp, 1)

            def ffn(r, again):
                if again:
                    act.wait_ge(y_stored, r * STORED)

                def basis0(n):
                    act.wait_ge(xe_kept, r * EX + n + 1)
                    for g in range(G):
                        if g % 4 == 0 and n >= 2:
                            act.wait_ge(sq0_made, r * 8 + 2 * (n - 2) + g // 4 + 1)
                        i = act.activation(T0[:, n % 2, g], xe[:, n], ACT.Tanh, bias=tanh_bias(g))
                        if g % 4 == 3:
                            i.then_inc(t0_made, 1)

                def hidden(m):
                    for c in range(4):
                        k = 4 * m + c
                        act.wait_ge(hid_made, r * 8 + k // 2 + 1)
                        if k == 0:
                            act.wait_ge(sq0_made, r * 8 + 8)
                        act.activation(hT[:, m, c], Z[c // 2][:, c % 2 * SLOTS:(c % 2 + 1) * SLOTS], ACT.Gelu,
                                       bias=vec[:, MB1 + k:MB1 + k + 1], scale=1.0).then_inc(hid_kept, 1)

                def basis1(n):
                    act.wait_ge(u1_made, r * E2 + n + 1)
                    if n == 1:
                        act.wait_ge(y_made, r * EX + E2)
                    for g in range(G):
                        if g % 2 == 0 and n >= 2:
                            act.wait_ge(sq1_made, r * 16 + 4 * (n - 2) + g // 2 + 1)
                        i = act.activation(T1[:, n % 2, g], zs[:, n], ACT.Tanh, bias=tanh_bias(g))
                        if g % 2 == 1:
                            i.then_inc(t1_made, 1)

                def rows_out(n):
                    act.wait_ge(yn_made, r * EX + n + 1)
                    act.activation(yn[:, n, 0], YN[n % 2][:, 0:P], ACT.Copy)
                    act.activation(yn[0:REST, n, 1], YN[n % 2][0:REST, P:2 * P], ACT.Copy).then_inc(yn_kept_kan, 1)

                for n in range(E2):
                    basis0(n)
                hidden(0)
                hidden(1)
                act.wait_ge(vars_kept, r * E2 + E2)
                act.activation(var, var, ACT.Sqrt).then_inc(std_made, 1)
                hidden(2)
                hidden(3)
                basis1(0)
                for n in range(E2):
                    if n + 1 < E2:
                        basis1(n + 1)
                    if n:
                        rows_out(E2 + n - 1)
                rows_out(EX - 1)

            act.wait_ge(cst_in, 32)
            ffn(0, False)
            act.wait_ge(over_made, 1)
            over = act.value_load(over_i[0:1, 0:1])
            with act.If(over > 0):
                with act.Fori(1, ROUNDS) as r:
                    ffn(r, True)

        @block.tensor
        def _(pe):
            mm = nc.tensor.matmul
            for s in (h_kv, h_scores, h_T, h_mixed):
                pe.sem_inc(s, CREDIT)
            def keys_values(b):
                pe.wait_ge(ctx_in[b], 16)
                if b >= 2:
                    pe.wait_ge(kv_kept, 2 * (b - 1))
                k, v = KV[b % 2]
                mm(k[:, :], wk[:], ctx_t[:, b], start=True, stop=True)
                for t in range(TAIL):
                    last = mm(v[:, t * P:(t + 1) * P], ctx_t[:, b, t * P:(t + 1) * P], wv[:], start=True, stop=True)
                last.then_inc(kv_made, 1)

            pe.wait_ge(cst_in, 32)
            for b in range(B):
                pe.wait_ge(xn_made, b + 1)
                last = nc.tensor.transpose(A[0][:, b * P:(b + 1) * P], xn[:, b], ident)
            last.then_inc(xnT_made, 1)
            pe.wait_ge(ones_made, 4)
            pe.wait_ge(flags_made, 1)
            mm(A[1][0:1, 0:B * TILES], ones[:, 0:1], flags[:].rearrange("p b t -> p (b t)"), start=True, stop=True
               ).then_inc(anyq_made, 1)
            pe.wait_ge(xnT_kept, 1)
            pe.wait_ge(wq_in, 16)
            mm(A[0][:, 512:1024], wq[:], xnT, start=True, stop=True).then_inc(qT_made, 1)
            pe.wait_ge(wkv_in, 32)
            for b in range(B):
                keys_values(b)
            tail, head = load_flags(pe)
            pe.wait_ge(kv_kept, 2 * B)
            pe.wait_ge(pads_made, 4)

            def open_sums(b):
                mm(OV[b % 2][:, 0:256], zeros[:, 0:P], zeros[:, :], start=True, stop=True, skip_group_check=True
                   ).then_inc(ov_zeroed, 1)

            def mix_heads(b, v, probsT):
                for h in range(H):
                    last = mm(OV[b % 2][VW * (h % 4):VW * (h % 4 + 1), (h // 4) * P:(h // 4 + 1) * P], v[:, h],
                              probsT[:, h * P:(h + 1) * P], start=False, stop=True, skip_group_check=True)
                return last

            def stream(sums):
                pe.wait_ge(qm_rest, B - 1)
                for b in range(B):
                    seq = b + B * sums
                    if sums:
                        if b:
                            pe.wait_ge(h_added, b)
                        open_sums(1)
                    with pe.Fori(0, HEAD) as i:
                        pe.wait_ge(h_in, i * 32 + 32 * (HEAD * seq + 1))
                        pe.wait_ge(h_kvkept, kv_before(seq) + i * (1 + sums))
                        if sums:
                            pe.wait_ge(h_Tkept, CREDIT + i * 2 + 2 * HEAD * b)
                            mm(C[0][:, 0:P], wk[:], h_ctx, start=True, stop=True)
                            mm(C[0][:, P:2 * P], h_ctx, wv[:], start=True, stop=True).then_inc(h_kv, 1)
                        else:
                            mm(C[0][:, 0:P], wk[:], h_ctx, start=True, stop=True).then_inc(h_kv, 1)
                        pe.wait_ge(h_kvkept, kv_before(seq) + i * (1 + sums) + 1 + sums)
                        pe.wait_ge(h_kept, CREDIT + i + HEAD * seq)
                        for h in range(H):
                            last = mm(A[0][:, h * P:(h + 1) * P], QM[:, b, h], h_kT, start=True, stop=True)
                        last.then_inc(h_scores, 1)
                        if sums:
                            pe.wait_ge(h_probs, i + HEAD * b + 1)
                            for g in range(2):
                                for j in range(4):
                                    last = nc.tensor.transpose(C[g][:, j * P:(j + 1) * P], h_S[:, 4 * g + j], ident)
                                last.then_inc(h_T, 1)
                            pe.wait_ge(h_Tkept, CREDIT + i * 2 + 2 * HEAD * b + 2)
                            mix_heads(1, h_V, h_PT).then_inc(h_mixed, 1)
                pe.wait_ge(h_kept, CREDIT + HEAD * B * (1 + sums))

            def scores(k):
                b, t = divmod(k, TAIL)
                if b and t == 0:
                    pe.wait_ge(qm_rest, b)

                def body():
                    if k >= 2:
                        pe.wait_ge(scores_kept, k - 1)
                    for h in range(H):
                        last = mm(A[k % 2][:, h * P:(h + 1) * P], QM[:, b, h], kT[:, b, t * P:(t + 1) * P],
                                  start=True, stop=True)
                    last.then_inc(scores_made, 1)
                when(pe, tail[k], body, [(scores_made, 1)])

            def transposes(k):
                def body():
                    for g in range(2):
                        pe.wait_ge(probs_made, 2 * k + g + 1)
                        if k:
                            pe.wait_ge(*out_of_psum(k - 1, g))
                        for j in range(4):
                            last = nc.tensor.transpose(C[g][:, j * P:(j + 1) * P], S[:, k // TAIL % 2, k % TAIL, 4 * g + j], ident)
                        last.then_inc(probsT_made, 1)
                when(pe, tail[k], body, [(probsT_made, 2)])

            def mix(k):
                b, t = divmod(k, TAIL)
                if t == 0:
                    if b >= 2:
                        pe.wait_ge(oT_kept, b - 1)
                    if b == B - 1:
                        pe.wait_ge(h_added, B)
                    open_sums(b)

                def body():
                    for g in range(2):
                        pe.wait_ge(*out_of_psum(k, g))
                    mix_heads(b, V[:, b, t], PT[:, k % 2]).then_inc(mixed, 1)
                when(pe, tail[k], body, [(mixed, 1)])

            pe.wait_ge(qm_made, 1)
            when(pe, head, lambda: stream(False), [(h_kv, HEAD * B), (h_scores, HEAD * B)])
            AHEAD = TAIL + 2
            for k in range(AHEAD):
                scores(k)
            def to_queries(b):
                pe.wait_ge(oT_kept, b + 1)
                for g in range(2):
                    n = 2 * b + g
                    last = nc.tensor.transpose(A[1][:, n * P:(n + 1) * P], oT[:, b, g * P:(g + 1) * P], ident)
                last.then_inc(o_tok, 1)

            for k in range(B * TAIL):
                if k and k % TAIL == 0:
                    mix(k - 1)
                if k == LAST:
                    pe.wait_ge(scores_kept, B * TAIL)
                    pe.wait_ge(oT_kept, 2)
                    when(pe, head, lambda: stream(True),
                         [(h_kv, HEAD * B), (h_scores, HEAD * B), (h_T, 2 * HEAD * B), (h_mixed, HEAD * B)])
                    pe.wait_ge(h_added, B)
                    to_queries(0)
                    to_queries(1)
                transposes(k)
                if k % TAIL:
                    mix(k - 1)
                if k == LAST + 2:
                    to_queries(2)
                if k + AHEAD < B * TAIL:
                    scores(k + AHEAD)

            pe.wait_ge(on_made, B - 1)
            for b in range(B - 1):
                last = nc.tensor.transpose(A[0][:, b * P:(b + 1) * P], on[:, b * P:(b + 1) * P], ident)
            last.then_inc(onT_made, 1)
            mix(B * TAIL - 1)
            pe.wait_ge(wo_in, 32)
            pe.wait_ge(onT_kept, 1)
            for b in range(B - 1):
                last = mm(A[0][:, (4 + b) * P:(5 + b) * P], onT[:, b * P:(b + 1) * P], wo[:], start=True, stop=True)
            last.then_inc(proj_made, 1)
            to_queries(B - 1)
            pe.wait_ge(on_made, B)
            for g in range(2):
                pe.wait_ge(*out_of_psum(B * TAIL - 1, g))
            nc.tensor.transpose(C[0][:, 0:P], on[:, (B - 1) * P:], ident).then_inc(onT_made, 1)
            pe.wait_ge(onT_kept, 2)
            mm(C[1][:, 0:P], onT[:, (B - 1) * P:], wo[:], start=True, stop=True).then_inc(proj_made, 1)
            pe.wait_ge(ffn_in, 64)
            for i in range(2):
                if i:
                    pe.wait_ge(x1_made, 2)
                for b in (2 * i, 2 * i + 1):
                    pe.wait_ge(xf_made, b + 1)
                    last = nc.tensor.transpose(C[i][:, b % 2 * P:(b % 2 + 1) * P], xf[:, b], ident)
                last.then_inc(xfT_made, 1)
            for b in range(B):
                pe.wait_ge(xfT_kept, b // 2 + 1)
                last = mm(D[1][:, b * EX:(b + 1) * EX], xfT[:, b * P:(b + 1) * P], gate[:], start=True, stop=True)
            last.then_inc(logits_made, 1)
            pe.wait_ge(sel_made, 2)
            mm(D[1][:, 0:B * EX], upper, sel[:].rearrange("p i e -> p (i e)"), start=True, stop=False)
            mm(D[1][:, 0:B * EX], ones[:], cum[:, 0:B].rearrange("p i e -> p (i e)"), start=False, stop=True)
            mm(D[1][:, 64:64 + EX], ones[:], cum[:, B], start=True, stop=True).then_inc(pos_made, 1)

            def ffn(r, again):
                if again:
                    pe.wait_ge(y_stored, r * STORED)

                def gather(n):
                    src = xln if n < E2 else xf
                    pe.wait_ge(onehot_made, r * EX + n + 1)
                    if n >= 2:
                        pe.wait_ge(xe_kept, r * EX + n - 1)
                    for i in range(B):
                        last = mm(X[n % 2][:, 0:SLOTS], src[:, i], onehot[:, n % 4, i], start=(i == 0), stop=(i == B - 1))
                    last.then_inc(gathered, 1)

                def layer0(n):
                    if n >= 2:
                        pe.wait_ge(z_kept, r * E2 + n - 1)
                    for c in range(2):
                        for g in range(G):
                            if c == 0 and g % 4 == 0:
                                pe.wait_ge(sq0_made, r * 8 + 2 * n + g // 4 + 1)
                            last = mm(Z[n % 2][:, c * (SLOTS + 1):(c + 1) * (SLOTS + 1)], kw0[:, n, g, c * P:(c + 1) * P],
                                      SQ0[:, n % 2, g], start=(g == 0), stop=(g == G - 1))
                    last.then_inc(z_made, 1)

                def means(n):
                    pe.wait_ge(z_kept, r * E2 + n + 1)
                    if n:
                        pe.wait_ge(zd_made, r * E2 + n)
                    for c in range(2):
                        last = mm(MEAN[:, 0:SLOTS], mean_w[:], zs[:, n, c], start=(c == 0), stop=(c == 1))
                    last.then_inc(mean_made, 1)

                def variances(n):
                    pe.wait_ge(zq_made, r * E2 + n + 1)
                    if n:
                        pe.wait_ge(vars_kept, r * E2 + n)
                    for c in range(2):
                        last = mm(VAR[:, 0:SLOTS], mean_w[:], zq[:, n, c], start=(c == 0), stop=(c == 1))
                    last.then_inc(vars_made, 1)

                def up(m):
                    pe.wait_ge(xe_kept, r * EX + E2 + m + 1)
                    for c in range(4):
                        if m and c % 2 == 0:
                            pe.wait_ge(hid_kept, r * 16 + 4 * (m - 1) + c + 2)
                        last = mm(Z[c // 2][:, c % 2 * SLOTS:(c % 2 + 1) * SLOTS], mw1[:, m, c * P:(c + 1) * P], xe[:, E2 + m],
                                  start=True, stop=True)
                        if c % 2:
                            last.then_inc(hid_made, 1)

                def down(m):
                    if m >= 2:
                        pe.wait_ge(yT_kept, r * EX + m - 1)
                    for c in range(4):
                        pe.wait_ge(hid_kept, r * 16 + 4 * m + c + 1)
                        last = mm(Y[m % 2][:, 0:SLOTS], mw2[:, m, c], hT[:, m, c], start=(c == 0), stop=(c == 3))
                    last.then_inc(y_made, 1)

                def layer1(n):
                    pe.wait_ge(yT_kept, r * EX + E2 + n - 1)
                    for g in range(G):
                        if g == 4:
                            to_rows(E2 + n - 1)
                        if g % 2 == 0:
                            pe.wait_ge(sq1_made, r * 16 + 4 * n + g // 2 + 1)
                        for c in range(2):
                            last = mm(Y[n % 2], kw1[:, n, c, g], SQ1[:, n % 2, g, c],
                                      start=(g == 0 and c == 0), stop=(g == G - 1 and c == 1))
                    last.then_inc(y_made, 1)

                def to_rows(n):
                    pe.wait_ge(yT_kept, r * EX + n + 1)
                    if n >= 2:
                        pe.wait_ge(*rows_kept(r, n - 2))
                    else:
                        pe.wait_ge(xe_kept, r * EX + EX)
                    nc.tensor.transpose(YN[n % 2][:, 0:P], yT[:, n % 2, 0:P], ident)
                    nc.tensor.transpose(YN[n % 2][0:REST, P:2 * P], yT[:, n % 2, P:SLOTS], ident).then_inc(yn_made, 1)

                gather(0)
                gather(1)
                for n in range(E2):
                    layer0(n)
                    gather(n + 2)
                    if n:
                        means(n - 1)
                    if n >= 2:
                        variances(n - 2)
                pe.wait_ge(z_kept, r * E2 + E2)
                up(0)
                gather(6)
                means(3)
                variances(2)
                up(1)
                gather(7)
                variances(3)
                up(2)
                down(0)
                up(3)
                down(1)
                to_rows(0)
                down(2)
                to_rows(1)
                down(3)
                to_rows(2)
                pe.wait_ge(kw1_in, 16)
                for n in range(E2):
                    layer1(n)
                to_rows(7)

            ffn(0, False)
            pe.wait_ge(over_made, 1)
            over = pe.value_load(over_i[0:1, 0:1])
            with pe.If(over > 0):
                with pe.Fori(1, ROUNDS) as r:
                    ffn(r, True)

        @block.vector
        def _(dve):
            v = nc.vector
            for s in (h_biased, h_kept, h_vec):
                dve.sem_inc(s, CREDIT)
            count = [0]

            def own(ins):
                count[0] += 1
                ins.then_inc(dv, 1)

            def own_done():
                dve.wait_ge(dv, count[0])

            def statistics(j, src):
                n, lo, hi = GROUPS[j]
                for b in range(lo, hi):
                    own(v.bn_stats(stats[:, n, b], src[:, b]))
                for b in range(lo, hi):
                    if b == lo:
                        dve.wait_ge(dv, count[0] - (hi - lo) + 1)
                    else:
                        dve.wait_ge(dv, count[0])
                    i = v.bn_aggr(mv[:, n, b], stats[:, n, b])
                    if b < hi - 1:
                        own(i)
                    else:
                        i.then_inc(var_ready, 1)

            def normed(j, src, dst, made, blocks=None):
                n, lo, hi = GROUPS[j]
                own_done()
                dve.wait_ge(var_ready, j + 1)
                dve.wait_ge(rstd_made, j + 1)
                for b in (blocks or range(lo, hi)):
                    v.tensor_scalar(dst[:, b], src[:, b], mv[:, n, b, 0:1], rstd[:, n, b:b + 1], ALU.subtract, ALU.mult
                                    ).then_inc(made, 1)

            own(v.memset(mx[:], -NEG))
            dve.wait_ge(x_in, 16)
            statistics(0, xs)
            normed(0, xs, xn, xn_made)
            dve.wait_ge(mask_in, 16)
            own(v.tensor_reduce(flags[:].rearrange("p b t -> p (b t)"), mask_i32, AX, ALU.max))
            own_done()
            v.tensor_scalar(flags[:], flags[:], 0.0, None, ALU.is_gt).then_inc(flags_made, 1)
            dve.wait_ge(xnT_made, 1)
            v.tensor_copy(xnT, A[0][:, 0:512]).then_inc(xnT_kept, 1)
            dve.wait_ge(anyq_made, 1)
            dve.wait_ge(cst_in, 32)
            anyq = A[1][0:1, 0:B * TILES].rearrange("p (b t) -> p b t", b=B)
            own(v.tensor_copy(anyf[:, 0:B * TAIL].rearrange("p (b t) -> p b t", b=B), anyq[:, :, HEAD:]))
            own(v.tensor_reduce(anyf[:, B * TAIL:], anyq[:, :, 0:HEAD], mybir.AxisListType.XY, ALU.max))
            own_done()
            own(v.scalar_tensor_tensor(anyf[:], anyf[:], 1.0, powers, ALU.min, ALU.mult))
            own_done()
            own(v.tensor_reduce(word_f[:], anyf[:], AX, ALU.add))
            own_done()
            v.tensor_copy(word_i[:], word_f[:]).then_inc(word_made, 1)
            dve.wait_ge(qT_made, 1)
            v.tensor_scalar(qs, A[0][:, 512:1024], vec[:, BQ:BQ + 1], float(HD) ** -0.5, ALU.add, ALU.mult).then_inc(q_scaled, 1)
            dve.wait_ge(q_scaled, 1)
            v.tensor_tensor(QM[:, 0], qs[:, 0:P].unsqueeze(1).broadcast_to([P, H, P]),
                            hmask.unsqueeze(2).broadcast_to([P, H, P]), ALU.mult).then_inc(qm_made, 1)
            own(v.tensor_reduce(notwipe[:], flags[:], AX, ALU.max))
            own(v.tensor_scalar(hvec[:, 0:8], vec[:, G0:G0 + 8], 0.5, None, ALU.mult))
            own(v.tensor_scalar(hvec[:, 8:24], vec[:, G1:G1 + 16], 0.5, None, ALU.mult))
            tail, head = load_flags(dve)
            dve.wait_ge(bias_made, 1)

            def bias(ap):
                return ap.unsqueeze(1).broadcast_to([P, H, P])

            def spread(ap, n):
                return ap.unsqueeze(2).broadcast_to([P, H, n])

            def stream(sums):
                for b in range(B):
                    seq = b + B * sums
                    with dve.Fori(0, HEAD) as i:
                        dve.wait_ge(h_in, i * 32 + 32 * (HEAD * seq + 1))
                        dve.wait_ge(h_vec, CREDIT + i + HEAD * seq)
                        v.tensor_scalar(h_bias, h_mask_u8, NEG, -NEG, ALU.mult, ALU.add).then_inc(h_biased, 1)
                        dve.wait_ge(h_scores, CREDIT + i + HEAD * seq + 1)
                        dve.wait_ge(h_biased, CREDIT + i + HEAD * seq + 1)
                        if sums:
                            dve.wait_ge(h_T, CREDIT + i * 2 + 2 * HEAD * b)
                        v.tensor_tensor(h_S, A[0][:, :].rearrange("p (h k) -> p h k", h=H), bias(h_bias), ALU.add
                                        ).then_inc(h_kept, 1)
                        dve.wait_ge(h_kept, CREDIT + i + HEAD * seq + 1)
                        if sums:
                            v.tensor_tensor(h_S, h_S, spread(mxb[:, b], P), ALU.subtract).then_inc(h_vec, 1)
                        else:
                            v.tensor_reduce(mxt[:], h_S, AX, ALU.max).then_inc(h_max, 1)
                            dve.wait_ge(h_max, i + HEAD * b + 1)
                            v.tensor_tensor(mx[:, b, :, TAIL], mx[:, b, :, TAIL], mxt[:], ALU.max).then_inc(h_vec, 1)
                    if sums:
                        dve.wait_ge(h_mixed, CREDIT + HEAD * (b + 1))
                        v.tensor_tensor(oT[:, b], oT[:, b], OV[1][:, 0:256], ALU.add).then_inc(h_added, 1)

            def keep_scores(k):
                b, t = divmod(k, TAIL)
                if b and t == 0:
                    dve.wait_ge(bias_made, b + 1)

                def body():
                    dve.wait_ge(scores_made, k + 1)
                    if b >= 2:
                        dve.wait_ge(probsT_made, 2 * (k - 2 * TAIL) + 2)
                    s = S[:, b % 2, t]
                    v.tensor_tensor(s, A[k % 2][:, :].rearrange("p (h k) -> p h k", h=H), bias(mbias[:, b, t]), ALU.add
                                    ).then_inc(scores_kept, 1)
                    dve.wait_ge(scores_kept, k + 1)
                    v.tensor_reduce(mx[:, b, :, t], s, AX, ALU.max).then_inc(tile_max, 1)
                when(dve, tail[k], body, [(scores_kept, 1), (tile_max, 1)])

            def shift(k):
                def body():
                    for g in range(2):
                        s = S[:, k // TAIL % 2, k % TAIL, 4 * g:4 * g + 4]
                        v.tensor_tensor(s, s, mxb[:, B - 1, 4 * g:4 * g + 4].unsqueeze(2).broadcast_to([P, 4, P]),
                                        ALU.subtract).then_inc(shifted_last, 1)
                when(dve, tail[k], body, [(shifted_last, 2)])

            def keep_probsT(k):
                def body():
                    dve.wait_ge(mixed, k - 1)
                    dve.wait_ge(probsT_made, 2 * k + 2)
                    v.tensor_copy(PT[:, k % 2, 512:1024], C[1][:, :]).then_inc(probsT_last, 1)
                when(dve, tail[k], body, [(probsT_last, 1)])

            def maximum(b):
                dve.wait_ge(tile_max, TAIL * (b + 1))
                dve.wait_ge(h_vec, CREDIT + HEAD * B)
                v.tensor_reduce(mxb[:, b], mx[:, b], AX, ALU.max).then_inc(batch_max, 1)

            def keep_sums(b):
                dve.wait_ge(ov_zeroed, b + 1)
                dve.wait_ge(mixed, TAIL * (b + 1))
                if b < 2:
                    dve.wait_ge(bias_made, B)
                    v.tensor_copy(oT[:, b], OV[b % 2][:, 0:256]).then_inc(oT_kept, 1)
                else:
                    dve.wait_ge(h_added, B)
                    v.tensor_tensor(oT[:, b], oT[:, b], OV[b % 2][:, 0:256], ALU.add).then_inc(oT_kept, 1)

            own_done()
            when(dve, head, lambda: stream(False),
                 [(h_biased, HEAD * B), (h_kept, HEAD * B), (h_vec, HEAD * B), (h_max, HEAD * B)])
            for k in range(TAIL):
                keep_scores(k)
            for k in range(B * TAIL):
                b, t = divmod(k, TAIL)
                if t == 0:
                    maximum(b)
                if k < LAST:
                    keep_scores(k + TAIL)
                elif t == 0:
                    dve.wait_ge(batch_max, B)
                    dve.wait_ge(oT_kept, 2)
                    dve.wait_ge(oT_cleared, 1)
                    when(dve, head, lambda: stream(True),
                         [(h_biased, HEAD * B), (h_kept, HEAD * B), (h_vec, HEAD * B), (h_added, B)])
                    shift(k)
                    shift(k + 1)
                elif t + 1 < TAIL:
                    keep_probsT(k - 1)
                    shift(k + 1)
                if 0 < b and t == 1:
                    keep_sums(b - 1)

            def divide(lo, hi):
                dve.wait_ge(o_tok, hi)
                otok = A[1][:, lo * 256:hi * 256]
                own(v.tensor_scalar(den[:, lo:hi], otok.rearrange("p (b h w) -> p b h w", h=H, w=VW)[:, :, :, HD], 0.5, None, ALU.max))
                own_done()
                own(v.reciprocal(rden[:, lo:hi], den[:, lo:hi]))
                own_done()
                own(v.tensor_tensor(rdw[:, lo:hi], rden[:, lo:hi], notwipe[:, lo:hi].unsqueeze(2).broadcast_to([P, hi - lo, H]), ALU.mult))
                own_done()
                own(v.tensor_tensor(on[:, lo * P:hi * P].rearrange("p (n w) -> p n w", w=HD),
                                    otok.rearrange("p (n w) -> p n w", w=VW)[:, :, 0:HD],
                                    rdw[:, lo:hi].rearrange("p b h -> p (b h)").unsqueeze(2).broadcast_to([P, (hi - lo) * H, HD]), ALU.mult))
                dve.wait_ge(wo_in, 32)
                own_done()
                for b in range(lo, hi):
                    v.scalar_tensor_tensor(on[:, b * P:(b + 1) * P], rows[:, 0], notwipe[:, b:b + 1], on[:, b * P:(b + 1) * P],
                                           ALU.mult, ALU.add).then_inc(on_made, 1)

            keep_probsT(B * TAIL - 2)
            divide(0, B - 1)
            keep_probsT(B * TAIL - 1)
            keep_sums(B - 1)
            dve.wait_ge(xb_made, B)
            dve.wait_ge(proj_made, 1)
            v.tensor_tensor(x1[:, 0:B - 1], A[0][:, 4 * P:(3 + B) * P].rearrange("p (b d) -> p b d", d=P), xb[:, 0:B - 1], ALU.add
                            ).then_inc(x1_made, 1)
            dve.wait_ge(x1_made, 1)
            divide(B - 1, B)
            for b in range(B - 1):
                own(v.bn_stats(stats[:, 1, b], x1[:, b]))
            dve.wait_ge(proj_made, 2)
            v.tensor_tensor(x1[:, B - 1], C[1][:, 0:P], xb[:, B - 1], ALU.add).then_inc(x1_made, 1)
            dve.wait_ge(x1_made, 2)
            own(v.bn_stats(stats[:, 1, B - 1], x1[:, B - 1]))
            for b in range(B):
                dve.wait_ge(dv, count[0])
                i = v.bn_aggr(mv[:, 1, b], stats[:, 1, b])
                if b < B - 1:
                    own(i)
                else:
                    i.then_inc(var_ready, 1)
            normed(1, x1, xn1, xn1_made)
            for n, (s, t) in enumerate(((0, 1), (0, 2), (1, 2), (0, 3), (1, 3), (2, 3))):
                dve.wait_ge(xn1_made, t + 1)
                own(v.tensor_tensor_reduce(prod[:, n], xn1[:, s], xn1[:, t], 1.0, 0.0, ALU.mult, ALU.add, sc[:, s, t:t + 1]))
            own_done()
            for s in range(B - 1):
                own(v.tensor_copy(sc[:, s + 1:B, s], sc[:, s, s + 1:B]))
            own_done()
            dve.wait_ge(sc_own, B)
            own(v.tensor_reduce(scm[:], sc[:], AX, ALU.max))
            own_done()
            v.tensor_tensor(scd[:], sc[:], scm[:].unsqueeze(2).broadcast_to([P, B, B]), ALU.subtract).then_inc(sc_ready, 1)
            dve.wait_ge(sc_exp, 1)
            own(v.tensor_reduce(scs[:], sce[:], AX, ALU.add))
            own_done()
            own(v.reciprocal(scr[:], scs[:]))
            own_done()
            own(v.tensor_tensor(scp[:], sce[:], scr[:].unsqueeze(2).broadcast_to([P, B, B]), ALU.mult))
            own_done()
            for i in range(2):
                for t in range(B):
                    for s in (2 * i, 2 * i + 1):
                        if t:
                            dve.wait_ge(dv, count[0] - 1)
                        own(v.scalar_tensor_tensor(x2[:, s], xn1[:, t], scp[:, s, t:t + 1], (x2 if t else x1)[:, s], ALU.mult, ALU.add))
                own_done()
                statistics(2 + i, x2)
            for i in range(2):
                normed(2 + i, x2, xf, xf_made)
                dve.wait_ge(xf_made, 2 * i + 2)
                statistics(4 + i, xf)
            normed(4, xf, xln, xln_made)
            dve.wait_ge(logits_made, 1)
            lg = D[1][:, 0:B * EX].rearrange("p (i e) -> p i e", i=B)
            own(v.tensor_reduce(lgm[:], lg, AX, ALU.max))
            own_done()
            v.tensor_tensor(lgd[:], lg, lgm[:].unsqueeze(2).broadcast_to([P, B, EX]), ALU.subtract).then_inc(lg_ready, 1)
            normed(5, xf, xln, xln_made, (2,))
            dve.wait_ge(lg_exp, 1)
            mine = lge[:].unsqueeze(3).broadcast_to([P, B, EX, EX])
            other = lge[:].unsqueeze(2).broadcast_to([P, B, EX, EX])
            own(v.tensor_tensor(cmp_gt[:], other, mine, ALU.is_gt))
            own(v.tensor_tensor(cmp_eq[:], other, mine, ALU.is_equal))
            own_done()
            own(v.tensor_tensor(cmp_eq[:], cmp_eq[:], lower.unsqueeze(1).broadcast_to([P, B, EX, EX]), ALU.mult))
            own_done()
            own(v.tensor_tensor(cmp_gt[:], cmp_gt[:], cmp_eq[:], ALU.add))
            own_done()
            own(v.tensor_reduce(rank[:], cmp_gt[:], AX, ALU.add))
            own_done()
            v.tensor_scalar(sel[:], rank[:], 1.5, None, ALU.is_lt).then_inc(sel_made, 1)
            for k in range(2):
                own(v.tensor_scalar(first[:, k], rank[:], float(k), None, ALU.is_equal))
            own(v.memset(cum[:, 0], 0.0))
            dve.wait_ge(sel_made, 1)
            for i in range(B):
                own_done()
                ins = v.tensor_tensor(cum[:, i + 1], cum[:, i], sel[:, i], ALU.add)
                if i < B - 1:
                    own(ins)
                else:
                    ins.then_inc(sel_made, 1)
            normed(5, xf, xln, xln_made, (3,))
            dve.wait_ge(pos_made, 1)
            own(v.tensor_reduce(cmax[:], D[1][0:1, 64:64 + EX], AX, ALU.max))
            pos = D[1][:, 0:B * EX].rearrange("p (i e) -> p i e", i=B)
            own(v.scalar_tensor_tensor(posm[:], pos, 1.0, sel[:], ALU.add, ALU.mult))
            own(v.tensor_tensor(rowid[:], pos, eoff.unsqueeze(1).broadcast_to([P, B, EX]), ALU.add))
            own_done()
            v.tensor_scalar(over_i[:], cmax[:], float(SLOTS), None, ALU.is_gt).then_inc(over_made, 1)
            v.memset(SQ1[:, :, :, :, SLOTS:], 1.0).then_inc(sq_ones, 1)
            dve.wait_ge(sq_ones, 1)

            def route_weights():
                own(v.tensor_tensor(wtmp[:, 0], lge[:], first[:, 0], ALU.mult))
                own(v.tensor_tensor(wtmp[:, 1], lge[:], first[:, 1], ALU.mult))
                own(v.tensor_tensor(dtmp[:, 0], rowid[:], first[:, 0], ALU.mult))
                own(v.tensor_tensor(dtmp[:, 1], rowid[:], first[:, 1], ALU.mult))
                own_done()
                own(v.tensor_reduce(wsum[:], wtmp[:], AX, ALU.add))
                own(v.tensor_reduce(destf[:], dtmp[:], AX, ALU.add))
                own_done()
                v.tensor_copy(dest[:], destf[:]).then_inc(dest_made, 1)
                own(v.tensor_tensor(wden[:], wsum[:, 0], wsum[:, 1], ALU.add))
                own_done()
                own(v.reciprocal(wden[:], wden[:]))
                own_done()
                own(v.tensor_tensor(wgt[:], wsum[:], wden[:].unsqueeze(1).broadcast_to([P, 2, B]), ALU.mult))

            def ffn(r, again, off):
                mine = [0]

                def step(ins):
                    mine[0] += 1
                    ins.then_inc(fv, 1)

                def step_done(back=0):
                    dve.wait_ge(fv, off + (mine[0] - back))

                if again:
                    dve.wait_ge(y_stored, r * STORED)
                    step(v.tensor_scalar(posm[:], posm[:], -float(SLOTS), None, ALU.add))
                    step_done()

                def choose(n):
                    e = E2 + n if n < E2 else n - E2
                    if n >= 4:
                        dve.wait_ge(gathered, r * EX + n - 3)
                    for i in range(B):
                        ins = v.tensor_scalar(onehot[:, n % 4, i], iota1, posm[:, i, e:e + 1], None, ALU.is_equal)
                    ins.then_inc(onehot_made, 1)

                def keep_tokens(n):
                    dve.wait_ge(gathered, r * EX + n + 1)
                    if n < E2:
                        ins = v.tensor_scalar(xe[:, n], X[n % 2][:, 0:SLOTS], hvec[:, n:n + 1], hvec[:, 4 + n:5 + n],
                                              ALU.mult, ALU.add)
                    else:
                        ins = v.tensor_copy(xe[:, n], X[n % 2][:, 0:SLOTS])
                    ins.then_inc(xe_kept, 1)

                def squares0(n):
                    for g in range(0, G, 4):
                        dve.wait_ge(t0_made, r * 8 + 2 * n + g // 4 + 1)
                        if n >= 2 and g == 0:
                            dve.wait_ge(z_made, r * E2 + n - 1)
                        t = T0[:, n % 2, g:g + 4]
                        v.tensor_tensor(SQ0[:, n % 2, g:g + 4, 0:SLOTS], t, t, ALU.mult).then_inc(sq0_made, 1)

                def keep_z(n):
                    dve.wait_ge(z_made, r * E2 + n + 1)
                    z = Z[n % 2][:, 0:2 * (SLOTS + 1)].rearrange("p (c s) -> p c s", c=2)
                    step(v.tensor_tensor(cz[:, n], z[:, :, SLOTS], vec[:, SB0 + 2 * n:SB0 + 2 * n + 2], ALU.add))
                    step_done()
                    step(v.tensor_scalar(zs[:, n, 0], z[:, 0, 0:SLOTS], -1.0, cz[:, n, 0:1], ALU.mult, ALU.add))
                    v.tensor_scalar(zs[:, n, 1], z[:, 1, 0:SLOTS], -1.0, cz[:, n, 1:2], ALU.mult, ALU.add).then_inc(z_kept, 1)

                def centre(n):
                    dve.wait_ge(mean_made, r * E2 + n + 1)
                    v.tensor_tensor(zd[:, n], zs[:, n], MEAN[:, 0:SLOTS].unsqueeze(1).broadcast_to([P, 2, SLOTS]), ALU.subtract
                                    ).then_inc(zd_made, 1)
                    dve.wait_ge(zd_made, r * E2 + n + 1)
                    v.tensor_tensor(zq[:, n], zd[:, n], zd[:, n], ALU.mult).then_inc(zq_made, 1)

                def keep_var(n):
                    dve.wait_ge(vars_made, r * E2 + n + 1)
                    v.tensor_scalar(var[:, n], VAR[:, 0:SLOTS], EPS, None, ALU.add).then_inc(vars_kept, 1)

                def normalise(n):
                    dve.wait_ge(std_made, r + 1)
                    step(v.reciprocal(rsd[:, n], var[:, n]))
                    step_done()
                    step(v.tensor_tensor(zq[:, n], zd[:, n], rsd[:, n].unsqueeze(1).broadcast_to([P, 2, SLOTS]), ALU.mult))
                    step_done()
                    for c in range(2):
                        k = 2 * n + c
                        ins = v.tensor_scalar(zs[:, n, c], zq[:, n, c], hvec[:, 8 + k:9 + k], hvec[:, 16 + k:17 + k], ALU.mult, ALU.add)
                        if c == 0:
                            step(ins)
                        else:
                            step_done()
                            ins.then_inc(u1_made, 1)

                def squares1(n, gs=range(G)):
                    for g in gs[::2]:
                        dve.wait_ge(t1_made, r * 16 + 4 * n + g // 2 + 1)
                        if g == 0 and n >= 2:
                            dve.wait_ge(y_made, r * EX + E2 + n - 1)
                        if g == 0 and n == 0:
                            dve.wait_ge(z_made, r * E2 + E2)
                        for c in range(2):
                            t = T1[:, n % 2, g:g + 2, c]
                            ins = v.tensor_tensor(SQ1[:, n % 2, g:g + 2, c, 0:SLOTS], t, t, ALU.mult)
                        ins.then_inc(sq1_made, 1)

                def keep_y(n):
                    dve.wait_ge(y_made, r * EX + n + 1)
                    if n >= 2:
                        dve.wait_ge(yn_made, r * EX + n - 1)
                    y = Y[n % 2]
                    if n < E2:
                        v.tensor_scalar(yT[:, n % 2], y[:, 0:SLOTS], vec[:, MB2 + n:MB2 + n + 1], None, ALU.add).then_inc(yT_kept, 1)
                    else:
                        k = n - E2
                        step(v.tensor_tensor(cy[:, k:k + 1], y[:, SLOTS:SLOTS + 1], vec[:, SB1 + k:SB1 + k + 1], ALU.add))
                        step_done()
                        v.tensor_scalar(yT[:, n % 2], y[:, 0:SLOTS], -1.0, cy[:, k:k + 1], ALU.mult, ALU.add).then_inc(yT_kept, 1)

                def rows_out(n):
                    dve.wait_ge(yn_made, r * EX + n + 1)
                    v.tensor_copy(yn[:, n, 0], YN[n % 2][:, 0:P])
                    v.tensor_copy(yn[0:REST, n, 1], YN[n % 2][0:REST, P:2 * P]).then_inc(yn_kept_mlp, 1)

                choose(0)
                choose(1)
                keep_tokens(0)
                keep_tokens(1)
                choose(2)
                squares0(0)
                squares0(1)
                choose(3)
                if not again:
                    route_weights()
                for n in range(E2):
                    keep_z(n)
                    keep_tokens(n + 2)
                    if n:
                        centre(n - 1)
                    choose(n + 4)
                    if n + 2 < E2:
                        squares0(n + 2)
                    if n >= 2:
                        keep_var(n - 2)
                keep_tokens(6)
                centre(3)
                keep_var(2)
                keep_tokens(7)
                keep_var(3)
                normalise(0)
                keep_y(0)
                keep_y(1)
                rows_out(0)
                normalise(1)
                squares1(0, range(0, 2))
                keep_y(2)
                rows_out(1)
                squares1(0, range(2, 4))
                keep_y(3)
                rows_out(2)
                squares1(0, range(4, 8))
                squares1(1)
                rows_out(3)
                normalise(2)
                keep_y(4)
                squares1(2)
                normalise(3)
                keep_y(5)
                squares1(3)
                keep_y(6)
                keep_y(7)
                return mine[0]

            own_done()
            steps = ffn(0, False, 0)
            over = dve.value_load(over_i[0:1, 0:1])
            with dve.If(over > 0):
                with dve.Fori(1, ROUNDS) as r:
                    assert ffn(r, True, r * (steps + 1) - 1) == steps + 1
            own_done()
            for i in range(B):
                dve.wait_ge(y_back[i], 2 * 16)
                own(v.scalar_tensor_tensor(fin[:, i], yg[:, 0, i], wgt[:, 0, i:i + 1], x2[:, i], ALU.mult, ALU.add))
                own_done()
                v.scalar_tensor_tensor(fin[:, i], yg[:, 1, i], wgt[:, 1, i:i + 1], fin[:, i], ALU.mult, ALU.add).then_inc(fin_made, 1)


def constants():
    c = np.zeros((P, NC), np.float32)
    p = np.arange(P)
    c[:, C_ID:C_ID + P] = np.eye(P)
    c[:, C_U:C_U + P] = p[:, None] < p[None, :]
    c[:, C_HM:C_HM + H] = p[:, None] // HD == np.arange(H)[None, :]
    c[:, C_IOTA:C_IOTA + SLOTS] = 1 + np.arange(SLOTS)
    c[:, C_EOFF:C_EOFF + EX] = ROWS * np.arange(EX)
    e = np.arange(EX)
    c[:, C_POW:C_POW + B * TAIL + 1] = 2.0 ** np.arange(B * TAIL + 1)
    c[:, C_LT:C_LT + EX * EX] = (e[None, :] < e[:, None]).reshape(-1)
    return c


def arrays_of(i):
    def a(name):
        return np.asarray(i[name])

    rows = [a("L0_xattn_bq").reshape(1, P), a("L0_xattn_bk").reshape(1, P), a("L0_ffn_kan_ln_g0"), a("L0_ffn_kan_ln_b0"),
            a("L0_ffn_kan_sl_b0").reshape(-1, P), a("L0_ffn_kan_ln_g1").reshape(-1, P), a("L0_ffn_kan_ln_b1").reshape(-1, P),
            a("L0_ffn_kan_sl_b1"), a("L0_ffn_mlp_b2"), a("L0_ffn_mlp_b1").reshape(-1, P)]
    return {
        "x": a("x").transpose(1, 0, 2),
        "ctxT": a("ctx_1024").transpose(0, 2, 1),
        "mask": a("mask_BxSxS2_bk0").transpose(1, 0, 2),
        "Wq": a("L0_xattn_Wq"), "Wk": a("L0_xattn_Wk"), "Wv": a("L0_xattn_Wv"), "Wo": a("L0_xattn_Wo"),
        "rows2": np.stack([a("L0_xattn_bv"), a("L0_xattn_bo")]),
        "gateW": a("L0_ffn_gate_W"),
        "KW0": a("L0_ffn_kan_sl_W0").reshape(E2, P, G, F2).transpose(1, 0, 2, 3),
        "KW1": a("L0_ffn_kan_sl_W1").reshape(E2, 2, P, G, P).transpose(2, 0, 1, 3, 4),
        "MW1": a("L0_ffn_mlp_W1").transpose(1, 0, 2),
        "MW2": a("L0_ffn_mlp_W2").reshape(E2, 4, P, P).transpose(2, 0, 1, 3),
        "vecs": np.concatenate(rows, 0).T,
        "consts": constants(),
    }


def build(nc, arrays):
    args = []
    for name, value in arrays.items():
        args.append(nc.dram_tensor(name, value.shape, mybir.dt.from_np(value.dtype), kind="ExternalInput").ap())
    out = nc.dram_tensor("out", (B, P, P), F32, kind="ExternalOutput").ap()
    args[2] = args[2].bitcast(U8) if args[2].dtype != U8 else args[2]
    layer(nc, *args, out.rearrange("b q d -> q b d"))


def kernel(**inputs):
    import concourse.bacc as bacc
    from concourse.bass_utils import run_bass_kernel_spmd

    arrays = {k: np.ascontiguousarray(v) for k, v in arrays_of(inputs).items()}
    nc = bacc.Bacc("TRN2", target_bir_lowering=False, num_devices=1)
    build(nc, arrays)
    r = run_bass_kernel_spmd(nc, [arrays], core_ids=[0])
    return r.results[0]["out"]
```

```python
from contextlib import ExitStack

import concourse.bass as bass
from concourse import mybir
import numpy as np

F32 = mybir.dt.float32
I32 = mybir.dt.int32
U32 = mybir.dt.uint32
U8 = mybir.dt.uint8
ALU = mybir.AluOpType
ACT = mybir.ActivationFunctionType
AX = mybir.AxisListType.X

P = 128
B = 4
H = 8
HD = 16
VW = 32
KEYS = 2048
TILES = KEYS // P
TAIL = 4
HEAD = TILES - TAIL
CREDIT = 1
EPS = 1e-5
NEG = 1e30

NORMS = 4
GROUPS = ((0, 0, 4), (1, 0, 3), (1, 3, 4), (2, 0, 2), (2, 2, 4), (3, 0, 2), (3, 2, 4))

EX = 8
E2 = 4
G = 8
GRID = np.linspace(-1.2, 0.2, G).astype(np.float32)
F = 512
F2 = 256
SLOTS = 160
ROUNDS = 4
ROWS = SLOTS * ROUNDS
REST = SLOTS - P
ZP = 120

BQ, BK, G0, B0, SB0, G1, B1, SB1, MB2, MB1, NV = 0, 1, 2, 6, 10, 18, 26, 34, 38, 42, 58
C_ID, C_U, C_HM, C_IOTA, C_EOFF, C_LT, C_POW, NC = 0, 128, 256, 264, 264 + SLOTS, 272 + SLOTS, 336 + SLOTS, 353 + SLOTS


def layer(nc, x, ctxT, mask, Wqkv, Wo, rows2, gateW, KW0, KW1, MW1, MW2, vecs, consts, out):
    y_table = nc.dram_tensor("y_table", [EX * ROWS, P], F32, kind="Internal").ap()
    with ExitStack() as ctx:
        def sb(name, shape, dt=F32):
            return ctx.enter_context(nc.sbuf_tensor(name, shape, dt))

        def sem(name):
            return ctx.enter_context(nc.semaphore(name))

        cst = sb("cst", [P, NC])
        vec = sb("vec", [P, NV])
        hvec = sb("hvec", [P, 32])
        wqkv = sb("wqkv", [P, 3, P])
        wq, wk, wv = (wqkv[:, i] for i in range(3))
        bq4 = sb("bq4", [P, 1])
        wo = sb("wo", [P, P])
        rows = sb("rows", [P, 2, P])
        gate = sb("gate", [P, EX])
        kw0 = sb("kw0", [P, E2, G, F2])
        mw1 = sb("mw1", [P, E2, F])
        mw2 = sb("mw2", [P, E2, 4, P])
        ones = sb("ones", [P, P])
        mean_w = sb("mean_w", [P, P])
        row_w = sb("row_w", [P, E2, E2])
        spread_w = sb("spread_w", [E2, E2, P])
        zeros = sb("zeros", [P, 256])
        xs = sb("xs", [P, B, P])
        xb = sb("xb", [P, B, P])
        xn = sb("xn", [P, B, P])
        x1 = sb("x1", [P, B, P])
        xn1 = sb("xn1", [P, B, P])
        x2 = sb("x2", [P, B, P])
        xf = sb("xf", [P, B, P])
        xln = sb("xln", [P, B, P])
        stats = sb("stats", [P, NORMS, B, 6])
        mv = sb("mv", [P, NORMS, B, 2])
        vare = sb("vare", [P, NORMS, B])
        rstd = sb("rstd", [P, NORMS, B])
        mhalf = sb("mhalf", [P, B])
        flags = sb("flags", [P, B, TILES])
        anyf = sb("anyf", [1, B * TAIL + 1])
        word_f = sb("word_f", [1, 1])
        word_i = sb("word_i", [1, 1], I32)
        notwipe = sb("notwipe", [P, B])
        mx = sb("mx", [P, B, H, TAIL + 1])
        mxb = sb("mxb", [P, B, H])
        mxt = sb("mxt", [P, H])
        den = sb("den", [P, B, H])
        rden = sb("rden", [P, B, H])
        rdw = sb("rdw", [P, B, H])
        sc = sb("sc", [P, B, B])
        scm = sb("scm", [P, B])
        scd = sb("scd", [P, B, B])
        sce = sb("sce", [P, B, B])
        scs = sb("scs", [P, B])
        scr = sb("scr", [P, B])
        scp = sb("scp", [P, B, B])
        lgm = sb("lgm", [P, B])
        lgd = sb("lgd", [P, B, EX])
        lge = sb("lge", [P, B, EX])
        cmp_gt = sb("cmp_gt", [P, B, EX, EX])
        cmp_eq = sb("cmp_eq", [P, B, EX, EX])
        rank = sb("rank", [P, B, EX])
        mask_k = sb("mask_k", [P, 2, B, EX])
        sel = sb("sel", [P, B, EX])
        cum = sb("cum", [P, B + 1, EX])
        wsum = sb("wsum", [P, 2, B])
        wtmp = sb("wtmp", [P, 2, B, EX])
        wden = sb("wden", [P, B])
        wgt = sb("wgt", [P, 2, B])
        posm = sb("posm", [P, B, EX])
        rowid = sb("rowid", [P, B, EX])
        dtmp = sb("dtmp", [P, 2, B, EX])
        destf = sb("destf", [P, 2, B])
        dest = sb("dest", [P, 2, B], U32)
        cmax = sb("cmax", [1, 1])
        over_i = sb("over_i", [1, 1], I32)

        ARENA = 31440
        arena = sb("arena", [P, ARENA])
        at = [0]

        def part(size, pattern=None, **kw):
            a = arena[:, at[0]:at[0] + size]
            at[0] += size
            return a.rearrange(pattern, **kw) if pattern else a

        S = part(2 * TAIL * H * P, "p (u t h k) -> p u t h k", u=2, t=TAIL, h=H)
        PT = part(2 * H * P, "p (u n) -> p u n", u=2)
        V = part(B * TAIL * H * VW, "p (b t h w) -> p b t h w", b=B, t=TAIL, h=H)
        QM = part(H * B * P, "p (b h q) -> p b h q", h=H, b=B)
        kT = part(B * TAIL * P, "p (b n) -> p b n", b=B)
        ctx_t = part(B * TAIL * P, "p (b n) -> p b n", b=B)
        mask_f = part(B * KEYS // 4)
        mbias = part(B * TAIL * P, "p (b t k) -> p b t k", b=B, t=TAIL)
        h_ctx = part(P)
        h_mask = part(P // 4)
        h_bias = part(P)
        h_kT = part(P)
        h_V = part(H * VW, "p (h w) -> p h w", h=H)
        h_S = part(H * P, "p (h k) -> p h k", h=H)
        h_PT = part(H * P)
        xnT = PT[:, 0, 0:B * P]
        qs = PT[:, 1, 0:B * P]
        mask_u8 = mask_f.bitcast(U8).rearrange("p (b k) -> p b k", b=B)
        mask_i32 = mask_f.bitcast(I32).rearrange("p (t w) -> p t w", w=P // 4)
        h_mask_u8 = h_mask.bitcast(U8)
        oT = mask_f[:, 0:B * 256].rearrange("p (b n) -> p b n", b=B)
        on = S[:, 0, 0:2].rearrange("p t h k -> p (t h k)")[:, 0:B * P]
        onT = S[:, 0, 2:4].rearrange("p t h k -> p (t h k)")[:, 0:B * P]
        prod = S[:, 1, 0]
        squares = S[:, 1, 1, 0:B]

        at[0] = 0
        T1 = part(2 * G * 2 * SLOTS, "p (u g c s) -> p u g c s", u=2, g=G, c=2)
        SQ1 = part(2 * G * 2 * (SLOTS + 1), "p (u g c s) -> p u g c s", u=2, g=G, c=2)
        hT = T1[:, 1].rearrange("p g c s -> p (g c s)").rearrange("p (m c s) -> p m c s", m=E2, c=4)
        T0 = T1[:, :, :, 0]
        SQ0 = SQ1[:, :, :, 0]
        onehot = part(4 * B * SLOTS, "p (u i s) -> p u i s", u=4, i=B)
        xe = part(EX * SLOTS, "p (n s) -> p n s", n=EX)
        zs = part(E2 * 2 * SLOTS, "p (n c s) -> p n c s", n=E2, c=2)
        zd = part(E2 * 2 * SLOTS, "p (n c s) -> p n c s", n=E2, c=2)
        zq = part(E2 * 2 * SLOTS, "p (n c s) -> p n c s", n=E2, c=2)
        var = part(SLOTS)[0:E2, :]
        rsd = part(SLOTS)[0:E2, :]
        yT = part(2 * SLOTS, "p (u s) -> p u s", u=2)
        yn = part(EX * 2 * P, "p (n j d) -> p n j d", n=EX, j=2)
        cz = part(E2 * 2, "p (n c) -> p n c", n=E2)
        cy = part(E2)
        xfT = part(B * P)
        kw1 = part(E2 * 2 * G * P, "p (e c g o) -> p e c g o", e=E2, c=2, g=G)
        onehot_flat = onehot.rearrange("p u i s -> p (u i s)")
        yg = onehot_flat[:, 0:2 * B * P].rearrange("p (k i d) -> p k i d", k=2, i=B)
        fin = onehot_flat[:, 2 * B * P:3 * B * P].rearrange("p (i d) -> p i d", i=B)

        ident = cst[:, C_ID:C_ID + P]
        upper = cst[:, C_U:C_U + P]
        hmask = cst[:, C_HM:C_HM + H]
        iota1 = cst[:, C_IOTA:C_IOTA + SLOTS]
        eoff = cst[:, C_EOFF:C_EOFF + EX]
        powers = cst[0:1, C_POW:C_POW + B * TAIL + 1]
        lower = cst[:, C_LT:C_LT + EX * EX].rearrange("p (a b) -> p a b", a=EX)

        A = [ctx.enter_context(nc.psum_tensor(f"A{i}", [P, 1024], F32)) for i in range(2)]
        C = [ctx.enter_context(nc.psum_tensor(f"C{i}", [P, 512], F32)) for i in range(2)]
        D = [ctx.enter_context(nc.psum_tensor(f"D{i}", [P, 512], F32)) for i in range(2)]
        OV = D
        CA = [A[0][:, 0:512], A[0][:, 512:1024]]
        KV = [C, D]
        X = [C[0], C[1]]
        Z = [A[0][:, 0:512], A[0][:, 512:1024]]
        HID = [[a[:, 0:512], a[:, 512:1024]] for a in A]
        MEAN = A[1][:, 0:512]
        VAR = A[1][0:E2, 512:512 + SLOTS]
        Y = [d[:, 0:SLOTS + 1] for d in D]
        YN = X

        x_in = sem("x_in")
        cst_in = sem("cst_in")
        wqkv_in = sem("wqkv_in")
        vec_in = sem("vec_in")
        mask_in = sem("mask_in")
        ctx_in = [sem(f"ctx_in{b}") for b in range(B)]
        wo_in = sem("wo_in")
        ffn_in = sem("ffn_in")
        kw1_in = sem("kw1_in")
        ones_made = sem("ones_made")
        pads_made = sem("pads_made")
        row_w_cleared = sem("row_w_cleared")
        row_w_made = sem("row_w_made")
        spread_w_made = sem("spread_w_made")
        vhalf_made = sem("vhalf_made")
        dv = sem("dv")
        var_ready = sem("var_ready")
        eps_added = sem("eps_added")
        rstd_made = sem("rstd_made")
        xn_made = sem("xn_made")
        xnT_made = sem("xnT_made")
        xnT_kept = sem("xnT_kept")
        qT_made = sem("qT_made")
        bq_made = sem("bq_made")
        q_scaled = sem("q_scaled")
        qm_made = sem("qm_made")
        qm_rest = sem("qm_rest")
        kv_made = sem("kv_made")
        kv_kept = sem("kv_kept")
        flags_made = sem("flags_made")
        anyq_made = sem("anyq_made")
        word_made = sem("word_made")
        bias_made = sem("bias_made")
        xb_made = sem("xb_made")
        scores_made = sem("scores_made")
        scores_kept = sem("scores_kept")
        tile_max = sem("tile_max")
        batch_max = sem("batch_max")
        shifted = sem("shifted")
        shifted_last = sem("shifted_last")
        probs_made = sem("probs_made")
        probsT_made = sem("probsT_made")
        probsT_kept = sem("probsT_kept")
        probsT_last = sem("probsT_last")
        ov_zeroed = sem("ov_zeroed")
        mixed = sem("mixed")
        oT_cleared = sem("oT_cleared")
        oT_kept = sem("oT_kept")
        h_in = sem("h_in")
        h_biased = sem("h_biased")
        h_kv = sem("h_kv")
        h_kvkept = sem("h_kvkept")
        h_scores = sem("h_scores")
        h_kept = sem("h_kept")
        h_max = sem("h_max")
        h_vec = sem("h_vec")
        h_probs = sem("h_probs")
        h_T = sem("h_T")
        h_Tkept = sem("h_Tkept")
        h_mixed = sem("h_mixed")
        h_added = sem("h_added")
        on_made = sem("on_made")
        o_tok = sem("o_tok")
        scp_made = sem("scp_made")
        term_made = sem("term_made")
        x2_last = sem("x2_last")
        onT_made = sem("onT_made")
        onT_kept = sem("onT_kept")
        proj_made = sem("proj_made")
        xn1_made = sem("xn1_made")
        sc_own = sem("sc_own")
        x1_made = sem("x1_made")
        sc_ready = sem("sc_ready")
        sc_exp = sem("sc_exp")
        xf_made = sem("xf_made")
        xln_made = sem("xln_made")
        xfT_made = sem("xfT_made")
        xfT_kept = sem("xfT_kept")
        logits_made = sem("logits_made")
        lg_ready = sem("lg_ready")
        lg_exp = sem("lg_exp")
        sel_made = sem("sel_made")
        pos_made = sem("pos_made")
        over_made = sem("over_made")
        dest_made = sem("dest_made")
        sq_ones = sem("sq_ones")
        onehot_made = sem("onehot_made")
        gathered = sem("gathered")
        xe_kept = sem("xe_kept")
        t0_made = sem("t0_made")
        sq0_made = sem("sq0_made")
        z_made = sem("z_made")
        z_kept = sem("z_kept")
        mean_made = sem("mean_made")
        zd_made = sem("zd_made")
        zq_made = sem("zq_made")
        vars_made = sem("vars_made")
        vars_kept = sem("vars_kept")
        std_made = sem("std_made")
        inverse_made = sem("inverse_made")
        spread_made = sem("spread_made")
        scaled = sem("scaled")
        hid_made = sem("hid_made")
        hid_kept = sem("hid_kept")
        u1_made = sem("u1_made")
        t1_made = sem("t1_made")
        sq1_made = sem("sq1_made")
        l1_done = sem("l1_done")
        y_made = sem("y_made")
        yT_kept = sem("yT_kept")
        yn_made = sem("yn_made")
        yn_kept_mlp = sem("yn_kept_mlp")
        yn_kept_kan = sem("yn_kept_kan")
        y_stored = sem("y_stored")
        y_stored_last = sem("y_stored_last")
        fv = sem("fv")
        rows_cleared = sem("rows_cleared")
        y_back = [[sem(f"y_back{k}_{i}") for i in range(B)] for k in range(2)]
        fin_made = sem("fin_made")
        out_done = sem("out_done")
        STORED = (EX - 1) * 32
        FAR = float(1 << 20)

        def last_round_stored(eng, r):
            eng.wait_ge(y_stored, r * STORED)
            eng.wait_ge(y_stored_last, r * 32)

        def tanh_bias(g):
            return float(-0.5 * GRID[g])

        block = ctx.enter_context(nc.Block())

        def tile_no(b, t):
            return b * TAIL + t

        LAST = (B - 1) * TAIL

        def out_of_psum(k, g):
            if k < LAST:
                return probsT_kept, 2 * k + g + 1
            return (probsT_last if g else probsT_kept), (0 if g else 2 * LAST) + k - LAST + 1

        def probsT_psum(k, g):
            return CA[g] if k > LAST and k % 2 else C[g][:, :]

        def kv_before(seq):
            return CREDIT + HEAD * (seq if seq < B else 2 * seq - B)

        def load_flags(eng):
            eng.wait_ge(word_made, 1)
            word = eng.value_load(word_i[0:1, 0:1])
            return [word & (1 << k) for k in range(B * TAIL)], word & (1 << (B * TAIL))

        def rows_kept(r, n):
            return (yn_kept_mlp if n < E2 else yn_kept_kan), r * E2 + n % E2 + 1

        def when(eng, flag, body, passed_over):
            with eng.If(flag > 0):
                body()
            with eng.Else():
                eng.drain()
                for s, n in passed_over:
                    eng.sem_inc(s, n)

        @block.sync
        def _(sp):
            sp.dma_start(xs[:], x).then_inc(x_in, 16)
            sp.dma_start(ctx_t[:, 0], ctxT[0, :, HEAD * P:]).then_inc(ctx_in[0], 16)
            sp.dma_start(mask_u8, mask).then_inc(mask_in, 16)
            sp.dma_start(cst[:], consts).then_inc(cst_in, 16)
            for b in range(1, B):
                sp.dma_start(ctx_t[:, b], ctxT[b, :, HEAD * P:]).then_inc(ctx_in[b], 16)
            sp.dma_start(gate[:], gateW).then_inc(ffn_in, 16)
            sp.dma_start(kw0[:], KW0).then_inc(ffn_in, 16)
            sp.dma_start(mw1[:], MW1).then_inc(ffn_in, 16)
            sp.dma_start(mw2[:], MW2).then_inc(ffn_in, 16)
            sp.wait_ge(ones_made, 4)
            for e in range(EX):
                sp.dma_start(y_table[e * ROWS + SLOTS:(e + 1) * ROWS, :].rearrange("(p r) w -> p r w", p=ZP),
                             zeros[0:ZP, 0:P].unsqueeze(1).broadcast_to([ZP, (ROWS - SLOTS) // ZP, P])).then_inc(rows_cleared, 16)
            tail, head = load_flags(sp)

            def stream(first):
                for seq in range(first, first + B):
                    with sp.Fori(0, HEAD) as i:
                        sp.wait_ge(h_kv, CREDIT + i + HEAD * seq)
                        sp.wait_ge(h_biased, CREDIT + i + HEAD * seq)
                        sp.dma_start(h_ctx, ctxT[seq % B, :, bass.ds(i * P, P)]).then_inc(h_in, 16)
                        sp.dma_start(h_mask_u8, mask[:, seq % B, bass.ds(i * P, P)]).then_inc(h_in, 16)
                sp.wait_ge(h_in, 32 * HEAD * (first + B))

            for first in (0, B):
                when(sp, head, lambda: stream(first), [(h_in, 32 * HEAD * B)])
            sp.wait_ge(o_tok, B)
            sp.dma_start(kw1, KW1).then_inc(kw1_in, 16)

            def store_round(off, row):
                for n in range(EX):
                    e = n
                    stored = y_stored if n < EX - 1 else y_stored_last
                    sp.wait_ge(*rows_kept(off, n))
                    sp.dma_start(y_table[bass.ds(row + e * ROWS, P), :], yn[:, n, 0]).then_inc(stored, 16)
                    sp.dma_start(y_table[bass.ds(row + e * ROWS + P, REST), :], yn[0:REST, n, 1]).then_inc(stored, 16)

            store_round(0, 0)
            sp.wait_ge(rows_cleared, 16 * EX)
            sp.wait_ge(over_made, 1)
            over = sp.value_load(over_i[0:1, 0:1])
            with sp.If(over > 0):
                with sp.Fori(1, ROUNDS) as r:
                    store_round(r, r * SLOTS)
            for i in range(B):
                sp.wait_ge(fin_made, i + 1)
                sp.dma_start(out[:, i], fin[:, i]).then_inc(out_done, 16)
            sp.wait_ge(out_done, 16 * B)

        @block.gpsimd
        def _(pool):
            nc.gpsimd.memset(ones[:], 1.0).then_inc(ones_made, 1)
            nc.gpsimd.memset(mhalf[:], -0.5).then_inc(ones_made, 1)
            nc.gpsimd.memset(mean_w[:], 1.0 / F2).then_inc(ones_made, 1)
            nc.gpsimd.memset(row_w[:], 0.0).then_inc(row_w_cleared, 1)
            nc.gpsimd.memset(zeros[:], 0.0).then_inc(ones_made, 1)
            def rstd_step(j):
                n, lo, hi = GROUPS[j]
                pool.wait_ge(var_ready, j + 1)
                nc.gpsimd.tensor_scalar(vare[:, n, lo:hi], mv[:, n, lo:hi, 1], EPS, None, ALU.add).then_inc(eps_added, 1)
                pool.wait_ge(eps_added, j + 1)
                nc.gpsimd.tensor_tensor(rstd[:, n, lo:hi], vare[:, n, lo:hi], mhalf[:, lo:hi], ALU.pow).then_inc(rstd_made, 1)

            pool.wait_ge(ones_made, 2)
            rstd_step(0)
            pool.wait_ge(row_w_cleared, 1)
            nc.gpsimd.memset(row_w[:].rearrange("p a b -> p (a b)")[:, 0::E2 + 1], 1.0 / F2).then_inc(row_w_made, 1)
            for v in (V.rearrange("p b t h w -> p (b t h) w"), h_V):
                nc.gpsimd.memset(v[:, :, HD + 1:], 0.0).then_inc(pads_made, 1)
                nc.gpsimd.memset(v[:, :, HD:HD + 1], 1.0).then_inc(pads_made, 1)
            pool.wait_ge(mask_in, 16)
            for b in range(B):
                nc.gpsimd.tensor_scalar(mbias[:, b], mask_u8[:, b, HEAD * P:].rearrange("p (t k) -> p t k", t=TAIL),
                                        NEG, -NEG, ALU.mult, ALU.add).then_inc(bias_made, 1)
            pool.wait_ge(q_scaled, 1)
            pool.wait_ge(cst_in, 16)
            pool.wait_ge(flags_made, 1)
            pool.wait_ge(bias_made, B)
            nc.gpsimd.memset(oT[:, 2:], 0.0).then_inc(oT_cleared, 1)
            for b in range(1, B):
                nc.gpsimd.tensor_tensor(QM[:, b], qs[:, b * P:(b + 1) * P].unsqueeze(1).broadcast_to([P, H, P]),
                                        hmask.unsqueeze(2).broadcast_to([P, H, P]), ALU.mult).then_inc(qm_rest, 1)
            tail, _ = load_flags(pool)

            def shift(b, t):
                def body():
                    for g in range(2):
                        s = S[:, b % 2, t, 4 * g:4 * g + 4]
                        nc.gpsimd.tensor_tensor(s, s, mxb[:, b, 4 * g:4 * g + 4].unsqueeze(2).broadcast_to([P, 4, P]),
                                                ALU.subtract).then_inc(shifted, 1)
                when(pool, tail[tile_no(b, t)], body, [(shifted, 2)])

            for b in range(B - 1):
                pool.wait_ge(batch_max, b + 1)
                for t in range(TAIL):
                    shift(b, t)
            pool.wait_ge(wo_in, 32)
            for b in range(B):
                nc.gpsimd.tensor_tensor(xb[:, b], xs[:, b], rows[:, 1], ALU.add).then_inc(xb_made, 1)
            for j in (1, 2):
                rstd_step(j)
            pool.wait_ge(x1_made, 2)
            for t in range(B - 1):
                pool.wait_ge(term_made, 2 * t + 2)
                if t:
                    pool.wait_ge(x2_last, t)
                nc.gpsimd.tensor_tensor(x2[:, 2:4], (x2 if t else x1)[:, 2:4], prod[:, 2 * t:2 * t + 2], ALU.add).then_inc(x2_last, 1)
            for j in range(3, len(GROUPS)):
                rstd_step(j)
            pool.wait_ge(over_made, 1)
            over = pool.value_load(over_i[0:1, 0:1])
            pool.wait_ge(rows_cleared, 16 * EX)
            pool.wait_ge(y_stored, STORED)
            with pool.If(over > 0):
                pool.wait_ge(y_stored, ROUNDS * STORED)
            pool.wait_ge(dest_made, 1)
            for k in range(2):
                if k:
                    pool.wait_ge(y_stored_last, 32)
                    with pool.If(over > 0):
                        pool.wait_ge(y_stored_last, ROUNDS * 32)
                for i in range(B):
                    pool.indirect_dma_start(out=yg[:, k, i], out_offset=None,
                                            in_=y_table if k else y_table[0:(EX - 1) * ROWS, :],
                                            in_offset=bass.IndirectOffsetOnAxis(ap=dest[:, k, i:i + 1], axis=0)
                                            ).then_inc(y_back[k][i], 16)

        @block.scalar
        def _(act):
            for s in (h_kvkept, h_Tkept):
                act.sem_inc(s, CREDIT)
            act.dma_start(wqkv[:], Wqkv).then_inc(wqkv_in, 16)
            act.dma_start(vec[:], vecs).then_inc(vec_in, 16)
            act.dma_start(wo[:], Wo).then_inc(wo_in, 16)
            act.dma_start(rows[:], rows2.partition_broadcast(P)).then_inc(wo_in, 16)
            act.wait_ge(vec_in, 16)
            act.activation(bq4[:], vec[:, BQ:BQ + 1], ACT.Copy, scale=float(HD) ** -0.5).then_inc(bq_made, 1)

            def keep_keys_values(b):
                act.wait_ge(kv_made, b + 1)
                act.activation(kT[:, b], KV[b % 2][0][:, :], ACT.Identity, bias=vec[:, BK:BK + 1], scale=1.0
                               ).then_inc(kv_kept, 1)
                act.activation(V[:, b, :, :, 0:HD], KV[b % 2][1][:, :].rearrange("p (t h w) -> p t h w", t=TAIL, h=H),
                               ACT.Copy).then_inc(kv_kept, 1)

            keep_keys_values(0)
            act.wait_ge(xnT_made, 1)
            act.activation(xnT, A[0][:, 0:512], ACT.Copy).then_inc(xnT_kept, 1)
            act.wait_ge(qT_made, 1)
            act.wait_ge(bq_made, 1)
            act.activation(qs, A[0][:, 512:1024], ACT.Identity, bias=bq4[:, 0:1], scale=float(HD) ** -0.5).then_inc(q_scaled, 1)
            for b in range(1, B):
                keep_keys_values(b)
            tail, head = load_flags(act)

            def stream(sums):
                for b in range(B):
                    seq = b + B * sums
                    with act.Fori(0, HEAD) as i:
                        act.wait_ge(h_kv, CREDIT + i + HEAD * seq + 1)
                        act.wait_ge(h_scores, CREDIT + i + HEAD * seq)
                        act.activation(h_kT, C[0][:, 0:P], ACT.Identity, bias=vec[:, BK:BK + 1], scale=1.0
                                       ).then_inc(h_kvkept, 1)
                        if sums:
                            act.wait_ge(h_mixed, CREDIT + i + HEAD * b)
                            act.activation(h_V[:, :, 0:HD], C[0][:, P:2 * P].rearrange("p (h w) -> p h w", h=H), ACT.Copy
                                           ).then_inc(h_kvkept, 1)
                            act.wait_ge(h_vec, CREDIT + i + HEAD * seq + 1)
                            act.activation(h_S, h_S, ACT.Exp).then_inc(h_probs, 1)
                            for g in range(2):
                                act.wait_ge(h_T, CREDIT + i * 2 + 2 * HEAD * b + g + 1)
                                act.activation(h_PT[:, g * 512:(g + 1) * 512], C[g][:, :], ACT.Copy).then_inc(h_Tkept, 1)

            def exponentials(k):
                def body():
                    for g in range(2):
                        if k < LAST:
                            act.wait_ge(shifted, 2 * k + g + 1)
                        else:
                            act.wait_ge(shifted_last, 2 * (k - LAST) + g + 1)
                        s = S[:, k // TAIL % 2, k % TAIL, 4 * g:4 * g + 4]
                        act.activation(s, s, ACT.Exp).then_inc(probs_made, 1)
                when(act, tail[k], body, [(probs_made, 2)])

            def keep_probsT(k):
                def body():
                    if k >= 2:
                        act.wait_ge(mixed, k - 1)
                    for g in range(2 if k < LAST else 1):
                        act.wait_ge(probsT_made, 2 * k + g + 1)
                        act.activation(PT[:, k % 2, g * 512:(g + 1) * 512], probsT_psum(k, g), ACT.Copy).then_inc(probsT_kept, 1)
                when(act, tail[k], body, [(probsT_kept, 2 if k < LAST else 1)])

            when(act, head, lambda: stream(False), [(h_kvkept, HEAD * B)])
            for k in range(B * TAIL):
                if k and k % TAIL == 0:
                    keep_probsT(k - 1)
                if k == LAST:
                    when(act, head, lambda: stream(True), [(h_kvkept, 2 * HEAD * B), (h_probs, HEAD * B), (h_Tkept, 2 * HEAD * B)])
                exponentials(k)
                if k % TAIL:
                    keep_probsT(k - 1)
            keep_probsT(B * TAIL - 1)
            act.wait_ge(onT_made, 1)
            act.activation(onT[:, 0:(B - 1) * P], C[0][:, 0:(B - 1) * P], ACT.Copy).then_inc(onT_kept, 1)
            act.wait_ge(onT_made, 2)
            act.activation(onT[:, (B - 1) * P:], A[0][:, 0:P], ACT.Copy).then_inc(onT_kept, 1)
            for s in range(B):
                act.wait_ge(xn1_made, s + 1)
                act.activation(squares[:, s], xn1[:, s], ACT.Square, accum_out=sc[:, s, s:s + 1]).then_inc(sc_own, 1)
            act.wait_ge(sc_ready, 1)
            act.activation(sce[:], scd[:], ACT.Exp, scale=float(P) ** -0.5).then_inc(sc_exp, 1)
            act.wait_ge(scp_made, 1)
            for t in range(B):
                for s in (2, 3):
                    act.activation(prod[:, 2 * t + s - 2], xn1[:, t], ACT.Copy, scale=scp[:, s, t:t + 1]).then_inc(term_made, 1)
            for i in range(2):
                act.wait_ge(xfT_made, i + 1)
                act.activation(xfT[:, 2 * i * P:2 * (i + 1) * P], C[i][:, 0:2 * P], ACT.Copy).then_inc(xfT_kept, 1)
            act.wait_ge(lg_ready, 1)
            act.activation(lge[:], lgd[:], ACT.Exp).then_inc(lg_exp, 1)

            def ffn(r, again):
                if again:
                    last_round_stored(act, r)

                def basis0(n):
                    act.wait_ge(xe_kept, r * EX + n + 1)
                    for g in range(G):
                        if g % 4 == 0 and n >= 2:
                            act.wait_ge(sq0_made, r * 8 + 2 * (n - 2) + g // 4 + 1)
                        i = act.activation(T0[:, n % 2, g], xe[:, n], ACT.Tanh, bias=tanh_bias(g))
                        if g % 4 == 3:
                            i.then_inc(t0_made, 1)

                def hidden(m):
                    for c in range(4):
                        k = 4 * m + c
                        act.wait_ge(hid_made, r * 8 + k // 2 + 1)
                        if k == 0:
                            act.wait_ge(sq0_made, r * 8 + 8)
                        act.activation(hT[:, m, c], HID[m % 2][c // 2][:, c % 2 * SLOTS:(c % 2 + 1) * SLOTS], ACT.Gelu,
                                       bias=vec[:, MB1 + k:MB1 + k + 1], scale=1.0).then_inc(hid_kept, 1)

                def basis1(n):
                    act.wait_ge(u1_made, r * E2 + n + 1)
                    if n == 1:
                        act.wait_ge(y_made, r * EX + E2)
                    for g in range(G):
                        if g % 2 == 0 and n >= 2:
                            act.wait_ge(sq1_made, r * 16 + 4 * (n - 2) + g // 2 + 1)
                        i = act.activation(T1[:, n % 2, g], zs[:, n], ACT.Tanh, bias=tanh_bias(g))
                        if g % 2 == 1:
                            i.then_inc(t1_made, 1)

                def rows_out(n):
                    act.wait_ge(yn_made, r * EX + n + 1)
                    act.activation(yn[:, n, 0], YN[n % 2][:, 0:P], ACT.Copy)
                    act.activation(yn[0:REST, n, 1], YN[n % 2][0:REST, P:2 * P], ACT.Copy).then_inc(yn_kept_kan, 1)

                for n in range(E2):
                    basis0(n)
                act.wait_ge(vars_kept, r + 1)
                act.activation(var, var, ACT.Sqrt).then_inc(std_made, 1)
                for m in range(E2):
                    hidden(m)
                basis1(0)
                for n in range(E2):
                    if n + 1 < E2:
                        basis1(n + 1)
                    if n:
                        rows_out(E2 + n - 1)
                rows_out(EX - 1)

            ffn(0, False)
            act.wait_ge(over_made, 1)
            over = act.value_load(over_i[0:1, 0:1])
            with act.If(over > 0):
                with act.Fori(1, ROUNDS) as r:
                    ffn(r, True)

        @block.tensor
        def _(pe):
            mm = nc.tensor.matmul
            for s in (h_kv, h_scores, h_T, h_mixed):
                pe.sem_inc(s, CREDIT)
            def keys_values(b):
                pe.wait_ge(ctx_in[b], 16)
                if b >= 2:
                    pe.wait_ge(kv_kept, 2 * (b - 1))
                k, v = KV[b % 2]
                mm(k[:, :], wk[:], ctx_t[:, b], start=True, stop=True)
                for t in range(TAIL):
                    last = mm(v[:, t * P:(t + 1) * P], ctx_t[:, b, t * P:(t + 1) * P], wv[:], start=True, stop=True)
                last.then_inc(kv_made, 1)

            pe.wait_ge(wqkv_in, 16)
            keys_values(0)
            pe.wait_ge(cst_in, 16)
            for b in range(B):
                pe.wait_ge(xn_made, b + 1)
                last = nc.tensor.transpose(A[0][:, b * P:(b + 1) * P], xn[:, b], ident)
            last.then_inc(xnT_made, 1)
            pe.wait_ge(ones_made, 4)
            pe.wait_ge(flags_made, 1)
            mm(A[1][0:1, 0:B * TILES], ones[:, 0:1], flags[:].rearrange("p b t -> p (b t)"), start=True, stop=True
               ).then_inc(anyq_made, 1)
            pe.wait_ge(xnT_kept, 1)
            mm(A[0][:, 512:1024], wq[:], xnT, start=True, stop=True).then_inc(qT_made, 1)
            tail, head = load_flags(pe)

            def open_sums(b):
                mm(OV[b % 2][:, 0:256], zeros[:, 0:P], zeros[:, :], start=True, stop=True, skip_group_check=True
                   ).then_inc(ov_zeroed, 1)

            def mix_heads(b, v, probsT):
                for h in range(H):
                    last = mm(OV[b % 2][VW * (h % 4):VW * (h % 4 + 1), (h // 4) * P:(h // 4 + 1) * P], v[:, h],
                              probsT[:, h * P:(h + 1) * P], start=False, stop=True, skip_group_check=True)
                return last

            def stream(sums):
                pe.wait_ge(qm_rest, B - 1)
                pe.wait_ge(kv_kept, 2 * B)
                pe.wait_ge(scores_kept, B * TAIL if sums else TAIL)
                for b in range(B):
                    seq = b + B * sums
                    if sums:
                        if b:
                            pe.wait_ge(h_added, b)
                        open_sums(1)
                    with pe.Fori(0, HEAD) as i:
                        pe.wait_ge(h_in, i * 32 + 32 * (HEAD * seq + 1))
                        pe.wait_ge(h_kvkept, kv_before(seq) + i * (1 + sums))
                        if sums:
                            pe.wait_ge(h_Tkept, CREDIT + i * 2 + 2 * HEAD * b)
                            mm(C[0][:, 0:P], wk[:], h_ctx, start=True, stop=True)
                            mm(C[0][:, P:2 * P], h_ctx, wv[:], start=True, stop=True).then_inc(h_kv, 1)
                        else:
                            mm(C[0][:, 0:P], wk[:], h_ctx, start=True, stop=True).then_inc(h_kv, 1)
                        pe.wait_ge(h_kvkept, kv_before(seq) + i * (1 + sums) + 1 + sums)
                        pe.wait_ge(h_kept, CREDIT + i + HEAD * seq)
                        for h in range(H):
                            last = mm(A[0][:, h * P:(h + 1) * P], QM[:, b, h], h_kT, start=True, stop=True)
                        last.then_inc(h_scores, 1)
                        if sums:
                            pe.wait_ge(h_probs, i + HEAD * b + 1)
                            for g in range(2):
                                for j in range(4):
                                    last = nc.tensor.transpose(C[g][:, j * P:(j + 1) * P], h_S[:, 4 * g + j], ident)
                                last.then_inc(h_T, 1)
                            pe.wait_ge(h_Tkept, CREDIT + i * 2 + 2 * HEAD * b + 2)
                            mix_heads(1, h_V, h_PT).then_inc(h_mixed, 1)
                pe.wait_ge(h_kept, CREDIT + HEAD * B * (1 + sums))

            def scores(k):
                b, t = divmod(k, TAIL)
                if b and t == 0:
                    pe.wait_ge(qm_rest, b)
                    pe.wait_ge(kv_kept, 2 * b + 1)

                def body():
                    if k >= 2:
                        pe.wait_ge(scores_kept, k - 1)
                    for h in range(H):
                        last = mm(A[k % 2][:, h * P:(h + 1) * P], QM[:, b, h], kT[:, b, t * P:(t + 1) * P],
                                  start=True, stop=True)
                    last.then_inc(scores_made, 1)
                when(pe, tail[k], body, [(scores_made, 1)])

            def transposes(k):
                def body():
                    if k < TAIL:
                        pe.wait_ge(kv_kept, 2 * B)
                    for g in range(2):
                        pe.wait_ge(probs_made, 2 * k + g + 1)
                        if k > LAST:
                            pe.wait_ge(*out_of_psum(k - 2, g))
                        elif k:
                            pe.wait_ge(*out_of_psum(k - 1, g))
                        for j in range(4):
                            last = nc.tensor.transpose(probsT_psum(k, g)[:, j * P:(j + 1) * P], S[:, k // TAIL % 2, k % TAIL, 4 * g + j], ident)
                        last.then_inc(probsT_made, 1)
                when(pe, tail[k], body, [(probsT_made, 2)])

            def mix(k):
                b, t = divmod(k, TAIL)
                if t == 0:
                    if b >= 2:
                        pe.wait_ge(oT_kept, b - 1)
                    if b == B - 1:
                        pe.wait_ge(h_added, B)
                    if b == 0:
                        pe.wait_ge(kv_kept, 2 * B)
                        pe.wait_ge(pads_made, 4)
                    open_sums(b)

                def body():
                    for g in range(2):
                        pe.wait_ge(*out_of_psum(k, g))
                    mix_heads(b, V[:, b, t], PT[:, k % 2]).then_inc(mixed, 1)
                when(pe, tail[k], body, [(mixed, 1)])

            pe.wait_ge(qm_made, 1)
            pe.wait_ge(kv_kept, 2)
            for k in range(TAIL):
                scores(k)
            for b in range(1, B):
                keys_values(b)
            when(pe, head, lambda: stream(False), [(h_kv, HEAD * B), (h_scores, HEAD * B)])
            AHEAD = TAIL + 2
            for k in range(TAIL, AHEAD):
                scores(k)
            def to_queries(b):
                pe.wait_ge(oT_kept, b + 1)
                for g in range(2):
                    n = 2 * b + g
                    last = nc.tensor.transpose(A[1][:, n * P:(n + 1) * P], oT[:, b, g * P:(g + 1) * P], ident)
                last.then_inc(o_tok, 1)

            for k in range(B * TAIL):
                if k and k % TAIL == 0:
                    mix(k - 1)
                if k == LAST:
                    pe.wait_ge(scores_kept, B * TAIL)
                    pe.wait_ge(oT_kept, 2)
                    when(pe, head, lambda: stream(True),
                         [(h_kv, HEAD * B), (h_scores, HEAD * B), (h_T, 2 * HEAD * B), (h_mixed, HEAD * B)])
                    pe.wait_ge(h_added, B)
                    to_queries(0)
                    to_queries(1)
                transposes(k)
                if k % TAIL:
                    mix(k - 1)
                if k == LAST + 2:
                    to_queries(2)
                if k + AHEAD < B * TAIL:
                    scores(k + AHEAD)

            mix(B * TAIL - 1)
            pe.wait_ge(on_made, B - 1)
            for g in range(2):
                pe.wait_ge(*out_of_psum(B * TAIL - 2, g))
            for b in range(B - 1):
                last = nc.tensor.transpose(C[0][:, b * P:(b + 1) * P], on[:, b * P:(b + 1) * P], ident)
            last.then_inc(onT_made, 1)
            to_queries(B - 1)
            pe.wait_ge(wo_in, 32)
            pe.wait_ge(onT_kept, 1)
            for b in range(B - 1):
                last = mm(C[1][:, b * P:(b + 1) * P], onT[:, b * P:(b + 1) * P], wo[:], start=True, stop=True)
            last.then_inc(proj_made, 1)
            pe.wait_ge(on_made, B)
            for g in range(2):
                pe.wait_ge(*out_of_psum(B * TAIL - 1, g))
            nc.tensor.transpose(A[0][:, 0:P], on[:, (B - 1) * P:], ident).then_inc(onT_made, 1)
            pe.wait_ge(onT_kept, 2)
            mm(A[0][:, 512:512 + P], onT[:, (B - 1) * P:], wo[:], start=True, stop=True).then_inc(proj_made, 1)
            pe.wait_ge(ffn_in, 64)
            for i in range(2):
                if i:
                    pe.wait_ge(x1_made, 2)
                for b in (2 * i, 2 * i + 1):
                    pe.wait_ge(xf_made, b + 1)
                    last = nc.tensor.transpose(C[i][:, b % 2 * P:(b % 2 + 1) * P], xf[:, b], ident)
                last.then_inc(xfT_made, 1)
            for b in range(B):
                pe.wait_ge(xfT_kept, b // 2 + 1)
                last = mm(D[1][:, b * EX:(b + 1) * EX], xfT[:, b * P:(b + 1) * P], gate[:], start=True, stop=True)
            last.then_inc(logits_made, 1)
            pe.wait_ge(sel_made, 2)
            mm(D[1][:, 0:B * EX], upper, sel[:].rearrange("p i e -> p (i e)"), start=True, stop=False)
            mm(D[1][:, 0:B * EX], ones[:], cum[:, 0:B].rearrange("p i e -> p (i e)"), start=False, stop=True)
            mm(D[1][:, 64:64 + EX], ones[:], cum[:, B], start=True, stop=True).then_inc(pos_made, 1)

            pe.wait_ge(row_w_made, 1)
            pe.wait_ge(spread_w_made, 1)

            def ffn(r, again):
                if again:
                    last_round_stored(pe, r)

                def gather(n):
                    src = xln if n < E2 else xf
                    if n >= 2:
                        pe.wait_ge(xe_kept, r * EX + n - 1)
                    for i in range(B):
                        pe.wait_ge(onehot_made, (r * EX + n) * B + i + 1)
                        last = mm(X[n % 2][:, 0:SLOTS], src[:, i], onehot[:, n % 4, i], start=(i == 0), stop=(i == B - 1))
                    last.then_inc(gathered, 1)

                def layer0(n):
                    if n >= 2:
                        pe.wait_ge(z_kept, r * E2 + n - 1)
                    for c in range(2):
                        if c == 1 and n >= 2:
                            variances(n - 2)
                        for g in range(G):
                            if c == 0 and g % 4 == 0:
                                pe.wait_ge(sq0_made, r * 8 + 2 * n + g // 4 + 1)
                            last = mm(Z[n % 2][:, c * (SLOTS + 1):(c + 1) * (SLOTS + 1)], kw0[:, n, g, c * P:(c + 1) * P],
                                      SQ0[:, n % 2, g], start=(g == 0), stop=(g == G - 1))
                    last.then_inc(z_made, 1)

                def means(n):
                    pe.wait_ge(z_kept, r * E2 + n + 1)
                    if n:
                        pe.wait_ge(zd_made, r * E2 + n)
                    for c in range(2):
                        last = mm(MEAN[:, 0:SLOTS], mean_w[:], zs[:, n, c], start=(c == 0), stop=(c == 1))
                    last.then_inc(mean_made, 1)

                def variances(n):
                    pe.wait_ge(zq_made, r * E2 + n + 1)
                    for c in range(2):
                        last = mm(VAR, row_w[:, n], zq[:, n, c], start=(n == 0 and c == 0), stop=(n == E2 - 1 and c == 1))
                    if n == E2 - 1:
                        last.then_inc(vars_made, 1)

                def spread(n):
                    if n == 0:
                        pe.wait_ge(inverse_made, r + 1)
                        pe.wait_ge(xe_kept, r * EX + EX)
                    if n >= 2:
                        pe.wait_ge(scaled, r * E2 + n - 1)
                    mm(X[n % 2][:, 0:SLOTS], spread_w[:, n], rsd, start=True, stop=True).then_inc(spread_made, 1)

                def up(m):
                    pe.wait_ge(xe_kept, r * EX + E2 + m + 1)
                    if m == 1:
                        pe.wait_ge(vars_kept, r + 1)
                    for c in range(4):
                        if m >= 2 and c % 2 == 0:
                            pe.wait_ge(hid_kept, r * 16 + 4 * (m - 2) + c + 2)
                        last = mm(HID[m % 2][c // 2][:, c % 2 * SLOTS:(c % 2 + 1) * SLOTS], mw1[:, m, c * P:(c + 1) * P], xe[:, E2 + m],
                                  start=True, stop=True)
                        if c % 2:
                            last.then_inc(hid_made, 1)

                def down(m):
                    if m >= 2:
                        pe.wait_ge(yT_kept, r * EX + m - 1)
                    for c in range(4):
                        pe.wait_ge(hid_kept, r * 16 + 4 * m + c + 1)
                        last = mm(Y[m % 2][:, 0:SLOTS], mw2[:, m, c], hT[:, m, c], start=(c == 0), stop=(c == 3))
                    last.then_inc(y_made, 1)

                def layer1(n):
                    pe.wait_ge(yT_kept, r * EX + E2 + n - 1)
                    for g in range(G):
                        if g == 4:
                            to_rows(E2 + n - 1)
                        if g % 2 == 0:
                            pe.wait_ge(sq1_made, r * 16 + 4 * n + g // 2 + 1)
                        for c in range(2):
                            last = mm(Y[n % 2], kw1[:, n, c, g], SQ1[:, n % 2, g, c],
                                      start=(g == 0 and c == 0), stop=(g == G - 1 and c == 1))
                    last.then_inc(y_made, 1)

                def to_rows(n):
                    pe.wait_ge(yT_kept, r * EX + n + 1)
                    if n >= 2:
                        pe.wait_ge(*rows_kept(r, n - 2))
                    else:
                        pe.wait_ge(scaled, r * E2 + E2)
                    nc.tensor.transpose(YN[n % 2][:, 0:P], yT[:, n % 2, 0:P], ident)
                    nc.tensor.transpose(YN[n % 2][0:REST, P:2 * P], yT[:, n % 2, P:SLOTS], ident).then_inc(yn_made, 1)

                gather(0)
                gather(1)
                for n in range(E2):
                    layer0(n)
                    if n:
                        means(n - 1)
                    gather(n + 2)
                means(3)
                variances(2)
                gather(6)
                variances(3)
                pe.wait_ge(z_kept, r * E2 + E2)
                up(0)
                gather(7)
                up(1)
                spread(0)
                spread(1)
                down(0)
                spread(2)
                spread(3)
                up(2)
                down(1)
                up(3)
                to_rows(0)
                down(2)
                to_rows(1)
                down(3)
                to_rows(2)
                pe.wait_ge(kw1_in, 16)
                for n in range(E2):
                    layer1(n)
                to_rows(7)

            ffn(0, False)
            pe.wait_ge(over_made, 1)
            over = pe.value_load(over_i[0:1, 0:1])
            with pe.If(over > 0):
                with pe.Fori(1, ROUNDS) as r:
                    ffn(r, True)

        @block.vector
        def _(dve):
            v = nc.vector
            for s in (h_biased, h_kept, h_vec):
                dve.sem_inc(s, CREDIT)
            count = [0]

            def own(ins):
                count[0] += 1
                ins.then_inc(dv, 1)

            def own_done():
                dve.wait_ge(dv, count[0])

            def statistics(j, src):
                n, lo, hi = GROUPS[j]
                for b in range(lo, hi):
                    own(v.bn_stats(stats[:, n, b], src[:, b]))
                first = count[0] - (hi - lo)
                for b in range(lo, hi):
                    dve.wait_ge(dv, first + b - lo + 1)
                    i = v.bn_aggr(mv[:, n, b], stats[:, n, b])
                    if b < hi - 1:
                        own(i)
                    else:
                        i.then_inc(var_ready, 1)

            def normed(j, src, dst, made, blocks=None):
                n, lo, hi = GROUPS[j]
                own_done()
                dve.wait_ge(var_ready, j + 1)
                dve.wait_ge(rstd_made, j + 1)
                for b in (blocks or range(lo, hi)):
                    v.tensor_scalar(dst[:, b], src[:, b], mv[:, n, b, 0:1], rstd[:, n, b:b + 1], ALU.subtract, ALU.mult
                                    ).then_inc(made, 1)

            own(v.memset(mx[:], -NEG))
            dve.wait_ge(x_in, 16)
            statistics(0, xs)
            normed(0, xs, xn, xn_made)
            dve.wait_ge(mask_in, 16)
            own(v.tensor_reduce(flags[:].rearrange("p b t -> p (b t)"), mask_i32, AX, ALU.max))
            own_done()
            v.tensor_scalar(flags[:], flags[:], 0.0, None, ALU.is_gt).then_inc(flags_made, 1)
            dve.wait_ge(anyq_made, 1)
            dve.wait_ge(cst_in, 16)
            anyq = A[1][0:1, 0:B * TILES].rearrange("p (b t) -> p b t", b=B)
            own(v.tensor_copy(anyf[:, 0:B * TAIL].rearrange("p (b t) -> p b t", b=B), anyq[:, :, HEAD:]))
            own(v.tensor_reduce(anyf[:, B * TAIL:], anyq[:, :, 0:HEAD], mybir.AxisListType.XY, ALU.max))
            own_done()
            own(v.scalar_tensor_tensor(anyf[:], anyf[:], 1.0, powers, ALU.min, ALU.mult))
            own_done()
            own(v.tensor_reduce(word_f[:], anyf[:], AX, ALU.add))
            own_done()
            v.tensor_copy(word_i[:], word_f[:]).then_inc(word_made, 1)
            dve.wait_ge(q_scaled, 1)
            v.tensor_tensor(QM[:, 0], qs[:, 0:P].unsqueeze(1).broadcast_to([P, H, P]),
                            hmask.unsqueeze(2).broadcast_to([P, H, P]), ALU.mult).then_inc(qm_made, 1)
            own(v.tensor_reduce(notwipe[:], flags[:], AX, ALU.max))
            dve.wait_ge(vec_in, 16)
            v.tensor_copy(spread_w[:], ident[0:E2, 0:E2].unsqueeze(2).broadcast_to([E2, E2, P])).then_inc(spread_w_made, 1)
            own(v.tensor_scalar(hvec[:, 0:8], vec[:, G0:G0 + 8], 0.5, None, ALU.mult))
            own(v.tensor_scalar(hvec[:, 8:24], vec[:, G1:G1 + 16], 0.5, None, ALU.mult))
            tail, head = load_flags(dve)
            dve.wait_ge(bias_made, 1)

            def bias(ap):
                return ap.unsqueeze(1).broadcast_to([P, H, P])

            def spread(ap, n):
                return ap.unsqueeze(2).broadcast_to([P, H, n])

            def stream(sums):
                for b in range(B):
                    seq = b + B * sums
                    with dve.Fori(0, HEAD) as i:
                        dve.wait_ge(h_in, i * 32 + 32 * (HEAD * seq + 1))
                        dve.wait_ge(h_vec, CREDIT + i + HEAD * seq)
                        v.tensor_scalar(h_bias, h_mask_u8, NEG, -NEG, ALU.mult, ALU.add).then_inc(h_biased, 1)
                        dve.wait_ge(h_scores, CREDIT + i + HEAD * seq + 1)
                        dve.wait_ge(h_biased, CREDIT + i + HEAD * seq + 1)
                        if sums:
                            dve.wait_ge(h_T, CREDIT + i * 2 + 2 * HEAD * b)
                        v.tensor_tensor(h_S, A[0][:, :].rearrange("p (h k) -> p h k", h=H), bias(h_bias), ALU.add
                                        ).then_inc(h_kept, 1)
                        dve.wait_ge(h_kept, CREDIT + i + HEAD * seq + 1)
                        if sums:
                            v.tensor_tensor(h_S, h_S, spread(mxb[:, b], P), ALU.subtract).then_inc(h_vec, 1)
                        else:
                            v.tensor_reduce(mxt[:], h_S, AX, ALU.max).then_inc(h_max, 1)
                            dve.wait_ge(h_max, i + HEAD * b + 1)
                            v.tensor_tensor(mx[:, b, :, TAIL], mx[:, b, :, TAIL], mxt[:], ALU.max).then_inc(h_vec, 1)
                    if sums:
                        dve.wait_ge(h_mixed, CREDIT + HEAD * (b + 1))
                        v.tensor_tensor(oT[:, b], oT[:, b], OV[1][:, 0:256], ALU.add).then_inc(h_added, 1)

            def keep_scores(k):
                b, t = divmod(k, TAIL)
                if b and t == 0:
                    dve.wait_ge(bias_made, b + 1)

                def body():
                    dve.wait_ge(scores_made, k + 1)
                    if b >= 2:
                        dve.wait_ge(probsT_made, 2 * (k - 2 * TAIL) + 2)
                    s = S[:, b % 2, t]
                    v.tensor_tensor(s, A[k % 2][:, :].rearrange("p (h k) -> p h k", h=H), bias(mbias[:, b, t]), ALU.add
                                    ).then_inc(scores_kept, 1)
                    dve.wait_ge(scores_kept, k + 1)
                    v.tensor_reduce(mx[:, b, :, t], s, AX, ALU.max).then_inc(tile_max, 1)
                when(dve, tail[k], body, [(scores_kept, 1), (tile_max, 1)])

            def shift(k):
                def body():
                    for g in range(2):
                        s = S[:, k // TAIL % 2, k % TAIL, 4 * g:4 * g + 4]
                        v.tensor_tensor(s, s, mxb[:, B - 1, 4 * g:4 * g + 4].unsqueeze(2).broadcast_to([P, 4, P]),
                                        ALU.subtract).then_inc(shifted_last, 1)
                when(dve, tail[k], body, [(shifted_last, 2)])

            def keep_probsT(k):
                def body():
                    dve.wait_ge(mixed, k - 1)
                    dve.wait_ge(probsT_made, 2 * k + 2)
                    v.tensor_copy(PT[:, k % 2, 512:1024], probsT_psum(k, 1)).then_inc(probsT_last, 1)
                when(dve, tail[k], body, [(probsT_last, 1)])

            def maximum(b):
                dve.wait_ge(tile_max, TAIL * (b + 1))
                dve.wait_ge(h_vec, CREDIT + HEAD * B)
                v.tensor_reduce(mxb[:, b], mx[:, b], AX, ALU.max).then_inc(batch_max, 1)

            def keep_sums(b):
                dve.wait_ge(ov_zeroed, b + 1)
                dve.wait_ge(mixed, TAIL * (b + 1))
                if b < 2:
                    dve.wait_ge(bias_made, B)
                    v.tensor_copy(oT[:, b], OV[b % 2][:, 0:256]).then_inc(oT_kept, 1)
                else:
                    dve.wait_ge(h_added, B)
                    v.tensor_tensor(oT[:, b], oT[:, b], OV[b % 2][:, 0:256], ALU.add).then_inc(oT_kept, 1)

            own_done()
            for k in range(TAIL):
                keep_scores(k)
            when(dve, head, lambda: stream(False),
                 [(h_biased, HEAD * B), (h_kept, HEAD * B), (h_vec, HEAD * B), (h_max, HEAD * B)])
            for k in range(B * TAIL):
                b, t = divmod(k, TAIL)
                if t == 0:
                    maximum(b)
                if k < LAST:
                    keep_scores(k + TAIL)
                elif t == 0:
                    dve.wait_ge(batch_max, B)
                    dve.wait_ge(oT_kept, 2)
                    dve.wait_ge(oT_cleared, 1)
                    when(dve, head, lambda: stream(True),
                         [(h_biased, HEAD * B), (h_kept, HEAD * B), (h_vec, HEAD * B), (h_added, B)])
                    shift(k)
                    shift(k + 1)
                elif t + 1 < TAIL:
                    keep_probsT(k - 1)
                    shift(k + 1)
                if 0 < b and t == 1:
                    keep_sums(b - 1)

            def reciprocals(lo, hi):
                dve.wait_ge(o_tok, hi)
                otok = A[1][:, lo * 256:hi * 256]
                own(v.tensor_scalar(den[:, lo:hi], otok.rearrange("p (b h w) -> p b h w", h=H, w=VW)[:, :, :, HD], 0.5, None, ALU.max))
                own_done()
                own(v.reciprocal(rden[:, lo:hi], den[:, lo:hi]))

            def divide(lo, hi):
                otok = A[1][:, lo * 256:hi * 256]
                own_done()
                own(v.tensor_tensor(rdw[:, lo:hi], rden[:, lo:hi], notwipe[:, lo:hi].unsqueeze(2).broadcast_to([P, hi - lo, H]), ALU.mult))
                own_done()
                own(v.tensor_tensor(on[:, lo * P:hi * P].rearrange("p (n w) -> p n w", w=HD),
                                    otok.rearrange("p (n w) -> p n w", w=VW)[:, :, 0:HD],
                                    rdw[:, lo:hi].rearrange("p b h -> p (b h)").unsqueeze(2).broadcast_to([P, (hi - lo) * H, HD]), ALU.mult))

            def skip_wiped(lo, hi):
                dve.wait_ge(wo_in, 32)
                own_done()
                for b in range(lo, hi):
                    v.scalar_tensor_tensor(on[:, b * P:(b + 1) * P], rows[:, 0], notwipe[:, b:b + 1], on[:, b * P:(b + 1) * P],
                                           ALU.mult, ALU.add).then_inc(on_made, 1)

            keep_probsT(B * TAIL - 2)
            reciprocals(0, B - 1)
            keep_probsT(B * TAIL - 1)
            divide(0, B - 1)
            skip_wiped(0, B - 1)
            keep_sums(B - 1)
            reciprocals(B - 1, B)
            divide(B - 1, B)
            skip_wiped(B - 1, B)
            dve.wait_ge(xb_made, B)
            dve.wait_ge(proj_made, 1)
            v.tensor_tensor(x1[:, 0:B - 1], C[1][:, 0:(B - 1) * P].rearrange("p (b d) -> p b d", d=P), xb[:, 0:B - 1], ALU.add
                            ).then_inc(x1_made, 1)
            dve.wait_ge(x1_made, 1)
            statistics(1, x1)
            dve.wait_ge(proj_made, 2)
            v.tensor_tensor(x1[:, B - 1], A[0][:, 512:512 + P], xb[:, B - 1], ALU.add).then_inc(x1_made, 1)
            dve.wait_ge(x1_made, 2)
            statistics(2, x1)
            n = 0
            for j, pairs in ((1, ((0, 1), (0, 2), (1, 2))), (2, ((0, 3), (1, 3), (2, 3)))):
                normed(j, x1, xn1, xn1_made)
                for s, t in pairs:
                    dve.wait_ge(xn1_made, t + 1)
                    own(v.tensor_tensor_reduce(prod[:, n], xn1[:, s], xn1[:, t], 1.0, 0.0, ALU.mult, ALU.add, sc[:, s, t:t + 1]))
                    n += 1
            own_done()
            for s in range(B - 1):
                own(v.tensor_copy(sc[:, s + 1:B, s], sc[:, s, s + 1:B]))
            own_done()
            dve.wait_ge(sc_own, B)
            own(v.tensor_reduce(scm[:], sc[:], AX, ALU.max))
            own_done()
            v.tensor_tensor(scd[:], sc[:], scm[:].unsqueeze(2).broadcast_to([P, B, B]), ALU.subtract).then_inc(sc_ready, 1)
            dve.wait_ge(sc_exp, 1)
            own(v.tensor_reduce(scs[:], sce[:], AX, ALU.add))
            own_done()
            own(v.reciprocal(scr[:], scs[:]))
            own_done()
            v.tensor_tensor(scp[:], sce[:], scr[:].unsqueeze(2).broadcast_to([P, B, B]), ALU.mult).then_inc(scp_made, 1)
            dve.wait_ge(scp_made, 1)
            for t in range(B):
                for s in range(2):
                    if t:
                        dve.wait_ge(dv, count[0] - 1)
                    own(v.scalar_tensor_tensor(x2[:, s], xn1[:, t], scp[:, s, t:t + 1], (x2 if t else x1)[:, s], ALU.mult, ALU.add))
            own_done()
            statistics(3, x2)
            dve.wait_ge(term_made, 2 * B)
            dve.wait_ge(x2_last, B - 1)
            own(v.tensor_tensor(x2[:, 2:4], x2[:, 2:4], prod[:, 2 * B - 2:2 * B], ALU.add))
            own_done()
            statistics(4, x2)
            for i in range(2):
                normed(3 + i, x2, xf, xf_made)
                dve.wait_ge(xf_made, 2 * i + 2)
                statistics(5 + i, xf)
            normed(5, xf, xln, xln_made)
            dve.wait_ge(logits_made, 1)
            lg = D[1][:, 0:B * EX].rearrange("p (i e) -> p i e", i=B)
            own(v.tensor_reduce(lgm[:], lg, AX, ALU.max))
            own_done()
            v.tensor_tensor(lgd[:], lg, lgm[:].unsqueeze(2).broadcast_to([P, B, EX]), ALU.subtract).then_inc(lg_ready, 1)
            normed(6, xf, xln, xln_made, (2,))
            dve.wait_ge(lg_exp, 1)
            mine = lge[:].unsqueeze(3).broadcast_to([P, B, EX, EX])
            other = lge[:].unsqueeze(2).broadcast_to([P, B, EX, EX])
            own(v.tensor_tensor(cmp_eq[:], other, mine, ALU.is_equal))
            own(v.tensor_tensor(cmp_gt[:], other, mine, ALU.is_gt))
            dve.wait_ge(dv, count[0] - 1)
            own(v.tensor_tensor(cmp_eq[:], cmp_eq[:], lower.unsqueeze(1).broadcast_to([P, B, EX, EX]), ALU.mult))
            own_done()
            own(v.tensor_tensor(cmp_gt[:], cmp_gt[:], cmp_eq[:], ALU.add))
            own_done()
            own(v.tensor_reduce(rank[:], cmp_gt[:], AX, ALU.add))
            own_done()
            v.tensor_scalar(sel[:], rank[:], 1.5, None, ALU.is_lt).then_inc(sel_made, 1)
            own(v.memset(cum[:, 0], 0.0))
            dve.wait_ge(sel_made, 1)
            for i in range(B):
                own_done()
                ins = v.tensor_tensor(cum[:, i + 1], cum[:, i], sel[:, i], ALU.add)
                if i < B - 1:
                    own(ins)
                else:
                    ins.then_inc(sel_made, 1)
            normed(6, xf, xln, xln_made, (3,))
            v.memset(SQ1[:, :, :, :, SLOTS:], 1.0).then_inc(sq_ones, 1)
            dve.wait_ge(pos_made, 1)
            pos = D[1][:, 0:B * EX].rearrange("p (i e) -> p i e", i=B)
            own(v.scalar_tensor_tensor(posm[:], pos, 1.0, sel[:], ALU.add, ALU.mult))
            own(v.tensor_tensor(rowid[:], pos, eoff.unsqueeze(1).broadcast_to([P, B, EX]), ALU.add))
            dve.wait_ge(dv, count[0] - 1)
            dve.wait_ge(sq_ones, 1)

            def route_weights():
                own(v.tensor_reduce(cmax[:], D[1][0:1, 64:64 + EX], AX, ALU.max))
                own_done()
                v.tensor_scalar(over_i[:], cmax[:], float(SLOTS), None, ALU.is_gt).then_inc(over_made, 1)
                own(v.scalar_tensor_tensor(dtmp[:, 0], sel[:], -FAR, rowid[:], ALU.mult, ALU.add))
                own(v.tensor_tensor(dtmp[:, 1], rowid[:], sel[:], ALU.mult))
                own_done()
                own(v.tensor_reduce(destf[:, 0], dtmp[:, 0], AX, ALU.min))
                own(v.tensor_reduce(destf[:, 1], dtmp[:, 1], AX, ALU.max))
                own_done()
                own(v.tensor_scalar(dest[:, 0], destf[:, 0], FAR, None, ALU.add))
                v.tensor_copy(dest[:, 1], destf[:, 1]).then_inc(dest_made, 1)
                own(v.tensor_tensor(mask_k[:, 1], dtmp[:, 1], destf[:, 1].unsqueeze(2).broadcast_to([P, B, EX]), ALU.is_equal))
                own_done()
                own(v.tensor_tensor(mask_k[:, 0], sel[:], mask_k[:, 1], ALU.subtract))
                own_done()
                own(v.tensor_tensor(wtmp[:], mask_k[:], lge[:].unsqueeze(1).broadcast_to([P, 2, B, EX]), ALU.mult))
                own_done()
                own(v.tensor_reduce(wsum[:], wtmp[:], AX, ALU.add))
                own_done()
                own(v.tensor_tensor(wden[:], wsum[:, 0], wsum[:, 1], ALU.add))
                own_done()
                own(v.reciprocal(wden[:], wden[:]))
                own_done()
                own(v.tensor_tensor(wgt[:], wsum[:], wden[:].unsqueeze(1).broadcast_to([P, 2, B]), ALU.mult))

            def ffn(r, again, off):
                mine = [0]

                def step(ins):
                    mine[0] += 1
                    ins.then_inc(fv, 1)

                def step_done(back=0):
                    dve.wait_ge(fv, off + (mine[0] - back))

                if again:
                    last_round_stored(dve, r)
                    step(v.tensor_scalar(posm[:], posm[:], -float(SLOTS), None, ALU.add))
                    step_done()

                def choose(n):
                    e = E2 + n if n < E2 else n - E2
                    if n >= 4:
                        dve.wait_ge(gathered, r * EX + n - 3)
                    for i in range(B):
                        v.tensor_scalar(onehot[:, n % 4, i], iota1, posm[:, i, e:e + 1], None, ALU.is_equal
                                        ).then_inc(onehot_made, 1)

                def keep_tokens(n):
                    dve.wait_ge(gathered, r * EX + n + 1)
                    if n < E2:
                        ins = v.tensor_scalar(xe[:, n], X[n % 2][:, 0:SLOTS], hvec[:, n:n + 1], hvec[:, 4 + n:5 + n],
                                              ALU.mult, ALU.add)
                    else:
                        ins = v.tensor_copy(xe[:, n], X[n % 2][:, 0:SLOTS])
                    ins.then_inc(xe_kept, 1)

                def squares0(n, gs=(0, 4)):
                    for g in gs:
                        dve.wait_ge(t0_made, r * 8 + 2 * n + g // 4 + 1)
                        if n >= 2 and g == 0:
                            dve.wait_ge(z_made, r * E2 + n - 1)
                        t = T0[:, n % 2, g:g + 4]
                        v.tensor_tensor(SQ0[:, n % 2, g:g + 4, 0:SLOTS], t, t, ALU.mult).then_inc(sq0_made, 1)

                def keep_z(n):
                    dve.wait_ge(z_made, r * E2 + n + 1)
                    z = Z[n % 2][:, 0:2 * (SLOTS + 1)].rearrange("p (c s) -> p c s", c=2)
                    step(v.tensor_tensor(cz[:, n], z[:, :, SLOTS], vec[:, SB0 + 2 * n:SB0 + 2 * n + 2], ALU.add))
                    step_done()
                    step(v.tensor_scalar(zs[:, n, 0], z[:, 0, 0:SLOTS], -1.0, cz[:, n, 0:1], ALU.mult, ALU.add))
                    v.tensor_scalar(zs[:, n, 1], z[:, 1, 0:SLOTS], -1.0, cz[:, n, 1:2], ALU.mult, ALU.add).then_inc(z_kept, 1)

                def centre(n):
                    dve.wait_ge(mean_made, r * E2 + n + 1)
                    v.tensor_tensor(zd[:, n], zs[:, n], MEAN[:, 0:SLOTS].unsqueeze(1).broadcast_to([P, 2, SLOTS]), ALU.subtract
                                    ).then_inc(zd_made, 1)
                    dve.wait_ge(zd_made, r * E2 + n + 1)
                    v.tensor_tensor(zq[:, n], zd[:, n], zd[:, n], ALU.mult).then_inc(zq_made, 1)

                def keep_vars():
                    dve.wait_ge(vars_made, r + 1)
                    v.tensor_scalar(var, VAR, EPS, None, ALU.add).then_inc(vars_kept, 1)

                def invert():
                    dve.wait_ge(std_made, r + 1)
                    v.reciprocal(rsd, var).then_inc(inverse_made, 1)

                def scale(n):
                    dve.wait_ge(spread_made, r * E2 + n + 1)
                    v.tensor_tensor(zq[:, n], zd[:, n], X[n % 2][:, 0:SLOTS].unsqueeze(1).broadcast_to([P, 2, SLOTS]), ALU.mult
                                    ).then_inc(scaled, 1)

                def affine(n):
                    dve.wait_ge(scaled, r * E2 + n + 1)
                    for c in range(2):
                        k = 2 * n + c
                        ins = v.tensor_scalar(zs[:, n, c], zq[:, n, c], hvec[:, 8 + k:9 + k], hvec[:, 16 + k:17 + k], ALU.mult, ALU.add)
                        if c == 0:
                            step(ins)
                        else:
                            step_done()
                            ins.then_inc(u1_made, 1)

                def squares1(n, gs=range(G)):
                    for g in gs[::2]:
                        dve.wait_ge(t1_made, r * 16 + 4 * n + g // 2 + 1)
                        if g == 0 and n >= 2:
                            dve.wait_ge(y_made, r * EX + E2 + n - 1)
                        if g == 0 and n == 0:
                            dve.wait_ge(z_made, r * E2 + E2)
                        for c in range(2):
                            t = T1[:, n % 2, g:g + 2, c]
                            ins = v.tensor_tensor(SQ1[:, n % 2, g:g + 2, c, 0:SLOTS], t, t, ALU.mult)
                        ins.then_inc(sq1_made, 1)

                def keep_y(n):
                    dve.wait_ge(y_made, r * EX + n + 1)
                    if n >= 2:
                        dve.wait_ge(yn_made, r * EX + n - 1)
                    y = Y[n % 2]
                    if n < E2:
                        v.tensor_scalar(yT[:, n % 2], y[:, 0:SLOTS], vec[:, MB2 + n:MB2 + n + 1], None, ALU.add).then_inc(yT_kept, 1)
                    else:
                        k = n - E2
                        step(v.tensor_tensor(cy[:, k:k + 1], y[:, SLOTS:SLOTS + 1], vec[:, SB1 + k:SB1 + k + 1], ALU.add))
                        step_done()
                        v.tensor_scalar(yT[:, n % 2], y[:, 0:SLOTS], -1.0, cy[:, k:k + 1], ALU.mult, ALU.add).then_inc(yT_kept, 1)

                def rows_out(n):
                    dve.wait_ge(yn_made, r * EX + n + 1)
                    v.tensor_copy(yn[:, n, 0], YN[n % 2][:, 0:P])
                    v.tensor_copy(yn[0:REST, n, 1], YN[n % 2][0:REST, P:2 * P]).then_inc(yn_kept_mlp, 1)

                choose(0)
                choose(1)
                keep_tokens(0)
                choose(2)
                squares0(0, (0,))
                keep_tokens(1)
                squares0(0, (4,))
                squares0(1)
                choose(3)
                if not again:
                    route_weights()
                for n in range(E2):
                    keep_z(n)
                    if n:
                        centre(n - 1)
                    keep_tokens(n + 2)
                    if n + 2 < E2:
                        squares0(n + 2)
                    if n < 3:
                        choose(n + 4)
                    if n == 2:
                        choose(7)
                centre(3)
                keep_tokens(6)
                keep_vars()
                invert()
                keep_tokens(7)
                scale(0)
                scale(1)
                affine(0)
                scale(2)
                scale(3)
                affine(1)
                keep_y(0)
                keep_y(1)
                rows_out(0)
                affine(2)
                keep_y(2)
                rows_out(1)
                squares1(0, range(0, 2))
                keep_y(3)
                rows_out(2)
                squares1(0, range(2, 8))
                affine(3)
                squares1(1)
                rows_out(3)
                keep_y(4)
                squares1(2)
                keep_y(5)
                squares1(3)
                keep_y(6)
                keep_y(7)
                return mine[0]

            own_done()
            steps = ffn(0, False, 0)
            over = dve.value_load(over_i[0:1, 0:1])
            with dve.If(over > 0):
                with dve.Fori(1, ROUNDS) as r:
                    assert ffn(r, True, r * (steps + 1) - 1) == steps + 1
            own_done()
            for i in range(B):
                dve.wait_ge(y_back[0][i], 16)
                own(v.scalar_tensor_tensor(fin[:, i], yg[:, 0, i], wgt[:, 0, i:i + 1], x2[:, i], ALU.mult, ALU.add))
            own_done()
            for i in range(B):
                dve.wait_ge(y_back[1][i], 16)
                v.scalar_tensor_tensor(fin[:, i], yg[:, 1, i], wgt[:, 1, i:i + 1], fin[:, i], ALU.mult, ALU.add).then_inc(fin_made, 1)


def constants():
    c = np.zeros((P, NC), np.float32)
    p = np.arange(P)
    c[:, C_ID:C_ID + P] = np.eye(P)
    c[:, C_U:C_U + P] = p[:, None] < p[None, :]
    c[:, C_HM:C_HM + H] = p[:, None] // HD == np.arange(H)[None, :]
    c[:, C_IOTA:C_IOTA + SLOTS] = 1 + np.arange(SLOTS)
    c[:, C_EOFF:C_EOFF + EX] = ROWS * np.arange(EX)
    e = np.arange(EX)
    c[:, C_POW:C_POW + B * TAIL + 1] = 2.0 ** np.arange(B * TAIL + 1)
    c[:, C_LT:C_LT + EX * EX] = (e[None, :] < e[:, None]).reshape(-1)
    return c


def arrays_of(i):
    def a(name):
        return np.asarray(i[name])

    rows = [a("L0_xattn_bq").reshape(1, P), a("L0_xattn_bk").reshape(1, P), a("L0_ffn_kan_ln_g0"), a("L0_ffn_kan_ln_b0"),
            a("L0_ffn_kan_sl_b0").reshape(-1, P), a("L0_ffn_kan_ln_g1").reshape(-1, P), a("L0_ffn_kan_ln_b1").reshape(-1, P),
            a("L0_ffn_kan_sl_b1"), a("L0_ffn_mlp_b2"), a("L0_ffn_mlp_b1").reshape(-1, P)]
    return {
        "x": a("x").transpose(1, 0, 2),
        "ctxT": a("ctx_1024").transpose(0, 2, 1),
        "mask": a("mask_BxSxS2_bk0").transpose(1, 0, 2),
        "Wqkv": np.stack([a("L0_xattn_W" + w) for w in "qkv"], 1),
        "Wo": a("L0_xattn_Wo"),
        "rows2": np.stack([a("L0_xattn_bv"), a("L0_xattn_bo")]),
        "gateW": a("L0_ffn_gate_W"),
        "KW0": a("L0_ffn_kan_sl_W0").reshape(E2, P, G, F2).transpose(1, 0, 2, 3),
        "KW1": a("L0_ffn_kan_sl_W1").reshape(E2, 2, P, G, P).transpose(2, 0, 1, 3, 4),
        "MW1": a("L0_ffn_mlp_W1").transpose(1, 0, 2),
        "MW2": a("L0_ffn_mlp_W2").reshape(E2, 4, P, P).transpose(2, 0, 1, 3),
        "vecs": np.concatenate(rows, 0).T,
        "consts": constants(),
    }


def build(nc, arrays):
    args = []
    for name, value in arrays.items():
        args.append(nc.dram_tensor(name, value.shape, mybir.dt.from_np(value.dtype), kind="ExternalInput").ap())
    out = nc.dram_tensor("out", (B, P, P), F32, kind="ExternalOutput").ap()
    args[2] = args[2].bitcast(U8) if args[2].dtype != U8 else args[2]
    layer(nc, *args, out.rearrange("b q d -> q b d"))


def kernel(**inputs):
    import concourse.bacc as bacc
    from concourse.bass_utils import run_bass_kernel_spmd

    arrays = {k: np.ascontiguousarray(v) for k, v in arrays_of(inputs).items()}
    nc = bacc.Bacc("TRN2", target_bir_lowering=False, num_devices=1)
    build(nc, arrays)
    r = run_bass_kernel_spmd(nc, [arrays], core_ids=[0])
    return r.results[0]["out"]
```
